# Optimizing a Trainium2 kernel written in Bass

```python
import numpy as np
import jax
import jax.numpy as jnp

def _softmax(x, axis=-1):
    return jax.nn.softmax(x, axis=axis)

def _gelu(x):
    return jax.nn.gelu(x, approximate=True)

def _silu(x):
    return jax.nn.silu(x)

def _sigmoid(x):
    return jax.nn.sigmoid(x)

def _layernorm(x, axis=-1, eps=1e-05):
    m = jnp.mean(x, axis=axis, keepdims=True)
    v = jnp.var(x, axis=axis, keepdims=True)
    return (x - m) / jnp.sqrt(v + eps)

def _scatter_add(tgt, idx, src, axis=0):
    return tgt.at[idx].add(src)

def _segment_sum(src, seg, n):
    return jax.ops.segment_sum(src, seg, n)
kernel_name = 'mk_adaln_d1_jaxref_r8_7ec6e3'

def setup_inputs(seed: int=0):
    np.random.seed(seed)
    _w = jnp.asarray

    def _L0_attn_setup():
        import jax, jax.numpy as jnp
        import numpy as np
        NUM_K_HEADS = 16
        NUM_V_HEADS = 32
        HEAD_K_DIM = 128
        HEAD_V_DIM = 128
        CONV_K = 4
        EPS = 1e-06

        def _causal_conv1d(x, w, b):
            B, S, C = x.shape
            K = w.shape[1]
            xp = jnp.pad(x, ((0, 0), (K - 1, 0), (0, 0)))
            out = sum((xp[:, K - 1 - i:K - 1 - i + S, :] * w[:, i] for i in range(K)))
            return out + b

        def _l2norm(x, eps=EPS):
            return x * jax.lax.rsqrt(jnp.sum(x * x, axis=-1, keepdims=True) + eps)

        def _gated_delta_scan(q, k, v, g, beta):
            B, S, H, Dk = q.shape
            Dv = v.shape[-1]
            q = _l2norm(q) * (1.0 / Dk ** 0.5)
            k = _l2norm(k)
            qT = jnp.transpose(q, (1, 0, 2, 3))
            kT = jnp.transpose(k, (1, 0, 2, 3))
            vT = jnp.transpose(v, (1, 0, 2, 3))
            gT = jnp.transpose(g, (1, 0, 2))
            bT = jnp.transpose(beta, (1, 0, 2))

            def step(state, inp):
                q_t, k_t, v_t, g_t, b_t = inp
                state = state * jnp.exp(g_t)[..., None, None]
                kv_pred = jnp.einsum('bhk,bhkv->bhv', k_t, state)
                delta = b_t[..., None] * (v_t - kv_pred)
                state = state + jnp.einsum('bhk,bhv->bhkv', k_t, delta)
                out_t = jnp.einsum('bhk,bhkv->bhv', q_t, state)
                return (state, out_t)
            state0 = jnp.zeros((B, H, Dk, Dv), dtype=jnp.float32)
            _, outT = jax.lax.scan(step, state0, (qT, kT, vT, gT, bT))
            return jnp.transpose(outT, (1, 0, 2, 3))
        key = jax.random.key(seed)
        ks = jax.random.split(key, 8)
        B, S, D = (2, 256, 256)
        key_dim = NUM_K_HEADS * HEAD_K_DIM
        value_dim = NUM_V_HEADS * HEAD_V_DIM
        conv_dim = 2 * key_dim + value_dim
        w = lambda k, shp: jax.random.normal(k, shp, dtype=jnp.float32) * 0.02
        return {'hidden_states': jax.random.normal(ks[0], (B, S, D), dtype=jnp.float32), 'W_qkv': w(ks[1], (D, conv_dim)), 'W_z': w(ks[2], (D, value_dim)), 'W_b': w(ks[3], (D, NUM_V_HEADS)), 'W_a': w(ks[4], (D, NUM_V_HEADS)), 'conv_w': w(ks[5], (conv_dim, CONV_K)), 'conv_b': jnp.zeros((conv_dim,), dtype=jnp.float32), 'dt_bias': jnp.ones((NUM_V_HEADS,), dtype=jnp.float32), 'A_log': jnp.zeros((NUM_V_HEADS,), dtype=jnp.float32), 'norm_gamma': jnp.ones((HEAD_V_DIM,), dtype=jnp.float32), 'W_out': w(ks[6], (value_dim, D))}
    _L0_attn_in = _L0_attn_setup()

    def _L0_ffn_setup():
        import jax, jax.numpy as jnp
        import numpy as np
        HIDDEN = 256
        INTER = 1024
        BATCH, LOCAL_SEQ = (2, 512)
        key = jax.random.key(seed)
        k1, k2, k3 = jax.random.split(key, 3)
        h_shard = jax.random.normal(k1, (BATCH, LOCAL_SEQ, HIDDEN), dtype=jnp.float32)
        w_gate_up = jax.random.normal(k2, (2 * INTER, HIDDEN), dtype=jnp.float32) * 0.02
        w_down = jax.random.normal(k3, (HIDDEN, INTER), dtype=jnp.float32) * 0.02
        return {'h_shard': h_shard, 'w_gate_up': w_gate_up, 'w_down': w_down}
    _L0_ffn_in = _L0_ffn_setup()
    _L0_c = _w((lambda *s: np.random.randn(*s).astype(np.float32) * 0.05)(4, 256))
    _L0_wmod = _w((lambda *s: np.random.randn(*s).astype(np.float32) * 0.05)(256, 6 * 256) * 256 ** (-0.5))
    _d = {'L0_attn_hidden_states': _L0_attn_in['hidden_states'], 'L0_attn_W_qkv': _L0_attn_in['W_qkv'], 'L0_attn_W_z': _L0_attn_in['W_z'], 'L0_attn_W_b': _L0_attn_in['W_b'], 'L0_attn_W_a': _L0_attn_in['W_a'], 'L0_attn_conv_w': _L0_attn_in['conv_w'], 'L0_attn_conv_b': _L0_attn_in['conv_b'], 'L0_attn_dt_bias': _L0_attn_in['dt_bias'], 'L0_attn_A_log': _L0_attn_in['A_log'], 'L0_attn_norm_gamma': _L0_attn_in['norm_gamma'], 'L0_attn_W_out': _L0_attn_in['W_out'], 'L0_ffn_w_gate_up': _L0_ffn_in['w_gate_up'], 'L0_ffn_w_down': _L0_ffn_in['w_down'], 'L0_c': _L0_c, 'L0_wmod': _L0_wmod}
    _x0 = _d['L0_attn_hidden_states']
    _d['L0_attn_hidden_states'] = jax.random.normal(jax.random.fold_in(jax.random.key(seed), 1), (4, 1024, 256), dtype=_x0.dtype)
    del _x0
    return _d

def reference(L0_attn_hidden_states, L0_attn_W_qkv, L0_attn_W_z, L0_attn_W_b, L0_attn_W_a, L0_attn_conv_w, L0_attn_conv_b, L0_attn_dt_bias, L0_attn_A_log, L0_attn_norm_gamma, L0_attn_W_out, L0_ffn_w_gate_up, L0_ffn_w_down, L0_c, L0_wmod):

    def _L0_attn_ref(hidden_states, W_qkv, W_z, W_b, W_a, conv_w, conv_b, dt_bias, A_log, norm_gamma, W_out):
        import jax, jax.numpy as jnp
        import numpy as np
        NUM_K_HEADS = 16
        NUM_V_HEADS = 32
        HEAD_K_DIM = 128
        HEAD_V_DIM = 128
        CONV_K = 4
        EPS = 1e-06

        def _causal_conv1d(x, w, b):
            B, S, C = x.shape
            K = w.shape[1]
            xp = jnp.pad(x, ((0, 0), (K - 1, 0), (0, 0)))
            out = sum((xp[:, K - 1 - i:K - 1 - i + S, :] * w[:, i] for i in range(K)))
            return out + b

        def _l2norm(x, eps=EPS):
            return x * jax.lax.rsqrt(jnp.sum(x * x, axis=-1, keepdims=True) + eps)

        def _gated_delta_scan(q, k, v, g, beta):
            B, S, H, Dk = q.shape
            Dv = v.shape[-1]
            q = _l2norm(q) * (1.0 / Dk ** 0.5)
            k = _l2norm(k)
            qT = jnp.transpose(q, (1, 0, 2, 3))
            kT = jnp.transpose(k, (1, 0, 2, 3))
            vT = jnp.transpose(v, (1, 0, 2, 3))
            gT = jnp.transpose(g, (1, 0, 2))
            bT = jnp.transpose(beta, (1, 0, 2))

            def step(state, inp):
                q_t, k_t, v_t, g_t, b_t = inp
                state = state * jnp.exp(g_t)[..., None, None]
                kv_pred = jnp.einsum('bhk,bhkv->bhv', k_t, state)
                delta = b_t[..., None] * (v_t - kv_pred)
                state = state + jnp.einsum('bhk,bhv->bhkv', k_t, delta)
                out_t = jnp.einsum('bhk,bhkv->bhv', q_t, state)
                return (state, out_t)
            state0 = jnp.zeros((B, H, Dk, Dv), dtype=jnp.float32)
            _, outT = jax.lax.scan(step, state0, (qT, kT, vT, gT, bT))
            return jnp.transpose(outT, (1, 0, 2, 3))
        B, S, D = hidden_states.shape
        key_dim = NUM_K_HEADS * HEAD_K_DIM
        value_dim = NUM_V_HEADS * HEAD_V_DIM
        mixed_qkv = hidden_states @ W_qkv
        z = (hidden_states @ W_z).reshape(B, S, NUM_V_HEADS, HEAD_V_DIM)
        b = hidden_states @ W_b
        a = hidden_states @ W_a
        mixed_qkv = _causal_conv1d(mixed_qkv, conv_w, conv_b)
        mixed_qkv = mixed_qkv * jax.nn.sigmoid(mixed_qkv)
        query = mixed_qkv[..., :key_dim].reshape(B, S, NUM_K_HEADS, HEAD_K_DIM)
        key = mixed_qkv[..., key_dim:2 * key_dim].reshape(B, S, NUM_K_HEADS, HEAD_K_DIM)
        value = mixed_qkv[..., 2 * key_dim:].reshape(B, S, NUM_V_HEADS, HEAD_V_DIM)
        beta = jax.nn.sigmoid(b).astype(jnp.float32)
        g = -jnp.exp(A_log.astype(jnp.float32)) * jax.nn.softplus(a.astype(jnp.float32) + dt_bias.astype(jnp.float32))
        rep = NUM_V_HEADS // NUM_K_HEADS
        if rep > 1:
            query = jnp.repeat(query, rep, axis=2)
            key = jnp.repeat(key, rep, axis=2)
        core = _gated_delta_scan(query.astype(jnp.float32), key.astype(jnp.float32), value.astype(jnp.float32), g, beta)
        rms = core * jax.lax.rsqrt(jnp.mean(core * core, axis=-1, keepdims=True) + EPS)
        gated = rms * norm_gamma * jax.nn.sigmoid(z)
        out = gated.reshape(B, S, value_dim) @ W_out
        return out

    def _L0_ffn_ref(h_shard, w_gate_up, w_down):
        import jax, jax.numpy as jnp
        import numpy as np
        HIDDEN = 256
        INTER = 1024
        BATCH, LOCAL_SEQ = (2, 512)
        batch, local_seq, hidden = h_shard.shape
        gate_up = jnp.einsum('bsh,oh->bso', h_shard, w_gate_up)
        gate, up = jnp.split(gate_up, 2, axis=-1)
        h = jax.nn.silu(gate) * up
        out = jnp.einsum('bsi,hi->bsh', h, w_down)
        return out
    x = L0_attn_hidden_states
    mod = (_silu(L0_c) @ L0_wmod).reshape(L0_c.shape[0], 6, 1, -1)
    sa, ca, ga, sb, cb, gb = (mod[:, 0], mod[:, 1], mod[:, 2], mod[:, 3], mod[:, 4], mod[:, 5])
    ga = (2 * (ga >= 0) - 1) * jnp.maximum(jnp.abs(ga), 0.25)
    gb = (2 * (gb >= 0) - 1) * jnp.maximum(jnp.abs(gb), 0.25)
    h = _layernorm(x, axis=-1) * (1 + ca) + sa
    x = x + ga * _L0_attn_ref(h, L0_attn_W_qkv, L0_attn_W_z, L0_attn_W_b, L0_attn_W_a, L0_attn_conv_w, L0_attn_conv_b, L0_attn_dt_bias, L0_attn_A_log, L0_attn_norm_gamma, L0_attn_W_out)
    h = _layernorm(x, axis=-1) * (1 + cb) + sb
    x = x + gb * _L0_ffn_ref(h, L0_ffn_w_gate_up, L0_ffn_w_down)
    return x

_drawn_inputs = setup_inputs


def setup_inputs(seed=0):
    import zlib

    import numpy as np

    out = dict(_drawn_inputs(seed))
    spreads = {'L0_attn_conv_b': (0.0, 0.1),
     'L0_attn_dt_bias': (1.0, 0.6),
     'L0_attn_A_log': (0.0, 0.8),
     'L0_attn_norm_gamma': (1.0, 0.6)}
    factors = {'L0_attn_W_qkv': 7.966,
     'L0_attn_W_z': 8.0,
     'L0_attn_W_b': 8.0,
     'L0_attn_W_a': 8.0,
     'L0_attn_conv_w': 8.0,
     'L0_ffn_w_gate_up': 6.229,
     'L0_ffn_w_down': 5.844}
    for name, (base, spread) in spreads.items():
        noise = np.random.default_rng([zlib.crc32(name.encode()), seed]).standard_normal(out[name].shape)
        drawn = base * np.exp(spread * noise) if base else spread * noise
        out[name] = jnp.asarray(drawn.astype(out[name].dtype))
    for name, factor in factors.items():
        out[name] = (out[name] * factor).astype(out[name].dtype)
    return out
```

```python
from contextlib import ExitStack

import concourse.bass as bass
from concourse import mybir
from typing import Any, NamedTuple

F32 = mybir.dt.float32
BF16 = mybir.dt.bfloat16
ALU = mybir.AluOpType
ACT = mybir.ActivationFunctionType

P = 128
BATCH, SEQ, D = 4, 1024, 256
KH, VH = 16, 32
C = 128
NC = 4
TOK = C * NC
TILES_PER_BATCH = SEQ // TOK
KD = D // P
KEY_DIM = KH * P
CONV_K = 4
TAIL = CONV_K - 1
INTER = 1024
NI = INTER // P
NU = 2 * NC
BL = 32
NBL = C // BL
SOLVE_OPS = 2 * (BL - 1)
EPS_NORM = 1e-6
EPS_LN = 1e-5
GATE_MIN = 0.25
BETA, G_, EXP_G, EXP_REST, EXP_ALL = range(5)
RQ, NK, NAA, EGQ = 0, NC, 2 * NC, 4 * NC
VEC = (0, 1, 3, 4)
SCALAR_OPS = 7
MLP_BATCHES = 12
POOL_SETUP = 15
DVE_SETUP = 4 + 3 + KD * BATCH + 4 + 3 + 4 * BATCH + MLP_BATCHES


class Item(NamedTuple):

    m: Any
    p: int
    k: Any

    @property
    def n(self):
        return 2 * self.m + self.p


def adaln_block(nc, x, w_qkv, w_z, w_b, w_a, conv_w, conv_b, dt_bias, a_log, gamma, w_out,
                w_gate_up, w_down, cond, w_mod, out):
    ctx = ExitStack()

    def sb(name, shape, dt=F32):
        return ctx.enter_context(nc.sbuf_tensor(name, shape, dt))

    def sem(name):
        return ctx.enter_context(nc.semaphore(name))

    with ctx:
        mask_incl = sb("mask_incl", [P, P])
        mask_strict = sb("mask_strict", [P, P])
        mask_after = sb("mask_after", [P, P])
        ident = sb("ident", [P, P])
        ones = sb("ones", [P, P])
        eye_blocks = sb("eye_blocks", [BL, BL * BL])
        minus_half = sb("minus_half", [P, 8])
        zero_b = sb("zero_b", [P, 512], BF16)
        conv_par = sb("conv_par", [P, KH, 4, 5])
        w_ba = sb("w_ba", [P, KD, 2 * VH])
        dt_b = sb("dt_b", [P, VH])
        neg_exp_a = sb("neg_exp_a", [P, VH])
        gamma_c = sb("gamma_c", [P, 1])
        cond_t = sb("cond_t", [P, KD, BATCH])
        cond_th = sb("cond_th", [P, KD, BATCH])
        cond_silu = sb("cond_silu", [P, KD, BATCH])
        mod_t = sb("mod_t", [P, 4, KD, BATCH])
        gate_rows = sb("gate_rows", [P, BATCH, 2, D])
        wgu_t = sb("wgu_t", [P, KD, 2 * INTER])
        wd_t = sb("wd_t", [P, NI, D])
        xt = sb("xt", [P, NC, D])
        ht = sb("ht", [P, KD, TOK])
        stats = sb("stats", [P, NC, 6])
        mean_var = sb("mean_var", [P, NC, 2])
        rstd = sb("rstd", [P, NC])
        mod_b = sb("mod_b", [P, 4, KD])
        gate_b = sb("gate_b", [P, 2, D])
        au = sb("au", [P, NC, VH])
        th_b = sb("th_b", [P, NC, VH])
        table = sb("table", [P, 5, NC, VH])
        states = sb("states", [P, KH, 2 * P])
        tails = sb("tails", [P, KH, 4, TAIL])
        wa = [sb(f"wa{p}", [P, KD, 4 * P]) for p in range(2)]
        wz = [sb(f"wz{p}", [P, KD, 2 * P]) for p in range(2)]
        wo = [sb(f"wo{p}", [P, 2, D]) for p in range(2)]
        qt = [sb(f"qt{p}", [P, TOK]) for p in range(2)]
        kt = [sb(f"kt{p}", [P, TOK]) for p in range(2)]
        lt = [sb(f"lt{p}", [P, NU, C]) for p in range(2)]
        pt = [sb(f"pt{p}", [P, NU, C]) for p in range(2)]
        vs = [sb(f"vs{p}", [P, NU, P]) for p in range(2)]
        k2 = [sb(f"k2{p}", [P, NU, P]) for p in range(2)]
        sc = [sb(f"sc{p}", [P, 5, NC, 2]) for p in range(2)]
        sca = [sb(f"sca{p}", [P, 6 * NC]) for p in range(2)]
        sw = [sb(f"sw{p}", [P, 2 * P]) for p in range(2)]
        cwp = sb("cwp", [P, 4, 5])
        g_item = sb("g_item", [P, NC, 2])
        gm = sb("gm", [P, NU, C])
        raw = sb("raw", [P, 4, TAIL + TOK])
        cv_th = sb("cv_th", [P, 8, TOK])
        cv, th, ff = cv_th[:, 0:4, :], cv_th[:, 4:8, :], cv_th
        vt = sb("vt", [P, 2, TOK])
        sq = sb("sq", [P, 2, TOK])
        ff_th, ff_g = vt, sq
        dec = sb("dec", [P, NU, C])
        kkm = sb("kkm", [P, NC, C])
        kqm = sb("kqm", [P, NC, C])
        ss = sb("ss", [P, 2 * NC])
        rs = sb("rs", [P, 2 * NC])
        rk2 = sb("rk2", [P, 3 * NC])
        ktok = sb("ktok", [P, NC, P])
        blocks = sb("blocks", [NU * NBL, BL * BL])
        tinv = sb("tinv", [NU * NBL, BL * BL])
        solve_tmp = sb("solve_tmp", [NU * NBL, BL * BL // 4 + BL])
        t32 = sb("t32", [P, NU, BL])
        minv = sb("minv", [P, NU, C])
        t64 = sb("t64", [64, NU, 64])
        q1s = sb("q1s", [P, NU, BL])
        q2s = sb("q2s", [P, NU, 64])
        rn = sb("rn", [P, 2, P])
        tmpq = sb("tmpq", [P, 2, P])
        us = sb("us", [P, 2, P])
        thz = sb("thz", [P, 2 * P])
        sg = sb("sg", [P, 2, 2 * P])
        ob = sb("ob", [P, 2, 2 * P])
        ssq = sb("ssq", [P, 2, 2])
        rr = sb("rr", [P, 2, 2])
        gt = sb("gt", [P, 2, P])
        got = sb("got", [P, 2, P])

        junk = q1s[:, 0:NC, :]
        hn = gm[:, :, :].rearrange("p (c a) i -> p c (a i)", c=NC)
        x1 = dec[:, :, :].rearrange("p (c a) i -> p c (a i)", c=NC)
        y_tmp = raw[:, :, 0:D]
        a_abs, a_exp, a_ln = (kqm[:, i, :].rearrange("p (c h) -> p c h", c=NC) for i in range(3))

        l_scr = nc.dram_tensor("l_scratch", [NU * NBL, BL * BL], F32, kind="Internal").ap()
        t_scr = nc.dram_tensor("t_scratch", [NU * NBL, BL * BL], F32, kind="Internal").ap()

        Y = [ctx.enter_context(nc.psum_tensor(f"y{i}", [P, 512], F32)) for i in range(2)]
        PB = [ctx.enter_context(nc.psum_tensor(f"pb{i}", [P, 512], F32)) for i in range(2)]
        R = [ctx.enter_context(nc.psum_tensor(f"r{i}", [P, 512], F32)) for i in range(4)]

        names = """pool_setup in_small in_cond in_wmod in_gu in_down in_conv act_setup pe_setup dve_setup
        x_in ln_stats ln_eps ln_rstd hn_ready ht_psum ht_ready ba_done au_ready thb_ready abs_ready aexp_ready
        aln_ready g_ready g_mul cum_done exp_ready beta_ready y_clear mod_copied
        x1_half x1_ready gate_done up_done th_ff ff_half ff_ready down_done down_half out_ready out_stored zeroed
        wa0 wa1 wc0 wc1
        a_in gm_ready proj_done raw_in conv_in conv_tap tail_saved d_done d_ready
        th_ready silu_done sq_ready kk_done kq_done kkm_ready kqm_ready norms_done ss_ready
        scal_step sc_ready kt_done ktok_ready k2_ready v_tr vs_ready lt_ready pt_ready
        lb_out lb_in tb_init solve_step tb_out t32_in
        mdiag t64_diag q1_done q1_ready m12_done t21_done m12_ready t21_ready q2_done q2_ready m2_done minv_ready
        s_load s_store ks_done qs_done r_ready tq_ready w_done u_ready su_done pu_done s_upd o_ready
        z_done z_ready sg_ready sq_acc rr_eps rr_ready gt_ready gtr_done got_ready y_done"""
        S = {n: sem(n) for n in names.split()}
        passed = {eng: sem(f"passed_{name}") for name, eng in
                  (("sp", nc.sync), ("pool", nc.gpsimd), ("dve", nc.vector), ("pe", nc.tensor))}
        wa_in, wc_in = [S["wa0"], S["wa1"]], [S["wc0"], S["wc1"]]

        def wait_apart(eng, sem, value):
            eng.wait_ge(sem, value)
            eng.sem_inc(passed[eng], 1)

        def tile_loop(eng, body, batch_start=None):
            with eng.Fori(0, BATCH) as b:
                if batch_start:
                    batch_start(b)
                with eng.Fori(0, TILES_PER_BATCH) as half:
                    t = b * TILES_PER_BATCH + half
                    body(t, b, b * (TILES_PER_BATCH * KH // 2) + half * (KH // 2))

        def slots(eng, m0, A, B, X, C_last):
            last = m0 + (KH // 2 - 1)
            A(Item(m0, 0, 0))
            B(Item(m0, 0, 0))
            X(Item(m0, 0, 0), None, Item(m0, 1, 1))
            with eng.Fori(0, KH // 2 - 1) as i:
                B(Item(m0 + i, 1, 2 * i + 1))
                X(Item(m0 + i, 1, 2 * i + 1), Item(m0 + i, 0, 2 * i), Item(m0 + i + 1, 0, 2 * i + 2))
                B(Item(m0 + i + 1, 0, 2 * i + 2))
                X(Item(m0 + i + 1, 0, 2 * i + 2), Item(m0 + i, 1, 2 * i + 1), Item(m0 + i + 1, 1, 2 * i + 3))
            B(Item(last, 1, KH - 1))
            X(Item(last, 1, KH - 1), Item(last, 0, KH - 2), None)
            C_last(Item(last, 1, KH - 1))

        def unit(h, c):
            return h * NC + c

        block = ctx.enter_context(nc.Block())

        @block.sync
        def _(sp):
            with nc.allow_non_contiguous_dma(reason="small vectors, once"):
                sp.dma_start(cond_t[:, 0, :], cond[:, 0:P].rearrange("b p -> p b")).then_inc(S["in_cond"], 16)
                sp.dma_start(cond_t[:, 1, :], cond[:, P:2 * P].rearrange("b p -> p b")).then_inc(S["in_cond"], 16)
                sp.dma_start(gamma_c[:, :], gamma.rearrange("(p a) -> p a", a=1)).then_inc(S["in_small"], 16)
            sp.dma_start(dt_b[:, :], dt_bias.rearrange("(a h) -> a h", a=1).to_broadcast([P, VH])).then_inc(S["in_small"], 16)
            sp.dma_start(neg_exp_a[:, :], a_log.rearrange("(a h) -> a h", a=1).to_broadcast([P, VH])).then_inc(S["in_small"], 16)
            sp.dma_start(w_ba[:, :, 0:VH], w_b.rearrange("(k p) h -> p k h", p=P)).then_inc(S["in_small"], 16)
            sp.dma_start(w_ba[:, :, VH:2 * VH], w_a.rearrange("(k p) h -> p k h", p=P)).then_inc(S["in_small"], 16)
            sp.dma_start(x1[0:64, 0:2, :].rearrange("t a b -> t (a b)"),
                         conv_w.rearrange("(t c) k -> t (c k)", c=P)).then_inc(S["in_conv"], 16)
            sp.dma_start(x1[0:64, 2, 0:P], conv_b.rearrange("(t c) -> t c", c=P)).then_inc(S["in_conv"], 16)
            sp.dma_start(ff[:, :, :].rearrange("p a b -> p (a b)")[:, 0:KD * 6 * D].rearrange("p (k n) -> p k n", k=KD),
                         w_mod.rearrange("(k p) n -> p k n", p=P)).then_inc(S["in_wmod"], 16)
            for k in range(KD):
                sp.dma_start(raw[:, 2 * k:2 * k + 2, 0:TOK],
                             w_down[k * P:(k + 1) * P, :].rearrange("p (a b) -> p a b", b=TOK)).then_inc(S["in_down"], 16)
            sp.wait_ge(S["pe_setup"], 2)
            sp.dma_start(ff[:, :, :].rearrange("p a (b n) -> p (a b) n", n=D),
                         w_gate_up.rearrange("(o p) n -> p o n", p=P)).then_inc(S["in_gu"], 16)

            def load_wa(p, k):
                w = w_qkv.rearrange("(k p) n -> p k n", p=P)
                sp.dma_start(wa[p][:, :, 0:P], w[:, :, bass.ds(k * P, P)]).then_inc(wa_in[p], 16)
                sp.dma_start(wa[p][:, :, P:2 * P], w[:, :, bass.ds(k * P + KEY_DIM, P)]).then_inc(wa_in[p], 16)
                sp.dma_start(wa[p][:, :, 2 * P:4 * P], w[:, :, bass.ds(k * (2 * P) + 2 * KEY_DIM, 2 * P)]).then_inc(wa_in[p], 16)

            def A(a):
                wait_apart(sp, S["proj_done"], a.n * 4)
                load_wa(0, 0)
                load_wa(1, 1)

            def B(s):
                n = s.n
                if not (isinstance(s.k, int)):
                    wait_apart(sp, S["proj_done"], n * 4)
                    load_wa(1 - s.p, s.k + 1)
                wait_apart(sp, S["y_done"], n * NC)
                sp.dma_start(wz[s.p][:, :, :], w_z.rearrange("(k p) n -> p k n", p=P)[:, :, bass.ds(s.k * (2 * P), 2 * P)]
                             ).then_inc(wc_in[s.p], 16)
                sp.dma_start(wo[s.p][:, :, :], w_out.rearrange("(h p) n -> p h n", p=P)[:, bass.ds(s.k * 2, 2), :]
                             ).then_inc(wc_in[s.p], 16)
                wait_apart(sp, S["lt_ready"], n * NU + NU)
                wait_apart(sp, S["lb_in"], n * 16)
                for b in range(NBL):
                    sp.dma_start(l_scr.rearrange("(u b) (j i) -> b j u i", b=NBL, i=BL)[b],
                                 lt[s.p][b * BL:(b + 1) * BL, :, b * BL:(b + 1) * BL]).then_inc(S["lb_out"], 16)
                wait_apart(sp, S["lb_out"], n * (16 * NBL) + 16 * NBL)
                wait_apart(sp, S["solve_step"], n * SOLVE_OPS)
                sp.dma_start(blocks[:, :], l_scr).then_inc(S["lb_in"], 16)

            def X(s, c, a):
                n = s.n
                wait_apart(sp, S["solve_step"], n * SOLVE_OPS + SOLVE_OPS)
                wait_apart(sp, S["t32_in"], n * 16)
                sp.dma_start(t_scr, tinv[:, :]).then_inc(S["tb_out"], 16)
                wait_apart(sp, S["tb_out"], n * 16 + 16)
                wait_apart(sp, S["mdiag"], n * NBL)
                wait_apart(sp, S["t64_diag"], n * 2)
                wait_apart(sp, S["q1_done"], n)
                sp.dma_start(t32[:, :, :], t_scr.rearrange("(u b) (i c) -> (b i) u c", b=NBL, c=BL)).then_inc(S["t32_in"], 16)

            def tile(t, b, m0):
                wait_apart(sp, S["x1_ready"], t * 2)
                by_tile = x.rearrange("b (t c p) d -> (b t) p c d", c=NC, p=P)
                sp.dma_start(xt[:, :, :], by_tile[bass.ds(t, 1), :, :, :].rearrange("a p c d -> p (a c) d")
                             ).then_inc(S["x_in"], 16)
                slots(sp, m0, A, B, X, lambda c: None)
                wait_apart(sp, S["out_ready"], t * 2 + 2)
                by_tile = out.rearrange("b (t c p) d -> (b t) p c d", c=NC, p=P)
                sp.dma_start(by_tile[bass.ds(t, 1), :, :, :].rearrange("a p c d -> p (a c) d"), y_tmp[:, :, :]
                             ).then_inc(S["out_stored"], 16)

            tile_loop(sp, tile)
            sp.wait_ge(S["out_stored"], 16 * BATCH * TILES_PER_BATCH)

        @block.gpsimd
        def _(pool):
            step = [0]

            def setup(ins, wait=True):
                step[0] += 1
                ins.then_inc(S["pool_setup"], 1)
                if wait:
                    pool.wait_ge(S["pool_setup"], step[0])

            setup(pool.memset(ones[:, :], 1.0), False)
            setup(pool.memset(minus_half[:, :], -0.5), False)
            setup(pool.memset(zero_b[:, :], 0.0), False)
            setup(pool.memset(minv[:, :, :], 0.0), False)
            setup(pool.memset(t64[:, :, :], 0.0), False)
            for m, value in ((mask_incl, 1.0), (mask_strict, 1.0), (mask_after, 1.0), (ident, 0.0)):
                setup(pool.memset(m[:, :], value), False)
            setup(pool.memset(eye_blocks[:, :], 0.0))
            setup(pool.affine_select(out=mask_incl[:, :], in_=mask_incl[:, :], compare_op=ALU.is_ge, fill=0.0,
                                     base=0, pattern=[[1, P]], channel_multiplier=-1), False)
            setup(pool.affine_select(out=mask_strict[:, :], in_=mask_strict[:, :], compare_op=ALU.is_gt, fill=0.0,
                                     base=0, pattern=[[1, P]], channel_multiplier=-1), False)
            setup(pool.affine_select(out=mask_after[:, :], in_=mask_after[:, :], compare_op=ALU.is_gt, fill=0.0,
                                     base=0, pattern=[[-1, P]], channel_multiplier=1), False)
            setup(pool.affine_select(out=ident[:, :], in_=ident[:, :], compare_op=ALU.not_equal, fill=1.0,
                                     base=0, pattern=[[-1, P]], channel_multiplier=1), False)
            setup(pool.affine_select(out=eye_blocks[:, :], in_=eye_blocks[:, :], compare_op=ALU.not_equal, fill=1.0,
                                     base=0, pattern=[[1, BL], [-1, BL]], channel_multiplier=0))

            def deviations(count):
                pool.tensor_scalar(rstd[:, :], mean_var[:, :, 1], 1.0, EPS_LN, ALU.mult, ALU.add).then_inc(S["ln_eps"], 1)
                pool.wait_ge(S["ln_eps"], count)
                pool.tensor_tensor(rstd[:, :], rstd[:, :], minus_half[:, 0:NC], ALU.pow).then_inc(S["ln_rstd"], 1)

            def A(a):
                n = a.n
                wait_apart(pool, S["conv_tap"], n * 12)
                pool.tensor_copy(cwp[:, :, :], conv_par[:, bass.ds(a.k, 1), :, :].rearrange("p a t w -> p (a t) w")
                                 ).then_inc(S["a_in"], 1)
                wait_apart(pool, S["gm_ready"], n * NU)
                pool.tensor_copy(g_item[:, :, :], table[:, G_, :, bass.ds(2 * a.k, 2)]).then_inc(S["a_in"], 1)
                pool.tensor_copy(raw[:, :, 0:TAIL], tails[:, bass.ds(a.k, 1), :, :].rearrange("p a t w -> p (a t) w")
                                 ).then_inc(S["a_in"], 1)
                pool.wait_ge(S["a_in"], n * 3 + 3)
                wait_apart(pool, S["d_done"], n * 2)
                for h in range(2):
                    for c in range(NC):
                        pool.tensor_scalar(gm[:, unit(h, c), :], mask_incl[:, :], g_item[:, c, h:h + 1], 1.0,
                                           ALU.mult, ALU.mult).then_inc(S["gm_ready"], 1)

            def save_tail(a):
                wait_apart(pool, S["raw_in"], a.n * 4 + 4)
                pool.tensor_copy(tails[:, bass.ds(a.k, 1), :, :].rearrange("p a t w -> p (a t) w"),
                                 raw[:, :, TOK:TOK + TAIL]).then_inc(S["tail_saved"], 1)

            def A_first(a):
                A(a)
                save_tail(a)

            def B(s):
                n, p = s.n, s.p
                wait_apart(pool, S["norms_done"], n)
                for i, src in enumerate((qt[p], kt[p])):
                    pool.wait_ge(S["silu_done"], n * 4 + i + 1)
                    pool.tensor_tensor(sq[:, i, :], src[:, :], src[:, :], ALU.mult).then_inc(S["sq_ready"], 1)
                wait_apart(pool, S["y_done"], n * NC)
                base = n * SCALAR_OPS
                pool.tensor_copy(sc[p][:, :, :, :], table[:, :, :, bass.ds(2 * s.k, 2)]).then_inc(S["scal_step"], 1)
                wait_apart(pool, S["ss_ready"], n + 1)
                rk = rs[:, NC:2 * NC]
                pool.tensor_tensor(rs[:, :], ss[:, :], minus_half[:, :], ALU.pow).then_inc(S["scal_step"], 1)
                wait_apart(pool, S["scal_step"], base + 2)
                pool.tensor_scalar(sca[p][:, RQ:RQ + NC], rs[:, 0:NC], float(P) ** -0.5, 1.0, ALU.mult, ALU.mult
                                   ).then_inc(S["scal_step"], 1)
                pool.tensor_tensor(rk2[:, 0:NC], ss[:, NC:2 * NC], rk, ALU.mult).then_inc(S["scal_step"], 1)
                pool.tensor_scalar(rk2[:, NC:2 * NC], rk, -1.0, 1.0, ALU.mult, ALU.mult).then_inc(S["scal_step"], 1)
                wait_apart(pool, S["scal_step"], base + 5)
                pool.tensor_scalar(sca[p][:, NK:NK + NC], rk2[:, 0:NC], 0.5, 1.0, ALU.mult, ALU.mult
                                   ).then_inc(S["scal_step"], 1)
                pool.tensor_tensor(rk2[:, 2 * NC:3 * NC], rk2[:, NC:2 * NC], rk, ALU.mult).then_inc(S["scal_step"], 1)
                wait_apart(pool, S["scal_step"], base + 7)
                for h in range(2):
                    pool.tensor_tensor(sca[p][:, NAA + h * NC:NAA + (h + 1) * NC], rk2[:, 2 * NC:3 * NC],
                                       sc[p][:, BETA, :, h], ALU.mult).then_inc(S["sc_ready"], 1)
                    pool.tensor_tensor(sca[p][:, EGQ + h * NC:EGQ + (h + 1) * NC], sca[p][:, RQ:RQ + NC],
                                       sc[p][:, EXP_G, :, h], ALU.mult).then_inc(S["sc_ready"], 1)
                wait_apart(pool, S["ktok_ready"], n + 1)
                for h in range(2):
                    for c in range(NC):
                        pool.tensor_scalar(k2[p][:, unit(h, c), :], ktok[:, c, :], sc[p][:, EXP_REST, c, h:h + 1], 1.0,
                                           ALU.mult, ALU.mult).then_inc(S["k2_ready"], 1)

            def load_state(c):
                wait_apart(pool, S["s_store"], c.n)
                pool.tensor_copy(sw[c.p][:, :], states[:, bass.ds(c.k, 1), :].rearrange("p a n -> p (a n)")
                                 ).then_inc(S["s_load"], 1)

            def store_state(c):
                wait_apart(pool, S["s_upd"], c.n * NU + NU)
                pool.tensor_copy(states[:, bass.ds(c.k, 1), :].rearrange("p a n -> p (a n)"), sw[c.p][:, :]
                                 ).then_inc(S["s_store"], 1)

            def steps(c):
                n = c.n
                for j in range(NC):
                    pool.wait_ge(S["z_ready"], n * NC + j + 1)
                    wait_apart(pool, S["gt_ready"], n * NU + 2 * max(j - 1, 0))
                    pool.tensor_scalar(sg[:, j % 2, :], thz[:, :], 0.5, 0.5, ALU.mult, ALU.add).then_inc(S["sg_ready"], 1)
                    wait_apart(pool, S["sq_acc"], n * NU + 2 * j + 2)
                    pool.tensor_scalar(ssq[:, j % 2, :], ssq[:, j % 2, :], 1.0 / P, EPS_NORM, ALU.mult, ALU.add
                                       ).then_inc(S["rr_eps"], 1)
                    pool.wait_ge(S["rr_eps"], n * NC + j + 1)
                    pool.tensor_tensor(rr[:, j % 2, :], ssq[:, j % 2, :], minus_half[:, 0:2], ALU.pow
                                       ).then_inc(S["rr_ready"], 1)

            def X(s, c, a):
                if c is not None:
                    load_state(c)
                wait_apart(pool, S["tb_out"], s.n * 16)
                pool.tensor_copy(tinv[:, :], eye_blocks[:, :]).then_inc(S["tb_init"], 1)
                if a is not None:
                    A(a)
                if c is not None:
                    steps(c)
                if a is not None:
                    save_tail(a)
                if c is not None:
                    store_state(c)

            def C_last(c):
                load_state(c)
                steps(c)
                store_state(c)

            def batch_start(b):
                wait_apart(pool, S["s_store"], b * (TILES_PER_BATCH * KH))
                pool.memset(states[:, :, :], 0.0).then_inc(S["zeroed"], 1)
                pool.memset(tails[:, :, :, :], 0.0).then_inc(S["zeroed"], 1)
                wait_apart(pool, S["zeroed"], b * 2 + 2)

            def tile(t, b, m0):
                pool.wait_ge(S["dve_setup"], DVE_SETUP)
                pool.wait_ge(S["ht_ready"], t * 4)
                wait_apart(pool, S["out_ready"], t * 2)
                pool.tensor_copy(mod_b[:, :, :], mod_t[:, :, :, bass.ds(b, 1)].rearrange("p v k a -> p v (k a)")
                                 ).then_inc(S["mod_copied"], 1)
                pool.tensor_copy(gate_b[:, :, :], gate_rows[:, bass.ds(b, 1), :, :].rearrange("p a g d -> p (a g) d")
                                 ).then_inc(S["mod_copied"], 1)
                wait_apart(pool, S["ln_stats"], t * 16 + 8)
                deviations(t * 2 + 1)
                wait_apart(pool, S["thb_ready"], t + 1)
                pool.tensor_scalar(table[:, BETA, :, :], th_b[:, :, :], 0.5, 0.5, ALU.mult, ALU.add).then_inc(S["beta_ready"], 1)
                pool.wait_ge(S["beta_ready"], t + 1)
                pool.wait_ge(S["g_ready"], t + 1)
                pool.wait_ge(S["exp_ready"], t + 1)
                wait_apart(pool, S["out_stored"], t * 16)
                slots(pool, m0, A_first, B, X, C_last)
                wait_apart(pool, S["ln_stats"], t * 16 + 16)
                deviations(t * 2 + 2)

            tile_loop(pool, tile, batch_start)

        @block.scalar
        def _(act):
            act.wait_ge(S["in_cond"], 32)
            act.activation(cond_th[:, :, :], cond_t[:, :, :], ACT.Tanh, scale=0.5).then_inc(S["act_setup"], 1)
            act.wait_ge(S["in_small"], 16 * 5)
            act.activation(neg_exp_a[:, :], neg_exp_a[:, :], ACT.Exp).then_inc(S["act_setup"], 1)

            def evacuate(a, i):
                n = a.n
                act.wait_ge(S["proj_done"], n * 4 + i + 1)
                if i == 0:
                    act.wait_ge(S["a_in"], n * 3 + 3)
                    act.wait_ge(S["silu_done"], n * 4)
                    act.wait_ge(S["tail_saved"], n)
                act.activation(raw[:, i, TAIL:TAIL + TOK], PB[i % 2][:, :], ACT.Copy).then_inc(S["raw_in"], 1)
                act.activation(cv[:, i, :], PB[i % 2][:, :], ACT.Identity, bias=cwp[:, i, 4:5], scale=cwp[:, i, 0:1]
                               ).then_inc(S["conv_in"], 1)

            def decay(a, h):
                act.wait_ge(S["d_done"], a.n * 2 + h + 1)
                act.wait_ge(S["pt_ready"], a.n * 2)
                act.activation(dec[:, h * NC:(h + 1) * NC, :], PB[h][:, :].rearrange("p (c i) -> p c i", c=NC), ACT.Exp
                               ).then_inc(S["d_ready"], 1)

            def A(a):
                for i in range(4):
                    evacuate(a, i)
                for h in range(2):
                    decay(a, h)

            def B(s):
                n, p = s.n, s.p
                for i in range(4):
                    act.wait_ge(S["conv_tap"], n * 12 + 3 * i + 3)
                    act.activation(th[:, i, :], cv[:, i, :], ACT.Tanh, scale=0.5).then_inc(S["th_ready"], 1)
                act.wait_ge(S["kt_done"], n + 1)
                act.wait_ge(S["k2_ready"], n * NU)
                act.activation(ktok[:, :, :], PB[1][:, :].rearrange("p (c i) -> p c i", c=NC), ACT.Copy
                               ).then_inc(S["ktok_ready"], 1)
                act.wait_ge(S["y_done"], n * NC)
                act.wait_ge(S["sc_ready"], n * 4 + 4)
                for h in range(2):
                    act.wait_ge(S["v_tr"], n * 2 + h + 1)
                    for c in range(NC):
                        act.activation(vs[p][:, unit(h, c), :], PB[h][:, c * P:(c + 1) * P], ACT.Copy,
                                       scale=sca[p][:, NK + c:NK + c + 1]).then_inc(S["vs_ready"], 1)

            def flush(c, j):
                n = c.n
                act.wait_ge(S["gtr_done"], n * NC + j + 1)
                act.wait_ge(S["y_done"], n * NC + j + NC)
                act.activation(got[:, :, :], R[3][:, 0:2 * P].rearrange("p (h i) -> p h i", h=2), ACT.Copy,
                               scale=gamma_c[:, 0:1]).then_inc(S["got_ready"], 1)

            def recur(c, a):
                n, p = c.n, c.p
                act.wait_ge(S["t32_in"], n * 16 + 16)
                act.wait_ge(S["q2_done"], n)
                for b in range(2):
                    act.activation(t64[b * BL:(b + 1) * BL, :, b * BL:(b + 1) * BL], t32[b * BL:(b + 1) * BL, :, :], ACT.Copy
                                   ).then_inc(S["t64_diag"], 1)
                act.wait_ge(S["q1_done"], n + 1)
                act.activation(q1s[:, :, :], R[0][:, 0:NU * BL].rearrange("p (u i) -> p u i", u=NU), ACT.Copy
                               ).then_inc(S["q1_ready"], 1)
                if a is not None:
                    evacuate(a, 0)
                act.wait_ge(S["m12_done"], n + 1)
                act.wait_ge(S["mdiag"], n * NBL + NBL)
                for b in range(2):
                    lo, mid = 64 * b, 64 * b + BL
                    act.activation(minv[lo:mid, :, mid:mid + BL],
                                   R[1][lo:mid, 0:NU * BL].rearrange("p (u i) -> p u i", u=NU), ACT.Copy
                                   ).then_inc(S["m12_ready"], 1)
                if a is not None:
                    evacuate(a, 1)
                act.wait_ge(S["m2_done"], n + 1)
                act.activation(minv[0:64, :, 64:P], R[1][0:64, :].rearrange("p (u i) -> p u i", u=NU), ACT.Copy
                               ).then_inc(S["minv_ready"], 1)
                for j in range(NC):
                    act.wait_ge(S["qs_done"], n * NC + j + 1)
                    act.wait_ge(S["o_ready"], n * NC + j)
                    for h in range(2):
                        e = EGQ + h * NC + j
                        act.activation(tmpq[:, h, :], R[1][:, h * P:(h + 1) * P], ACT.Copy, scale=sca[p][:, e:e + 1]
                                       ).then_inc(S["tq_ready"], 1)
                    if a is not None:
                        if j < 2:
                            evacuate(a, 2 + j)
                        else:
                            decay(a, j - 2)
                    act.wait_ge(S["w_done"], n * NC + j + 1)
                    act.wait_ge(S["pu_done"], n * NC + j)
                    for h in range(2):
                        e = NAA + h * NC + j
                        act.activation(us[:, h, :], R[1][:, (2 + h) * P:(3 + h) * P], ACT.Copy, scale=sca[p][:, e:e + 1]
                                       ).then_inc(S["u_ready"], 1)
                    act.wait_ge(S["z_done"], n * NC + j + 1)
                    act.wait_ge(S["sg_ready"], n * NC + j)
                    act.activation(thz[:, :], R[1][:, 0:2 * P], ACT.Tanh, scale=0.5).then_inc(S["z_ready"], 1)
                    act.wait_ge(S["o_ready"], n * NC + j + 1)
                    for h in range(2):
                        act.activation(junk, ob[:, j % 2, h * P:(h + 1) * P].rearrange("p (a b) -> p a b", a=NC), ACT.Square,
                                       accum_out=ssq[:, j % 2, h:h + 1]).then_inc(S["sq_acc"], 1)
                        act.wait_ge(S["sq_acc"], n * NU + 2 * j + h + 1)
                    if j > 0:
                        flush(c, j - 1)
                flush(c, NC - 1)

            def X(s, c, a):
                if c is None:
                    A(a)
                else:
                    recur(c, a)

            def modulate(count, mods, v):
                act.wait_ge(S["mod_copied"], mods)
                for k in range(KD):
                    act.wait_ge(S["ht_psum"], count + k + 1)
                    act.activation(ht[:, k, :], R[k][:, :], ACT.Identity, bias=mod_b[:, v, k:k + 1],
                                   scale=mod_b[:, v + 1, k:k + 1]).then_inc(S["ht_ready"], 1)

            def tile(t, b, m0):
                modulate(t * 4, t * 2 + 2, 0)
                act.wait_ge(S["au_ready"], t + 1)
                act.activation(th_b[:, :, :], R[2][:, 0:NC * 2 * VH].rearrange("p (c h) -> p c h", c=NC)[:, :, 0:VH], ACT.Tanh,
                               scale=0.5).then_inc(S["thb_ready"], 1)
                act.activation(a_abs[:, :, :], au[:, :, :], ACT.Abs).then_inc(S["abs_ready"], 1)
                act.wait_ge(S["abs_ready"], t + 1)
                act.activation(a_exp[:, :, :], a_abs[:, :, :], ACT.Exp, scale=-1.0).then_inc(S["aexp_ready"], 1)
                act.wait_ge(S["aexp_ready"], t + 1)
                act.activation(a_ln[:, :, :], a_exp[:, :, :], ACT.Ln, bias=ones[:, 0:1]).then_inc(S["aln_ready"], 1)
                act.wait_ge(S["cum_done"], t + 1)
                act.activation(table[:, EXP_G:EXP_ALL + 1, :, :].rearrange("p e c h -> p (e c h)"), R[3][:, 0:3 * NC * VH],
                               ACT.Exp).then_inc(S["exp_ready"], 1)
                act.wait_ge(S["out_stored"], t * 16)
                slots(act, m0, A, B, X, lambda c: recur(c, None))
                modulate(t * 4 + 2, t * 2 + 2, 2)
                for i in range(NI):
                    bank = PB[0] if i % 2 == 0 else R[2]
                    act.wait_ge(S["gate_done"], t * NI + i + 1)
                    if i >= 2:
                        act.wait_ge(S["ff_half"], t * NI + i - 1)
                    else:
                        act.wait_ge(S["ff_half"], t * NI)
                    act.activation(ff_th[:, i % 2, :], bank[:, :], ACT.Tanh, scale=0.5).then_inc(S["th_ff"], 1)

            tile_loop(act, tile)

        @block.vector
        def _(dve):
            step = [0]

            def setup(ins, wait=False):
                step[0] += 1
                ins.then_inc(S["dve_setup"], 1)
                if wait:
                    dve.wait_ge(S["dve_setup"], step[0])

            for r in R:
                setup(dve.memset(r[:, :], 0.0))
            dve.wait_ge(S["act_setup"], 2)
            setup(dve.tensor_scalar(neg_exp_a[:, :], neg_exp_a[:, :], -1.0, None, ALU.mult))
            setup(dve.scalar_tensor_tensor(out=cond_silu[:, :, :], in0=cond_th[:, :, :], scalar=1.0, in1=cond_t[:, :, :],
                                           op0=ALU.add, op1=ALU.mult), True)
            setup(dve.tensor_scalar(cond_silu[:, :, :], cond_silu[:, :, :], 0.5, None, ALU.mult), True)
            dve.wait_ge(S["pool_setup"], POOL_SETUP)
            cond_rows = hn[:, :, :].rearrange("p a (b i) -> p (a b) i", i=P)
            for k in range(KD):
                for b in range(BATCH):
                    setup(dve.tensor_scalar(cond_rows[:, k * BATCH + b, :], ones[:, :], cond_silu[:, k, b:b + 1], None,
                                            ALU.mult))
            dve.wait_ge(S["pe_setup"], 1)
            cols = R[0][:, 0:5 * 64].rearrange("p (w t) -> p w t", w=5)
            for i in range(2):
                setup(dve.tensor_copy(conv_par[:, :, i, :].rearrange("p k w -> p w k"), cols[:, :, i * KH:(i + 1) * KH]))
            for j in range(2):
                v = cols[:, :, 2 * KH:4 * KH].rearrange("p w (k j) -> p w k j", j=2)
                setup(dve.tensor_copy(conv_par[:, :, 2 + j, :].rearrange("p k w -> p w k"), v[:, :, :, j]))
            dve.wait_ge(S["pe_setup"], 2)
            setup(dve.tensor_copy(mod_t[:, :, :, :].rearrange("p v k b -> p (v k b)"), R[1][:, 0:4 * KD * BATCH]), True)
            for v in (1, 3):
                setup(dve.tensor_scalar(mod_t[:, v, :, :], mod_t[:, v, :, :], 1.0, None, ALU.add))
            for b, bank in enumerate((R[2], R[3], PB[0], PB[1])):
                row = bank[:, :].rearrange("p (g d) -> p g d", g=2)
                sign = vt[:, 0, :].rearrange("p (g d) -> p g d", g=2)
                setup(dve.tensor_scalar(sign, row, 0.0, 2.0, ALU.is_ge, ALU.mult), True)
                setup(dve.tensor_scalar(sign, sign, -1.0, None, ALU.add), True)
                setup(dve.tensor_tensor(gate_rows[:, b, :, :], row, sign, ALU.mult), True)
                setup(dve.scalar_tensor_tensor(out=gate_rows[:, b, :, :], in0=gate_rows[:, b, :, :], scalar=GATE_MIN,
                                               in1=sign, op0=ALU.max, op1=ALU.mult), True)
            for n in range(MLP_BATCHES):
                dve.wait_ge(S["pe_setup"], 3 + n)
                if n < 8:
                    k, o = n // 4, n % 4
                    dst = wgu_t[:, k, o * 512:(o + 1) * 512]
                else:
                    dst = wd_t[:, 2 * (n - 8):2 * (n - 8) + 2, :].rearrange("p i d -> p (i d)")
                setup(dve.tensor_copy(dst, R[n % 4][:, :]))
            assert step[0] == DVE_SETUP

            def taps(a, i):
                n = a.n
                dve.wait_ge(S["raw_in"], n * 4 + i + 1)
                dve.wait_ge(S["conv_in"], n * 4 + i + 1)
                for j in range(1, CONV_K):
                    dve.scalar_tensor_tensor(out=cv[:, i, :], in0=raw[:, i, TAIL - j:TAIL - j + TOK],
                                             scalar=cwp[:, i, j:j + 1], in1=cv[:, i, :], op0=ALU.mult, op1=ALU.add
                                             ).then_inc(S["conv_tap"], 1)
                    if j < CONV_K - 1:
                        dve.wait_ge(S["conv_tap"], n * 12 + 3 * i + j)

            def A(a):
                for i in range(4):
                    taps(a, i)

            def B(s):
                n, p = s.n, s.p
                dve.wait_ge(S["y_done"], n * NC)
                dve.wait_ge(S["v_tr"], n * 2)
                for i, dst in enumerate((qt[p][:, :], kt[p][:, :], vt[:, 0, :], vt[:, 1, :])):
                    dve.wait_ge(S["th_ready"], n * 4 + i + 1)
                    dve.scalar_tensor_tensor(out=dst, in0=th[:, i, :], scalar=1.0, in1=cv[:, i, :],
                                             op0=ALU.add, op1=ALU.mult).then_inc(S["silu_done"], 1)
                dve.wait_ge(S["kk_done"], n + 1)
                dve.tensor_tensor(kkm[:, :, :], PB[0][:, :].rearrange("p (c i) -> p c i", c=NC),
                                  mask_strict[:, :].unsqueeze(1).to_broadcast([P, NC, C]), ALU.mult).then_inc(S["kkm_ready"], 1)
                dve.wait_ge(S["kq_done"], n + 1)
                dve.tensor_tensor(kqm[:, :, :], PB[1][:, :].rearrange("p (c i) -> p c i", c=NC),
                                  mask_incl[:, :].unsqueeze(1).to_broadcast([P, NC, C]), ALU.mult).then_inc(S["kqm_ready"], 1)
                dve.wait_ge(S["norms_done"], n + 1)
                dve.tensor_scalar(ss[:, :], PB[0][:, 0:2 * NC], 4 * EPS_NORM, None, ALU.add).then_inc(S["ss_ready"], 1)
                dve.wait_ge(S["d_ready"], n * 2 + 2)
                dve.wait_ge(S["sc_ready"], n * 4 + 4)
                dve.wait_ge(S["kkm_ready"], n + 1)
                for h in range(2):
                    for c in range(NC):
                        u, e = unit(h, c), NAA + h * NC + c
                        dve.scalar_tensor_tensor(out=lt[p][:, u, :], in0=kkm[:, c, :], scalar=sca[p][:, e:e + 1],
                                                 in1=dec[:, u, :], op0=ALU.mult, op1=ALU.mult).then_inc(S["lt_ready"], 1)
                dve.wait_ge(S["kqm_ready"], n + 1)
                for h in range(2):
                    us_ = slice(h * NC, (h + 1) * NC)
                    dve.tensor_tensor(pt[p][:, us_, :], kqm[:, :, :], dec[:, us_, :], ALU.mult).then_inc(S["pt_ready"], 1)

            def solve(s, j0, j1):
                base = s.n * SOLVE_OPS
                if j0 == 0:
                    dve.wait_ge(S["lb_in"], s.n * 16 + 16)
                    dve.wait_ge(S["tb_init"], s.n + 1)
                for j in range(j0, j1):
                    rows, cols = BL - 1 - j, j + 1
                    if j > 0:
                        dve.wait_ge(S["solve_step"], base + 2 * j)
                    coef = blocks[:, j * BL + j + 1:(j + 1) * BL].unsqueeze(2).to_broadcast([NU * NBL, rows, cols])
                    row = tinv[:, j * BL:j * BL + cols].unsqueeze(1).to_broadcast([NU * NBL, rows, cols])
                    prod = solve_tmp[:, 0:rows * cols].rearrange("p (i c) -> p i c", c=cols)
                    dve.tensor_tensor(prod, coef, row, ALU.mult).then_inc(S["solve_step"], 1)
                    dve.wait_ge(S["solve_step"], base + 2 * j + 1)
                    rest = tinv[:, (j + 1) * BL:].rearrange("p (i c) -> p i c", c=BL)[:, :, 0:cols]
                    dve.tensor_tensor(rest, rest, prod, ALU.add).then_inc(S["solve_step"], 1)

            def flush(c, j):
                n = c.n
                dve.wait_ge(S["rr_ready"], n * NC + j + 1)
                dve.wait_ge(S["sg_ready"], n * NC + j + 1)
                dve.wait_ge(S["gtr_done"], n * NC + j)
                for h in range(2):
                    dve.scalar_tensor_tensor(out=gt[:, h, :], in0=ob[:, j % 2, h * P:(h + 1) * P], scalar=rr[:, j % 2, h:h + 1],
                                             in1=sg[:, j % 2, h * P:(h + 1) * P], op0=ALU.mult, op1=ALU.mult
                                             ).then_inc(S["gt_ready"], 1)

            def recur(s, c, a):
                n, p = c.n, c.p
                dve.wait_ge(S["t32_in"], n * 16 + 16)
                dve.wait_ge(S["w_done"], n * NC)
                for b in range(NBL):
                    blk = slice(b * BL, (b + 1) * BL)
                    dve.transpose(minv[blk, :, blk], t32[blk, :, :]).then_inc(S["mdiag"], 1)
                dve.wait_ge(S["t21_done"], n + 1)
                dve.tensor_copy(t64[BL:64, :, 0:BL], R[2][BL:64, 0:NU * BL].rearrange("p (u i) -> p u i", u=NU)
                                ).then_inc(S["t21_ready"], 1)
                dve.wait_ge(S["q2_done"], n + 1)
                dve.tensor_copy(q2s[64:P, :, :], R[0][64:P, :].rearrange("p (u i) -> p u i", u=NU)).then_inc(S["q2_ready"], 1)
                for j in range(NC):
                    dve.wait_ge(S["ks_done"], n * NC + j + 1)
                    dve.wait_ge(S["vs_ready"], n * NU + NU)
                    dve.wait_ge(S["w_done"], n * NC + j)
                    for h in range(2):
                        dve.scalar_tensor_tensor(out=rn[:, h, :], in0=R[0][:, h * P:(h + 1) * P],
                                                 scalar=sc[p][:, EXP_G, j, h:h + 1], in1=vs[p][:, unit(h, j), :],
                                                 op0=ALU.mult, op1=ALU.subtract).then_inc(S["r_ready"], 1)
                    if s is not None:
                        solve(s, 8 * j, 8 * j + 4)
                    dve.wait_ge(S["su_done"], n * NC + j + 1)
                    for h in range(2):
                        dve.scalar_tensor_tensor(out=sw[p][:, h * P:(h + 1) * P], in0=sw[p][:, h * P:(h + 1) * P],
                                                 scalar=sc[p][:, EXP_ALL, j, h:h + 1], in1=R[2][:, h * P:(h + 1) * P],
                                                 op0=ALU.mult, op1=ALU.add).then_inc(S["s_upd"], 1)
                    dve.wait_ge(S["pu_done"], n * NC + j + 1)
                    dve.wait_ge(S["tq_ready"], n * NU + 2 * j + 2)
                    dve.scalar_tensor_tensor(out=ob[:, j % 2, :], in0=R[0][:, 2 * P:4 * P], scalar=sca[p][:, RQ + j:RQ + j + 1],
                                             in1=tmpq[:, :, :].rearrange("p h i -> p (h i)"), op0=ALU.mult, op1=ALU.add
                                             ).then_inc(S["o_ready"], 1)
                    if j > 0:
                        flush(c, j - 1)
                    if a is not None:
                        taps(a, j)
                    if s is not None:
                        solve(s, 8 * j + 4, min(8 * j + 8, BL - 1))
                flush(c, NC - 1)

            def X(s, c, a):
                if c is None:
                    A(a)
                    solve(s, 0, BL - 1)
                else:
                    recur(s, c, a)

            def layernorm(src, t, second):
                base = t * 16 + 8 * second
                for c in range(NC):
                    dve.bn_stats(stats[:, c, :], src[:, c, :]).then_inc(S["ln_stats"], 1)
                wait_apart(dve, S["ln_stats"], base + 4)
                for c in range(NC):
                    dve.bn_aggr(mean_var[:, c, :], stats[:, c, :]).then_inc(S["ln_stats"], 1)
                dve.wait_ge(S["ln_stats"], base + 8)
                dve.wait_ge(S["ln_rstd"], t * 2 + second + 1)
                for c in range(NC):
                    dve.tensor_scalar(hn[:, c, :], src[:, c, :], mean_var[:, c, 0:1], rstd[:, c:c + 1], ALU.subtract, ALU.mult
                                      ).then_inc(S["hn_ready"], 1)

            def gated_add(dst, src, banks, gate, half_sem, done_sem, base):
                for i in range(2):
                    dve.tensor_tensor(y_tmp[:, 2 * i:2 * i + 2, :], banks[i][:, :].rearrange("p (c d) -> p c d", c=2),
                                      gate_b[:, gate, :].unsqueeze(1).to_broadcast([P, 2, D]), ALU.mult).then_inc(half_sem, 1)
                    dve.wait_ge(half_sem, base + i + 1)
                    dve.tensor_tensor(dst[:, 2 * i:2 * i + 2, :], y_tmp[:, 2 * i:2 * i + 2, :], src[:, 2 * i:2 * i + 2, :],
                                      ALU.add).then_inc(done_sem, 1)

            def tile(t, b, m0):
                n_end = (m0 + KH // 2) * 2
                dve.wait_ge(S["x_in"], t * 16 + 16)
                layernorm(xt, t, 0)
                dve.wait_ge(S["ba_done"], t + 1)
                dve.tensor_tensor(au[:, :, :], R[2][:, 0:NC * 2 * VH].rearrange("p (c h) -> p c h", c=NC)[:, :, VH:2 * VH],
                                  dt_b[:, :].unsqueeze(1).to_broadcast([P, NC, VH]), ALU.add).then_inc(S["au_ready"], 1)
                dve.wait_ge(S["aln_ready"], t + 1)
                dve.wait_ge(S["au_ready"], t + 1)
                dve.scalar_tensor_tensor(out=au[:, :, :], in0=au[:, :, :], scalar=0.0, in1=a_ln[:, :, :],
                                         op0=ALU.max, op1=ALU.add).then_inc(S["g_mul"], 1)
                dve.wait_ge(S["g_mul"], t + 1)
                dve.tensor_tensor(table[:, G_, :, :], au[:, :, :], neg_exp_a[:, :].unsqueeze(1).to_broadcast([P, NC, VH]),
                                  ALU.mult).then_inc(S["g_ready"], 1)
                slots(dve, m0, A, B, X, lambda c: recur(None, c, None))
                dve.wait_ge(S["y_done"], n_end * NC + NC)
                dve.wait_ge(S["out_stored"], t * 16)
                dve.wait_ge(S["mod_copied"], t * 2 + 2)
                gated_add(x1, xt, Y, 0, S["x1_half"], S["x1_ready"], t * 2)
                dve.wait_ge(S["x1_ready"], t * 2 + 2)
                layernorm(x1, t, 1)
                for i in range(NI):
                    gate, up = (PB[0], PB[1]) if i % 2 == 0 else (R[2], R[3])
                    dve.wait_ge(S["th_ff"], t * NI + i + 1)
                    dve.wait_ge(S["ff_ready"], t * NI + max(i - 1, 0))
                    dve.scalar_tensor_tensor(out=ff_g[:, i % 2, :], in0=ff_th[:, i % 2, :], scalar=1.0, in1=gate[:, :],
                                             op0=ALU.add, op1=ALU.mult).then_inc(S["ff_half"], 1)
                    dve.wait_ge(S["ff_half"], t * NI + i + 1)
                    dve.wait_ge(S["up_done"], t * NI + i + 1)
                    dve.scalar_tensor_tensor(out=ff[:, i, :], in0=ff_g[:, i % 2, :], scalar=0.5, in1=up[:, :],
                                             op0=ALU.mult, op1=ALU.mult).then_inc(S["ff_ready"], 1)
                dve.wait_ge(S["down_done"], t * 2 + 2)
                gated_add(y_tmp, x1, R, 1, S["down_half"], S["out_ready"], t * 2)

            tile_loop(dve, tile)

        @block.tensor
        def _(pe):
            mm = pe.matmul

            pe.wait_ge(S["pool_setup"], POOL_SETUP)
            pe.wait_ge(S["in_conv"], 32)
            pe.wait_ge(S["dve_setup"], 4)
            taps_rows = x1[0:64, 0:2, :].rearrange("t a b -> t (a b)").rearrange("t (c w) -> t c w", w=CONV_K)
            for w in range(CONV_K):
                pe.transpose(R[0][:, w * 64:(w + 1) * 64], taps_rows[:, :, w], ident[0:64, 0:64])
            pe.transpose(R[0][:, 4 * 64:5 * 64], x1[0:64, 2, 0:P], ident[0:64, 0:64]).then_inc(S["pe_setup"], 1)
            pe.wait_ge(S["in_wmod"], 16)
            pe.wait_ge(S["dve_setup"], 4 + 3 + KD * BATCH)
            wm = ff[:, :, :].rearrange("p a b -> p (a b)")[:, 0:KD * 6 * D].rearrange("p (k n) -> p k n", k=KD)
            for i, v in enumerate(VEC):
                for hh in range(KD):
                    o = (i * KD + hh) * BATCH
                    for k in range(KD):
                        mm(R[1][:, o:o + BATCH], wm[:, k, v * D + hh * P:v * D + (hh + 1) * P], cond_silu[:, k, :],
                           start=(k == 0), stop=(k == KD - 1))
            cond_rows = hn[:, :, :].rearrange("p a (b i) -> p (a b) i", i=P)
            for b, bank in enumerate((R[2], R[3], PB[0], PB[1])):
                for i, v in enumerate((2, 5)):
                    for k in range(KD):
                        last = mm(bank[:, i * D:(i + 1) * D], cond_rows[:, k * BATCH + b, :], wm[:, k, v * D:(v + 1) * D],
                                  start=(k == 0), stop=(k == KD - 1))
            last.then_inc(S["pe_setup"], 1)
            pe.wait_ge(S["in_gu"], 16)
            pe.wait_ge(S["in_down"], 32)
            rows = ff[:, :, :].rearrange("p a (b n) -> p (a b) n", n=D)
            for n in range(MLP_BATCHES):
                pe.wait_ge(S["dve_setup"], DVE_SETUP - MLP_BATCHES + max(n - 3, 0))
                for i in range(4):
                    if n < 8:
                        k, o = n // 4, n % 4 * 4 + i
                        src = rows[:, o, k * P:(k + 1) * P]
                    else:
                        col = (2 * (n - 8) + i // 2) * P
                        src = raw[:, 2 * (i % 2) + col // TOK, col % TOK:col % TOK + P]
                    last = pe.transpose(R[n % 4][:, i * P:(i + 1) * P], src, ident[:, :])
                last.then_inc(S["pe_setup"], 1)

            def project(a, i):
                n = a.n
                bank = PB[i % 2]
                if i == 0:
                    pe.wait_ge(wa_in[a.p], a.m * 48 + 48)
                if i < 2:
                    pe.wait_ge(S["vs_ready"], n * NU)
                else:
                    pe.wait_ge(S["conv_in"], n * 4 + i - 1)
                for k in range(KD):
                    last = mm(bank[:, :], wa[a.p][:, k, i * P:(i + 1) * P], ht[:, k, :], start=(k == 0), stop=(k == KD - 1))
                last.then_inc(S["proj_done"], 1)

            def decay(a, h):
                n = a.n
                pe.wait_ge(S["gm_ready"], n * NU + NU)
                pe.wait_ge(S["conv_in"], n * 4 + 3 + h)
                mm(PB[h][:, :], mask_after[:, :], gm[:, h * NC:(h + 1) * NC, :].rearrange("p c i -> p (c i)"),
                   start=True, stop=True).then_inc(S["d_done"], 1)

            def A(a):
                for i in range(4):
                    project(a, i)
                for h in range(2):
                    decay(a, h)

            def B(s):
                n, p = s.n, s.p
                for i, (rhs, done) in enumerate(((kt[p], S["kk_done"]), (qt[p], S["kq_done"]))):
                    pe.wait_ge(S["d_ready"], n * 2 + i + 1)
                    pe.wait_ge(S["silu_done"], n * 4 + 2)
                    for c in range(NC):
                        cs = slice(c * C, (c + 1) * C)
                        last = mm(PB[i][:, cs], kt[p][:, cs], rhs[:, cs], start=True, stop=True)
                    last.then_inc(done, 1)
                pe.wait_ge(S["kkm_ready"], n + 1)
                pe.wait_ge(S["sq_ready"], n * 2 + 2)
                for i in range(2):
                    for c in range(NC):
                        last = mm(PB[0][:, i * NC + c:i * NC + c + 1], sq[:, i, c * C:(c + 1) * C], ones[:, 0:1],
                                  start=True, stop=True)
                last.then_inc(S["norms_done"], 1)
                pe.wait_ge(S["kqm_ready"], n + 1)
                for c in range(NC):
                    last = pe.transpose(PB[1][:, c * P:(c + 1) * P], kt[p][:, c * C:(c + 1) * C], ident[:, :])
                last.then_inc(S["kt_done"], 1)
                for h in range(2):
                    pe.wait_ge(S["ktok_ready"] if h else S["ss_ready"], n + 1)
                    pe.wait_ge(S["silu_done"], n * 4 + 3 + h)
                    for c in range(NC):
                        last = pe.transpose(PB[h][:, c * P:(c + 1) * P], vt[:, h, c * C:(c + 1) * C], ident[:, :])
                    last.then_inc(S["v_tr"], 1)

            def flush(c, j):
                n, p = c.n, c.p
                pe.wait_ge(S["gt_ready"], n * NU + 2 * j + 2)
                pe.wait_ge(S["got_ready"], n * NC + j)
                for h in range(2):
                    last = pe.transpose(R[3][:, h * P:(h + 1) * P], gt[:, h, :], ident[:, :])
                last.then_inc(S["gtr_done"], 1)
                pe.wait_ge(S["got_ready"], n * NC + j + 1)
                for h in range(2):
                    last = mm(Y[j // 2][:, j % 2 * D:(j % 2 + 1) * D], got[:, h, :], wo[p][:, h, :], start=False, stop=False,
                              skip_group_check=True)
                last.then_inc(S["y_done"], 1)

            def recur(c, a):
                n, p = c.n, c.p
                pe.wait_ge(S["t32_in"], n * 16 + 16)
                pe.wait_ge(S["lt_ready"], n * NU + NU)
                wait_apart(pe, S["o_ready"], n * NC)
                for u in range(NU):
                    for b in range(2):
                        lo, mid, hi = 64 * b, 64 * b + BL, 64 * b + 64
                        last = mm(R[0][mid:hi, u * BL:(u + 1) * BL], lt[p][lo:mid, u, mid:hi], t32[lo:mid, u, :],
                                  start=True, stop=True)
                last.then_inc(S["q1_done"], 1)
                if a is not None:
                    project(a, 0)
                pe.wait_ge(S["q1_ready"], n + 1)
                pe.wait_ge(S["mdiag"], n * NBL + NBL)
                wait_apart(pe, S["z_ready"], n * NC)
                for u in range(NU):
                    for b in range(2):
                        lo, mid, hi = 64 * b, 64 * b + BL, 64 * b + 64
                        last = mm(R[1][lo:mid, u * BL:(u + 1) * BL], q1s[mid:hi, u, :], minv[mid:hi, u, mid:hi],
                                  start=True, stop=True)
                last.then_inc(S["m12_done"], 1)
                wait_apart(pe, S["s_upd"], n * NU)
                for u in range(NU):
                    last = mm(R[2][BL:64, u * BL:(u + 1) * BL], minv[BL:64, u, BL:64], q1s[BL:64, u, :], start=True, stop=True)
                last.then_inc(S["t21_done"], 1)
                if a is not None:
                    project(a, 1)
                pe.wait_ge(S["t21_ready"], n + 1)
                wait_apart(pe, S["t64_diag"], n * 2 + 2)
                for u in range(NU):
                    last = mm(R[0][64:P, u * 64:(u + 1) * 64], lt[p][0:64, u, 64:P], t64[:, u, :], start=True, stop=True)
                last.then_inc(S["q2_done"], 1)
                pe.wait_ge(S["q2_ready"], n + 1)
                wait_apart(pe, S["m12_ready"], n * 2 + 2)
                for u in range(NU):
                    last = mm(R[1][0:64, u * 64:(u + 1) * 64], q2s[64:P, u, :], minv[64:P, u, 64:P], start=True, stop=True)
                last.then_inc(S["m2_done"], 1)
                for j in range(NC):
                    cs = slice(j * C, (j + 1) * C)
                    if j == 0:
                        pe.wait_ge(S["s_load"], n + 1)
                        pe.wait_ge(S["minv_ready"], n + 1)
                        pe.wait_ge(wc_in[p], c.m * 32 + 32)
                    else:
                        pe.wait_ge(S["s_upd"], n * NU + 2 * j)
                        pe.wait_ge(S["o_ready"], n * NC + j)
                    mm(R[0][:, 0:2 * P], kt[p][:, cs], sw[p][:, :], start=True, stop=True).then_inc(S["ks_done"], 1)
                    if j > 0:
                        pe.wait_ge(S["z_ready"], n * NC + j)
                    mm(R[1][:, 0:2 * P], qt[p][:, cs], sw[p][:, :], start=True, stop=True).then_inc(S["qs_done"], 1)
                    if a is not None:
                        if j < 2:
                            project(a, 2 + j)
                        else:
                            decay(a, j - 2)
                    pe.wait_ge(S["r_ready"], n * NU + 2 * j + 2)
                    pe.wait_ge(S["tq_ready"], n * NU + 2 * j + 2)
                    for h in range(2):
                        last = mm(R[1][:, (2 + h) * P:(3 + h) * P], minv[:, unit(h, j), :], rn[:, h, :], start=True, stop=True)
                    last.then_inc(S["w_done"], 1)
                    pe.wait_ge(S["u_ready"], n * NU + 2 * j + 2)
                    pe.wait_ge(S["k2_ready"], n * NU + NU)
                    for h in range(2):
                        last = mm(R[2][:, h * P:(h + 1) * P], k2[p][:, unit(h, j), :], us[:, h, :], start=True, stop=True)
                    last.then_inc(S["su_done"], 1)
                    pe.wait_ge(S["pt_ready"], n * 2 + 2)
                    for h in range(2):
                        last = mm(R[0][:, (2 + h) * P:(3 + h) * P], pt[p][:, unit(h, j), :], us[:, h, :], start=True, stop=True)
                    last.then_inc(S["pu_done"], 1)
                    for k in range(KD):
                        last = mm(R[1][:, 0:2 * P], ht[:, k, cs], wz[p][:, k, :], start=(k == 0), stop=(k == KD - 1))
                    last.then_inc(S["z_done"], 1)
                    if j > 0:
                        flush(c, j - 1)
                flush(c, NC - 1)

            def X(s, c, a):
                if c is None:
                    A(a)
                else:
                    recur(c, a)

            def to_channels(t, second):
                pe.wait_ge(S["hn_ready"], t * 8 + 4 * second + 4)
                for k in range(KD):
                    for c in range(NC):
                        last = pe.transpose(R[k][:, c * P:(c + 1) * P], hn[:, c, k * P:(k + 1) * P], ident[:, :])
                    last.then_inc(S["ht_psum"], 1)

            pe.sem_inc(S["y_done"], NC)

            def tile(t, b, m0):
                n_end = (m0 + KH // 2) * 2
                pe.wait_ge(S["dve_setup"], DVE_SETUP)
                pe.wait_ge(S["out_ready"], t * 2)
                pe.wait_ge(S["ff_ready"], t * NI)
                to_channels(t, 0)
                pe.wait_ge(S["x1_half"], t * 2)
                for y in Y:
                    last = mm(y[:, :], zero_b[:, 0:P], zero_b[:, :], start=True, stop=True)
                pe.wait_ge(S["ht_ready"], t * 4 + 2)
                for c in range(NC):
                    for k in range(KD):
                        last = mm(R[2][:, c * 2 * VH:(c + 1) * 2 * VH], ht[:, k, c * C:(c + 1) * C], w_ba[:, k, :],
                                  start=(k == 0), stop=(k == KD - 1))
                last.then_inc(S["ba_done"], 1)
                pe.wait_ge(S["g_ready"], t + 1)
                g_all = table[:, G_, :, :].rearrange("p c h -> p (c h)")
                for i, m in enumerate((mask_incl, mask_after, ones)):
                    last = mm(R[3][:, i * NC * VH:(i + 1) * NC * VH], m[:, :], g_all, start=True, stop=True)
                last.then_inc(S["cum_done"], 1)
                pe.wait_ge(S["thb_ready"], t + 1)
                pe.wait_ge(S["exp_ready"], t + 1)
                slots(pe, m0, A, B, X, lambda c: recur(c, None))
                pe.wait_ge(S["o_ready"], n_end * NC)
                pe.wait_ge(S["z_ready"], n_end * NC)
                to_channels(t, 1)
                pe.wait_ge(S["ht_ready"], t * 4 + 4)
                pe.wait_ge(S["vs_ready"], n_end * NU)
                pe.wait_ge(S["s_upd"], n_end * NU)
                pe.wait_ge(S["got_ready"], n_end * NC)
                for i in range(NI):
                    pair = (PB[0], PB[1]) if i % 2 == 0 else (R[2], R[3])
                    if i >= 2:
                        pe.wait_ge(S["ff_ready"], t * NI + i - 1)
                    for bank, o, done in ((pair[0], i, S["gate_done"]), (pair[1], NI + i, S["up_done"])):
                        for k in range(KD):
                            last = mm(bank[:, :], wgu_t[:, k, o * P:(o + 1) * P], ht[:, k, :], start=(k == 0), stop=(k == KD - 1))
                        last.then_inc(done, 1)
                pe.wait_ge(S["ff_ready"], t * NI + NI)
                for c in range(NC):
                    for i in range(NI):
                        last = mm(R[c // 2][:, c % 2 * D:(c % 2 + 1) * D], ff[:, i, c * C:(c + 1) * C], wd_t[:, i, :],
                                  start=(i == 0), stop=(i == NI - 1))
                    if c % 2:
                        last.then_inc(S["down_done"], 1)

            tile_loop(pe, tile)


_INS = ['L0_attn_hidden_states', 'L0_attn_W_qkv', 'L0_attn_W_z', 'L0_attn_W_b', 'L0_attn_W_a', 'L0_attn_conv_w',
        'L0_attn_conv_b', 'L0_attn_dt_bias', 'L0_attn_A_log', 'L0_attn_norm_gamma', 'L0_attn_W_out',
        'L0_ffn_w_gate_up', 'L0_ffn_w_down', 'L0_c', 'L0_wmod']
_OUTS = [((BATCH, SEQ, D), 'float32')]


def kernel(**inputs):
    import numpy as _np
    import concourse.bacc as _bacc
    from concourse import mybir as _mybir
    from concourse.bass_utils import run_bass_kernel_spmd as _run

    nc = _bacc.Bacc("TRN2", target_bir_lowering=False, num_devices=1)
    arrays, args = {}, []
    for name in _INS:
        a = _np.ascontiguousarray(inputs[name])
        arrays[f"in_{name}_dram"] = a
        args.append(nc.dram_tensor(f"in_{name}_dram", a.shape, _mybir.dt.from_np(a.dtype), kind="ExternalInput").ap())
    for i, (shape, dtype) in enumerate(_OUTS):
        dt = _mybir.dt.from_np(_np.dtype(dtype))
        args.append(nc.dram_tensor(f"out_{i}_dram", shape, dt, kind="ExternalOutput").ap())
    adaln_block(nc, *args)
    r = _run(nc, [arrays], core_ids=[0])
    return r.results[0]["out_0_dram"]
```

```python
from contextlib import ExitStack

import concourse.bass as bass
from concourse import mybir
from typing import Any, NamedTuple

F32 = mybir.dt.float32
BF16 = mybir.dt.bfloat16
ALU = mybir.AluOpType
ACT = mybir.ActivationFunctionType

P = 128
BATCH, SEQ, D = 4, 1024, 256
KH, VH = 16, 32
C = 128
NC = 4
TOK = C * NC
TILES_PER_BATCH = SEQ // TOK
KD = D // P
KEY_DIM = KH * P
CONV_K = 4
TAIL = CONV_K - 1
INTER = 1024
NI = INTER // P
NU = 2 * NC
BL = 32
NBL = C // BL
SB = 16
NSB = C // SB
SOLVE_OPS = 2 * (SB - 1)
EPS_NORM = 1e-6
EPS_LN = 1e-5
GATE_MIN = 0.25
BETA, G_, EXP_G, EXP_REST, EXP_ALL = range(5)
RQ, NK, NAA, EGQ = 0, NC, 2 * NC, 4 * NC
VEC = (0, 1, 3, 4)
SCALAR_OPS = 7
MLP_BATCHES = 12
POOL_SETUP = 15
DVE_SETUP = 4 + 3 + KD * BATCH + 4 + 3 + 4 * BATCH + 3 + MLP_BATCHES


class Item(NamedTuple):

    m: Any
    p: int
    k: Any

    @property
    def n(self):
        return 2 * self.m + self.p


def adaln_block(nc, x, w_qkv, w_z, w_b, w_a, conv_w, conv_b, dt_bias, a_log, gamma, w_out,
                w_gate_up, w_down, cond, w_mod, out):
    ctx = ExitStack()

    def sb(name, shape, dt=F32):
        return ctx.enter_context(nc.sbuf_tensor(name, shape, dt))

    def sem(name):
        return ctx.enter_context(nc.semaphore(name))

    with ctx:
        mask_incl = sb("mask_incl", [P, P])
        mask_strict = sb("mask_strict", [P, P])
        mask_after = sb("mask_after", [P, P])
        ident = sb("ident", [P, P])
        ones = sb("ones", [P, P])
        eye_blocks = sb("eye_blocks", [NU * NSB, SB * SB])
        ident_bl = sb("ident_bl", [P, BL])
        second_half = sb("second_half", [P, 1])
        minus_half = sb("minus_half", [P, 8])
        zero_b = sb("zero_b", [P, 512], BF16)
        conv_par = sb("conv_par", [P, KH, 4, 5])
        w_ba = sb("w_ba", [P, KD, 2 * VH])
        dt_b = sb("dt_b", [P, VH])
        neg_exp_a = sb("neg_exp_a", [P, VH])
        gamma_c = sb("gamma_c", [P, 1])
        cond_t = sb("cond_t", [P, KD, BATCH])
        cond_th = sb("cond_th", [P, KD, BATCH])
        cond_silu = sb("cond_silu", [P, KD, BATCH])
        mod_t = sb("mod_t", [P, 4, KD, BATCH])
        gate_rows = sb("gate_rows", [P, BATCH, 2, D])
        wgu_t = sb("wgu_t", [P, KD, 2 * INTER])
        wd_t = sb("wd_t", [P, NI, D])
        xt = sb("xt", [P, NC, D])
        ht = sb("ht", [P, KD, TOK])
        stats = sb("stats", [P, NC, 6])
        mean_var = sb("mean_var", [P, NC, 2])
        rstd = sb("rstd", [P, NC])
        mod_b = sb("mod_b", [P, 4, KD])
        gate_b = sb("gate_b", [P, 2, D])
        au = sb("au", [P, NC, VH])
        th_b = sb("th_b", [P, NC, VH])
        table = sb("table", [P, 5, NC, VH])
        states = sb("states", [P, KH, 2 * P])
        tails = sb("tails", [P, KH, 4, TAIL])
        wa = [sb(f"wa{p}", [P, KD, 4 * P]) for p in range(2)]
        wz = [sb(f"wz{p}", [P, KD, 2 * P]) for p in range(2)]
        wo = [sb(f"wo{p}", [P, 2, D]) for p in range(2)]
        qt = [sb(f"qt{p}", [P, TOK]) for p in range(2)]
        kt = [sb(f"kt{p}", [P, TOK]) for p in range(2)]
        lt = [sb(f"lt{p}", [P, NU, C]) for p in range(2)]
        pt = [sb(f"pt{p}", [P, NU, C]) for p in range(2)]
        vs = [sb(f"vs{p}", [P, NU, P]) for p in range(2)]
        k2 = [sb(f"k2{p}", [P, NU, P]) for p in range(2)]
        sc = [sb(f"sc{p}", [P, 5, NC, 2]) for p in range(2)]
        sca = [sb(f"sca{p}", [P, 6 * NC]) for p in range(2)]
        sw = [sb(f"sw{p}", [P, 2 * P]) for p in range(2)]
        cwp = sb("cwp", [P, 4, 5])
        g_item = sb("g_item", [P, NC, 2])
        gm = sb("gm", [P, NU, C])
        raw = sb("raw", [P, 4, TAIL + TOK])
        cv_th = sb("cv_th", [P, 8, TOK])
        cv, th, ff = cv_th[:, 0:4, :], cv_th[:, 4:8, :], cv_th
        vt = sb("vt", [P, 2, TOK])
        sq = sb("sq", [P, 2, TOK])
        ff_th, ff_g = vt, sq
        dec = sb("dec", [P, NU, C])
        kkm = sb("kkm", [P, NC, C])
        kqm = sb("kqm", [P, NC, C])
        ss = sb("ss", [P, 2 * NC])
        rs = sb("rs", [P, 2 * NC])
        rk2 = sb("rk2", [P, 3 * NC])
        ktok = sb("ktok", [P, NC, P])
        blocks = sb("blocks", [NU * NSB, SB * SB])
        tinv = sb("tinv", [NU * NSB, SB * SB])
        solve_tmp = sb("solve_tmp", [NU * NSB, SB * SB // 4 + SB])
        t16 = sb("t16", [P, NU, BL])
        t16_t = sb("t16_t", [P, NU, BL])
        q0s = sb("q0s", [P, NU, BL])
        t32 = sb("t32", [P, NU, BL])
        minv = sb("minv", [P, NU, C])
        t64 = sb("t64", [64, NU, 64])
        q1s = sb("q1s", [P, NU, BL])
        q2s = sb("q2s", [P, NU, 64])
        rn = sb("rn", [P, 2, P])
        tmpq = sb("tmpq", [P, 2, P])
        us = sb("us", [P, 2, P])
        thz = sb("thz", [P, 2, 2 * P])
        sg = sb("sg", [P, NC, 2 * P])
        ob = sb("ob", [P, 2, 2 * P])
        ssq = sb("ssq", [P, 2, 2])
        rr = sb("rr", [P, 2, 2])
        gt = sb("gt", [P, 2, P])
        got = sb("got", [P, 2, P])

        junk = q1s[:, 0:NC, :]
        hn = gm[:, :, :].rearrange("p (c a) i -> p c (a i)", c=NC)
        x1 = dec[:, :, :].rearrange("p (c a) i -> p c (a i)", c=NC)
        y_tmp = raw[:, :, 0:D]
        a_abs, a_exp, a_ln = (kqm[:, i, :].rearrange("p (c h) -> p c h", c=NC) for i in range(3))

        l_scr = nc.dram_tensor("l_scratch", [NU * NBL, BL * BL], F32, kind="Internal").ap()
        t_scr = nc.dram_tensor("t_scratch", [NU * NBL, BL * BL], F32, kind="Internal").ap()

        Y = [ctx.enter_context(nc.psum_tensor(f"y{i}", [P, 512], F32)) for i in range(2)]
        PB = [ctx.enter_context(nc.psum_tensor(f"pb{i}", [P, 512], F32)) for i in range(2)]
        R = [ctx.enter_context(nc.psum_tensor(f"r{i}", [P, 512], F32)) for i in range(4)]

        names = """pool_setup in_small in_cond in_wmod in_gu in_down in_conv act_setup pe_setup dve_setup
        x_in ln_stats ln_eps ln_rstd hn_ready ht_psum ht_ready ba_done au_ready thb_ready abs_ready aexp_ready
        aln_ready g_ready g_mul cum_done exp_ready beta_ready y_clear mod_copied
        x1_half x1_ready gate_done up_done th_ff ff_half ff_ready down_done down_half out_ready out_stored zeroed
        wa0 wa1 wc0 wc1
        a_in gm_ready proj_done raw_in conv_in conv_tap tail_saved d_done d_ready
        th_ready silu_done sq_ready kk_done kq_done kkm_ready kqm_ready norms_done ss_ready
        scal_step sc_ready kt_done ktok_ready k2_ready v_tr vs_ready lt_ready pt_ready
        lb_out lb_in tb_init solve_step tb_out t16_in scratch_zero
        t16t_ready q0_done q0_ready mdiag_done t32_ready
        mdiag t64_diag q1_done q1_ready m12_done t21_done m12_ready t21_ready q2_done q2_ready m2_done minv_ready
        s_load s_store ks_done qs_done r_ready tq_ready w_done u_ready su_done pu_done s_upd o_ready
        z_done z_ready sg_ready sq_acc rr_eps rr_ready gt_ready gtr_done got_ready y_done"""
        S = {n: sem(n) for n in names.split()}
        passed = {eng: sem(f"passed_{name}") for name, eng in
                  (("sp", nc.sync), ("pool", nc.gpsimd), ("dve", nc.vector), ("pe", nc.tensor))}
        wa_in, wc_in = [S["wa0"], S["wa1"]], [S["wc0"], S["wc1"]]

        def wait_apart(eng, sem, value):
            eng.wait_ge(sem, value)
            eng.sem_inc(passed[eng], 1)

        def tile_loop(eng, body, batch_start=None):
            with eng.Fori(0, BATCH) as b:
                if batch_start:
                    batch_start(b)
                with eng.Fori(0, TILES_PER_BATCH) as half:
                    t = b * TILES_PER_BATCH + half
                    body(t, b, b * (TILES_PER_BATCH * KH // 2) + half * (KH // 2))

        def slots(eng, m0, A, slot):
            last = m0 + (KH // 2 - 1)
            A(Item(m0, 0, 0))
            slot(Item(m0, 0, 0), None, Item(m0, 1, 1))
            with eng.Fori(0, KH // 2 - 1) as i:
                slot(Item(m0 + i, 1, 2 * i + 1), Item(m0 + i, 0, 2 * i), Item(m0 + i + 1, 0, 2 * i + 2))
                slot(Item(m0 + i + 1, 0, 2 * i + 2), Item(m0 + i, 1, 2 * i + 1), Item(m0 + i + 1, 1, 2 * i + 3))
            slot(Item(last, 1, KH - 1), Item(last, 0, KH - 2), None)
            slot(None, Item(last, 1, KH - 1), None)

        def unit(h, c):
            return h * NC + c

        block = ctx.enter_context(nc.Block())

        @block.sync
        def _(sp):
            with nc.allow_non_contiguous_dma(reason="small vectors, once"):
                sp.dma_start(cond_t[:, 0, :], cond[:, 0:P].rearrange("b p -> p b")).then_inc(S["in_cond"], 16)
                sp.dma_start(cond_t[:, 1, :], cond[:, P:2 * P].rearrange("b p -> p b")).then_inc(S["in_cond"], 16)
                sp.dma_start(gamma_c[:, :], gamma.rearrange("(p a) -> p a", a=1)).then_inc(S["in_small"], 16)
            sp.dma_start(dt_b[:, :], dt_bias.rearrange("(a h) -> a h", a=1).to_broadcast([P, VH])).then_inc(S["in_small"], 16)
            sp.dma_start(neg_exp_a[:, :], a_log.rearrange("(a h) -> a h", a=1).to_broadcast([P, VH])).then_inc(S["in_small"], 16)
            sp.dma_start(w_ba[:, :, 0:VH], w_b.rearrange("(k p) h -> p k h", p=P)).then_inc(S["in_small"], 16)
            sp.dma_start(w_ba[:, :, VH:2 * VH], w_a.rearrange("(k p) h -> p k h", p=P)).then_inc(S["in_small"], 16)
            sp.dma_start(x1[0:64, 0:2, :].rearrange("t a b -> t (a b)"),
                         conv_w.rearrange("(t c) k -> t (c k)", c=P)).then_inc(S["in_conv"], 16)
            sp.dma_start(x1[0:64, 2, 0:P], conv_b.rearrange("(t c) -> t c", c=P)).then_inc(S["in_conv"], 16)
            sp.dma_start(ff[:, :, :].rearrange("p a b -> p (a b)")[:, 0:KD * 6 * D].rearrange("p (k n) -> p k n", k=KD),
                         w_mod.rearrange("(k p) n -> p k n", p=P)).then_inc(S["in_wmod"], 16)
            for k in range(KD):
                sp.dma_start(raw[:, 2 * k:2 * k + 2, 0:TOK],
                             w_down[k * P:(k + 1) * P, :].rearrange("p (a b) -> p a b", b=TOK)).then_inc(S["in_down"], 16)
            sp.wait_ge(S["pe_setup"], 2)
            sp.dma_start(ff[:, :, :].rearrange("p a (b n) -> p (a b) n", n=D),
                         w_gate_up.rearrange("(o p) n -> p o n", p=P)).then_inc(S["in_gu"], 16)

            sp.wait_ge(S["pool_setup"], POOL_SETUP)
            sp.dma_start(t_scr, minv[0:NU * NBL, :, :].rearrange("p u i -> p (u i)")).then_inc(S["scratch_zero"], 16)
            sp.wait_ge(S["scratch_zero"], 16)

            def load_wa(p, k):
                w = w_qkv.rearrange("(k p) n -> p k n", p=P)
                sp.dma_start(wa[p][:, :, 0:P], w[:, :, bass.ds(k * P, P)]).then_inc(wa_in[p], 16)
                sp.dma_start(wa[p][:, :, P:2 * P], w[:, :, bass.ds(k * P + KEY_DIM, P)]).then_inc(wa_in[p], 16)
                sp.dma_start(wa[p][:, :, 2 * P:4 * P], w[:, :, bass.ds(k * (2 * P) + 2 * KEY_DIM, 2 * P)]).then_inc(wa_in[p], 16)

            def A(a):
                wait_apart(sp, S["proj_done"], a.n * 4)
                load_wa(0, 0)
                load_wa(1, 1)

            def slot(s, c, a):
                if s is None:
                    return
                n = s.n
                if not (isinstance(s.k, int)):
                    wait_apart(sp, S["proj_done"], n * 4)
                    load_wa(1 - s.p, s.k + 1)
                wait_apart(sp, S["y_done"], n * NC)
                sp.dma_start(wz[s.p][:, :, :], w_z.rearrange("(k p) n -> p k n", p=P)[:, :, bass.ds(s.k * (2 * P), 2 * P)]
                             ).then_inc(wc_in[s.p], 16)
                sp.dma_start(wo[s.p][:, :, :], w_out.rearrange("(h p) n -> p h n", p=P)[:, bass.ds(s.k * 2, 2), :]
                             ).then_inc(wc_in[s.p], 16)
                wait_apart(sp, S["lt_ready"], n * NU + NU)
                wait_apart(sp, S["lb_in"], n * 32)
                for b in range(NBL):
                    sp.dma_start(l_scr.rearrange("(u b) (j i) -> b j u i", b=NBL, i=BL)[b],
                                 lt[s.p][b * BL:(b + 1) * BL, :, b * BL:(b + 1) * BL]).then_inc(S["lb_out"], 16)
                wait_apart(sp, S["lb_out"], n * (16 * NBL) + 16 * NBL)
                wait_apart(sp, S["solve_step"], n * SOLVE_OPS)
                for half in range(2):
                    ps, hs = slice(half * NU * NBL, (half + 1) * NU * NBL), slice(half * SB, (half + 1) * SB)
                    sp.dma_start(blocks[ps, :].rearrange("u (j i) -> u j i", i=SB),
                                 l_scr.rearrange("u (j i) -> u j i", i=BL)[:, hs, hs]).then_inc(S["lb_in"], 16)
                wait_apart(sp, S["solve_step"], n * SOLVE_OPS + SOLVE_OPS)
                wait_apart(sp, S["t16_in"], n * 16)
                for half in range(2):
                    ps, hs = slice(half * NU * NBL, (half + 1) * NU * NBL), slice(half * SB, (half + 1) * SB)
                    sp.dma_start(t_scr.rearrange("u (i c) -> u i c", c=BL)[:, hs, hs],
                                 tinv[ps, :].rearrange("u (i c) -> u i c", c=SB)).then_inc(S["tb_out"], 16)
                wait_apart(sp, S["tb_out"], n * 32 + 32)
                wait_apart(sp, S["t16t_ready"], n)
                wait_apart(sp, S["q0_done"], n)
                sp.dma_start(t16[:, :, :], t_scr.rearrange("(u b) (i c) -> (b i) u c", b=NBL, c=BL)).then_inc(S["t16_in"], 16)

            def tile(t, b, m0):
                wait_apart(sp, S["x1_ready"], t * 2)
                by_tile = x.rearrange("b (t c p) d -> (b t) p c d", c=NC, p=P)
                sp.dma_start(xt[:, :, :], by_tile[bass.ds(t, 1), :, :, :].rearrange("a p c d -> p (a c) d")
                             ).then_inc(S["x_in"], 16)
                slots(sp, m0, A, slot)
                wait_apart(sp, S["out_ready"], t * 2 + 2)
                by_tile = out.rearrange("b (t c p) d -> (b t) p c d", c=NC, p=P)
                sp.dma_start(by_tile[bass.ds(t, 1), :, :, :].rearrange("a p c d -> p (a c) d"), y_tmp[:, :, :]
                             ).then_inc(S["out_stored"], 16)

            tile_loop(sp, tile)
            sp.wait_ge(S["out_stored"], 16 * BATCH * TILES_PER_BATCH)

        @block.gpsimd
        def _(pool):
            step = [0]

            def setup(ins, wait=True):
                step[0] += 1
                ins.then_inc(S["pool_setup"], 1)
                if wait:
                    pool.wait_ge(S["pool_setup"], step[0])

            setup(pool.memset(ones[:, :], 1.0), False)
            setup(pool.memset(minus_half[:, :], -0.5), False)
            setup(pool.memset(zero_b[:, :], 0.0), False)
            setup(pool.memset(minv[:, :, :], 0.0), False)
            setup(pool.memset(t64[:, :, :], 0.0), False)
            for m, value in ((mask_incl, 1.0), (mask_strict, 1.0), (mask_after, 1.0), (ident, 0.0)):
                setup(pool.memset(m[:, :], value), False)
            setup(pool.memset(eye_blocks[:, :], 0.0))
            setup(pool.affine_select(out=mask_incl[:, :], in_=mask_incl[:, :], compare_op=ALU.is_ge, fill=0.0,
                                     base=0, pattern=[[1, P]], channel_multiplier=-1), False)
            setup(pool.affine_select(out=mask_strict[:, :], in_=mask_strict[:, :], compare_op=ALU.is_gt, fill=0.0,
                                     base=0, pattern=[[1, P]], channel_multiplier=-1), False)
            setup(pool.affine_select(out=mask_after[:, :], in_=mask_after[:, :], compare_op=ALU.is_gt, fill=0.0,
                                     base=0, pattern=[[-1, P]], channel_multiplier=1), False)
            setup(pool.affine_select(out=ident[:, :], in_=ident[:, :], compare_op=ALU.not_equal, fill=1.0,
                                     base=0, pattern=[[-1, P]], channel_multiplier=1), False)
            setup(pool.affine_select(out=eye_blocks[:, :], in_=eye_blocks[:, :], compare_op=ALU.not_equal, fill=1.0,
                                     base=0, pattern=[[1, SB], [-1, SB]], channel_multiplier=0))

            def deviations(count):
                pool.tensor_scalar(rstd[:, :], mean_var[:, :, 1], 1.0, EPS_LN, ALU.mult, ALU.add).then_inc(S["ln_eps"], 1)
                pool.wait_ge(S["ln_eps"], count)
                pool.tensor_tensor(rstd[:, :], rstd[:, :], minus_half[:, 0:NC], ALU.pow).then_inc(S["ln_rstd"], 1)

            def head(a):
                n = a.n
                wait_apart(pool, S["conv_tap"], n * 12)
                pool.tensor_copy(cwp[:, :, :], conv_par[:, bass.ds(a.k, 1), :, :].rearrange("p a t w -> p (a t) w")
                                 ).then_inc(S["a_in"], 1)
                wait_apart(pool, S["gm_ready"], n * NU)
                pool.tensor_copy(g_item[:, :, :], table[:, G_, :, bass.ds(2 * a.k, 2)]).then_inc(S["a_in"], 1)
                pool.tensor_copy(raw[:, :, 0:TAIL], tails[:, bass.ds(a.k, 1), :, :].rearrange("p a t w -> p (a t) w")
                                 ).then_inc(S["a_in"], 1)

            def masked_g(a):
                n = a.n
                wait_apart(pool, S["a_in"], n * 3 + 3)
                wait_apart(pool, S["d_done"], n * 2)
                for h in range(2):
                    for c in range(NC):
                        pool.tensor_scalar(gm[:, unit(h, c), :], mask_incl[:, :], g_item[:, c, h:h + 1], 1.0,
                                           ALU.mult, ALU.mult).then_inc(S["gm_ready"], 1)

            def save_tail(a):
                wait_apart(pool, S["raw_in"], a.n * 4 + 4)
                pool.tensor_copy(tails[:, bass.ds(a.k, 1), :, :].rearrange("p a t w -> p (a t) w"),
                                 raw[:, :, TOK:TOK + TAIL]).then_inc(S["tail_saved"], 1)

            def A(a):
                head(a)
                masked_g(a)
                save_tail(a)

            def B(s):
                n, p = s.n, s.p
                wait_apart(pool, S["norms_done"], n)
                for i, src in enumerate((qt[p], kt[p])):
                    pool.wait_ge(S["silu_done"], n * 4 + i + 1)
                    pool.tensor_tensor(sq[:, i, :], src[:, :], src[:, :], ALU.mult).then_inc(S["sq_ready"], 1)
                wait_apart(pool, S["y_done"], n * NC)
                base = n * SCALAR_OPS
                pool.tensor_copy(sc[p][:, :, :, :], table[:, :, :, bass.ds(2 * s.k, 2)]).then_inc(S["scal_step"], 1)
                wait_apart(pool, S["ss_ready"], n + 1)
                rk = rs[:, NC:2 * NC]
                pool.tensor_tensor(rs[:, :], ss[:, :], minus_half[:, :], ALU.pow).then_inc(S["scal_step"], 1)
                wait_apart(pool, S["scal_step"], base + 2)
                pool.tensor_scalar(sca[p][:, RQ:RQ + NC], rs[:, 0:NC], float(P) ** -0.5, 1.0, ALU.mult, ALU.mult
                                   ).then_inc(S["scal_step"], 1)
                pool.tensor_tensor(rk2[:, 0:NC], ss[:, NC:2 * NC], rk, ALU.mult).then_inc(S["scal_step"], 1)
                pool.tensor_scalar(rk2[:, NC:2 * NC], rk, -1.0, 1.0, ALU.mult, ALU.mult).then_inc(S["scal_step"], 1)
                wait_apart(pool, S["scal_step"], base + 5)
                pool.tensor_scalar(sca[p][:, NK:NK + NC], rk2[:, 0:NC], 0.5, 1.0, ALU.mult, ALU.mult
                                   ).then_inc(S["scal_step"], 1)
                pool.tensor_tensor(rk2[:, 2 * NC:3 * NC], rk2[:, NC:2 * NC], rk, ALU.mult).then_inc(S["scal_step"], 1)
                wait_apart(pool, S["scal_step"], base + 7)
                for h in range(2):
                    pool.tensor_tensor(sca[p][:, NAA + h * NC:NAA + (h + 1) * NC], rk2[:, 2 * NC:3 * NC],
                                       sc[p][:, BETA, :, h], ALU.mult).then_inc(S["sc_ready"], 1)
                    pool.tensor_tensor(sca[p][:, EGQ + h * NC:EGQ + (h + 1) * NC], sca[p][:, RQ:RQ + NC],
                                       sc[p][:, EXP_G, :, h], ALU.mult).then_inc(S["sc_ready"], 1)
                wait_apart(pool, S["ktok_ready"], n + 1)
                for h in range(2):
                    for c in range(NC):
                        pool.tensor_scalar(k2[p][:, unit(h, c), :], ktok[:, c, :], sc[p][:, EXP_REST, c, h:h + 1], 1.0,
                                           ALU.mult, ALU.mult).then_inc(S["k2_ready"], 1)

            def load_state(c):
                wait_apart(pool, S["s_store"], c.n)
                pool.tensor_copy(sw[c.p][:, :], states[:, bass.ds(c.k, 1), :].rearrange("p a n -> p (a n)")
                                 ).then_inc(S["s_load"], 1)

            def store_state(c):
                wait_apart(pool, S["s_upd"], c.n * NU + NU)
                pool.tensor_copy(states[:, bass.ds(c.k, 1), :].rearrange("p a n -> p (a n)"), sw[c.p][:, :]
                                 ).then_inc(S["s_store"], 1)

            def gates(c, i):
                n = c.n
                wait_apart(pool, S["z_ready"], n * 2 + i + 1)
                wait_apart(pool, S["gt_ready"], n * NU)
                pool.tensor_scalar(sg[:, 2 * i:2 * i + 2, :], thz[:, :, :], 0.5, 0.5, ALU.mult, ALU.add
                                   ).then_inc(S["sg_ready"], 1)

            def step(c, j):
                n = c.n
                wait_apart(pool, S["sq_acc"], n * NU + 2 * j + 2)
                pool.tensor_scalar(ssq[:, j % 2, :], ssq[:, j % 2, :], 1.0 / P, EPS_NORM, ALU.mult, ALU.add
                                   ).then_inc(S["rr_eps"], 1)
                pool.wait_ge(S["rr_eps"], n * NC + j + 1)
                pool.tensor_tensor(rr[:, j % 2, :], ssq[:, j % 2, :], minus_half[:, 0:2], ALU.pow
                                   ).then_inc(S["rr_ready"], 1)

            def slot(s, c, a):
                if c is not None:
                    load_state(c)
                if s is not None:
                    B(s)
                if a is not None:
                    head(a)
                if s is not None:
                    wait_apart(pool, S["tb_out"], s.n * 32)
                    pool.tensor_copy(tinv[:, :], eye_blocks[:, :]).then_inc(S["tb_init"], 1)
                if a is not None:
                    masked_g(a)
                if c is not None:
                    gates(c, 1)
                    for j in range(NC):
                        step(c, j)
                if a is not None:
                    save_tail(a)
                if c is not None:
                    store_state(c)
                if s is not None:
                    gates(s, 0)

            def batch_start(b):
                wait_apart(pool, S["s_store"], b * (TILES_PER_BATCH * KH))
                pool.memset(states[:, :, :], 0.0).then_inc(S["zeroed"], 1)
                pool.memset(tails[:, :, :, :], 0.0).then_inc(S["zeroed"], 1)
                wait_apart(pool, S["zeroed"], b * 2 + 2)

            def tile(t, b, m0):
                pool.wait_ge(S["dve_setup"], DVE_SETUP)
                pool.wait_ge(S["ht_ready"], t * 4)
                wait_apart(pool, S["out_ready"], t * 2)
                pool.tensor_copy(mod_b[:, :, :], mod_t[:, :, :, bass.ds(b, 1)].rearrange("p v k a -> p v (k a)")
                                 ).then_inc(S["mod_copied"], 1)
                pool.tensor_copy(gate_b[:, :, :], gate_rows[:, bass.ds(b, 1), :, :].rearrange("p a g d -> p (a g) d")
                                 ).then_inc(S["mod_copied"], 1)
                wait_apart(pool, S["ln_stats"], t * 16 + 8)
                deviations(t * 2 + 1)
                wait_apart(pool, S["thb_ready"], t + 1)
                pool.tensor_scalar(table[:, BETA, :, :], th_b[:, :, :], 0.5, 0.5, ALU.mult, ALU.add).then_inc(S["beta_ready"], 1)
                pool.wait_ge(S["beta_ready"], t + 1)
                pool.wait_ge(S["g_ready"], t + 1)
                pool.wait_ge(S["exp_ready"], t + 1)
                wait_apart(pool, S["out_stored"], t * 16)
                slots(pool, m0, A, slot)
                wait_apart(pool, S["ln_stats"], t * 16 + 16)
                deviations(t * 2 + 2)

            tile_loop(pool, tile, batch_start)

        @block.scalar
        def _(act):
            act.wait_ge(S["in_cond"], 32)
            act.activation(cond_th[:, :, :], cond_t[:, :, :], ACT.Tanh, scale=0.5).then_inc(S["act_setup"], 1)
            act.wait_ge(S["in_small"], 16 * 5)
            act.activation(neg_exp_a[:, :], neg_exp_a[:, :], ACT.Exp).then_inc(S["act_setup"], 1)

            def evacuate(a, i):
                n = a.n
                act.wait_ge(S["proj_done"], n * 4 + i + 1)
                if i == 0:
                    act.wait_ge(S["a_in"], n * 3 + 3)
                    act.wait_ge(S["silu_done"], n * 4)
                    act.wait_ge(S["tail_saved"], n)
                act.activation(raw[:, i, TAIL:TAIL + TOK], PB[i % 2][:, :], ACT.Copy).then_inc(S["raw_in"], 1)
                act.activation(cv[:, i, :], PB[i % 2][:, :], ACT.Identity, bias=cwp[:, i, 4:5], scale=cwp[:, i, 0:1]
                               ).then_inc(S["conv_in"], 1)

            def decay(a, h):
                act.wait_ge(S["d_done"], a.n * 2 + h + 1)
                act.wait_ge(S["pt_ready"], a.n * 2)
                act.activation(dec[:, h * NC:(h + 1) * NC, :], PB[h][:, :].rearrange("p (c i) -> p c i", c=NC), ACT.Exp
                               ).then_inc(S["d_ready"], 1)

            def tanh(a, i):
                act.wait_ge(S["conv_tap"], a.n * 12 + 3 * i + 3)
                act.wait_ge(S["silu_done"], a.n * 4)
                act.activation(th[:, i, :], cv[:, i, :], ACT.Tanh, scale=0.5).then_inc(S["th_ready"], 1)

            def A(a):
                for i in range(4):
                    evacuate(a, i)
                for h in range(2):
                    decay(a, h)
                for i in range(3):
                    tanh(a, i)

            def k_rows(s):
                n = s.n
                act.wait_ge(S["kt_done"], n + 1)
                act.wait_ge(S["k2_ready"], n * NU)
                act.activation(ktok[:, :, :], PB[1][:, :].rearrange("p (c i) -> p c i", c=NC), ACT.Copy
                               ).then_inc(S["ktok_ready"], 1)

            def v_rows(s, h):
                n, p = s.n, s.p
                act.wait_ge(S["y_done"], n * NC)
                act.wait_ge(S["sc_ready"], n * 4 + 4)
                act.wait_ge(S["v_tr"], n * 2 + h + 1)
                for c in range(NC):
                    act.activation(vs[p][:, unit(h, c), :], PB[h][:, c * P:(c + 1) * P], ACT.Copy,
                                   scale=sca[p][:, NK + c:NK + c + 1]).then_inc(S["vs_ready"], 1)

            def flush(c, j):
                n = c.n
                act.wait_ge(S["gtr_done"], n * NC + j + 1)
                act.wait_ge(S["y_done"], n * NC + j + NC)
                act.activation(got[:, :, :], R[3][:, 0:2 * P].rearrange("p (h i) -> p h i", h=2), ACT.Copy,
                               scale=gamma_c[:, 0:1]).then_inc(S["got_ready"], 1)

            def gates(c, i):
                n = c.n
                act.wait_ge(S["z_done"], n * 2 + i + 1)
                act.wait_ge(S["sg_ready"], n * 2 + i)
                act.activation(thz[:, :, :], R[2 + i][:, :].rearrange("p (j i) -> p j i", j=2), ACT.Tanh, scale=0.5
                               ).then_inc(S["z_ready"], 1)

            def slot(s, c, a):
                if c is not None:
                    n, p = c.n, c.p
                    act.wait_ge(S["t32_ready"], n + 1)
                    act.wait_ge(S["q2_done"], n)
                    for b in range(2):
                        act.activation(t64[b * BL:(b + 1) * BL, :, b * BL:(b + 1) * BL], t32[b * BL:(b + 1) * BL, :, :],
                                       ACT.Copy).then_inc(S["t64_diag"], 1)
                    act.wait_ge(S["q1_done"], n + 1)
                    act.activation(q1s[:, :, :], R[0][:, 0:NU * BL].rearrange("p (u i) -> p u i", u=NU), ACT.Copy
                                   ).then_inc(S["q1_ready"], 1)
                if s is not None:
                    k_rows(s)
                    tanh(s, 3)
                if c is not None:
                    act.wait_ge(S["m12_done"], n + 1)
                    act.wait_ge(S["mdiag"], n * NBL + NBL)
                    for b in range(2):
                        lo, mid = 64 * b, 64 * b + BL
                        act.activation(minv[lo:mid, :, mid:mid + BL],
                                       R[1][lo:mid, 0:NU * BL].rearrange("p (u i) -> p u i", u=NU), ACT.Copy
                                       ).then_inc(S["m12_ready"], 1)
                if s is not None:
                    v_rows(s, 0)
                if c is not None:
                    gates(c, 1)
                    act.wait_ge(S["m2_done"], n + 1)
                    act.activation(minv[0:64, :, 64:P], R[1][0:64, :].rearrange("p (u i) -> p u i", u=NU), ACT.Copy
                                   ).then_inc(S["minv_ready"], 1)
                if s is not None:
                    v_rows(s, 1)
                for j in range(NC):
                    if c is not None:
                        act.wait_ge(S["qs_done"], n * NC + j + 1 + NC)
                        act.wait_ge(S["o_ready"], n * NC + j)
                        for h in range(2):
                            e = EGQ + h * NC + j
                            act.activation(tmpq[:, h, :], R[1][:, h * P:(h + 1) * P], ACT.Copy, scale=sca[p][:, e:e + 1]
                                           ).then_inc(S["tq_ready"], 1)
                    if a is not None and j == 2:
                        tanh(a, 0)
                    if c is not None:
                        act.wait_ge(S["w_done"], n * NC + j + 1)
                        act.wait_ge(S["pu_done"], n * NC + j)
                        for h in range(2):
                            e = NAA + h * NC + j
                            act.activation(us[:, h, :], R[2][:, (2 + h) * P:(3 + h) * P], ACT.Copy, scale=sca[p][:, e:e + 1]
                                           ).then_inc(S["u_ready"], 1)
                        if j > 1:
                            flush(c, j - 2)
                        act.wait_ge(S["o_ready"], n * NC + j + 1)
                        for h in range(2):
                            act.activation(junk, ob[:, j % 2, h * P:(h + 1) * P].rearrange("p (a b) -> p a b", a=NC),
                                           ACT.Square, accum_out=ssq[:, j % 2, h:h + 1]).then_inc(S["sq_acc"], 1)
                            act.wait_ge(S["sq_acc"], n * NU + 2 * j + h + 1)
                    if a is not None:
                        evacuate(a, j)
                if c is not None:
                    flush(c, NC - 2)
                if a is not None:
                    for h in range(2):
                        decay(a, h)
                    tanh(a, 1)
                if c is not None:
                    flush(c, NC - 1)
                if s is not None:
                    gates(s, 0)
                if a is not None:
                    tanh(a, 2)

            def modulate(count, mods, v):
                act.wait_ge(S["mod_copied"], mods)
                for k in range(KD):
                    act.wait_ge(S["ht_psum"], count + k + 1)
                    act.activation(ht[:, k, :], R[k][:, :], ACT.Identity, bias=mod_b[:, v, k:k + 1],
                                   scale=mod_b[:, v + 1, k:k + 1]).then_inc(S["ht_ready"], 1)

            def tile(t, b, m0):
                modulate(t * 4, t * 2 + 2, 0)
                act.wait_ge(S["au_ready"], t + 1)
                act.activation(th_b[:, :, :], R[2][:, 0:NC * 2 * VH].rearrange("p (c h) -> p c h", c=NC)[:, :, 0:VH], ACT.Tanh,
                               scale=0.5).then_inc(S["thb_ready"], 1)
                act.activation(a_abs[:, :, :], au[:, :, :], ACT.Abs).then_inc(S["abs_ready"], 1)
                act.wait_ge(S["abs_ready"], t + 1)
                act.activation(a_exp[:, :, :], a_abs[:, :, :], ACT.Exp, scale=-1.0).then_inc(S["aexp_ready"], 1)
                act.wait_ge(S["aexp_ready"], t + 1)
                act.activation(a_ln[:, :, :], a_exp[:, :, :], ACT.Ln, bias=ones[:, 0:1]).then_inc(S["aln_ready"], 1)
                act.wait_ge(S["cum_done"], t + 1)
                act.activation(table[:, EXP_G:EXP_ALL + 1, :, :].rearrange("p e c h -> p (e c h)"), R[3][:, 0:3 * NC * VH],
                               ACT.Exp).then_inc(S["exp_ready"], 1)
                act.wait_ge(S["out_stored"], t * 16)
                slots(act, m0, A, slot)
                modulate(t * 4 + 2, t * 2 + 2, 2)
                for i in range(NI):
                    bank = PB[0] if i % 2 == 0 else R[2]
                    act.wait_ge(S["gate_done"], t * NI + i + 1)
                    if i >= 2:
                        act.wait_ge(S["ff_half"], t * NI + i - 1)
                    else:
                        act.wait_ge(S["ff_half"], t * NI)
                    act.activation(ff_th[:, i % 2, :], bank[:, :], ACT.Tanh, scale=0.5).then_inc(S["th_ff"], 1)

            tile_loop(act, tile)

        @block.vector
        def _(dve):
            step = [0]

            def setup(ins, wait=False):
                step[0] += 1
                ins.then_inc(S["dve_setup"], 1)
                if wait:
                    dve.wait_ge(S["dve_setup"], step[0])

            for r in R:
                setup(dve.memset(r[:, :], 0.0))
            dve.wait_ge(S["act_setup"], 2)
            setup(dve.tensor_scalar(neg_exp_a[:, :], neg_exp_a[:, :], -1.0, None, ALU.mult))
            setup(dve.scalar_tensor_tensor(out=cond_silu[:, :, :], in0=cond_th[:, :, :], scalar=1.0, in1=cond_t[:, :, :],
                                           op0=ALU.add, op1=ALU.mult), True)
            setup(dve.tensor_scalar(cond_silu[:, :, :], cond_silu[:, :, :], 0.5, None, ALU.mult), True)
            dve.wait_ge(S["pool_setup"], POOL_SETUP)
            cond_rows = hn[:, :, :].rearrange("p a (b i) -> p (a b) i", i=P)
            for k in range(KD):
                for b in range(BATCH):
                    setup(dve.tensor_scalar(cond_rows[:, k * BATCH + b, :], ones[:, :], cond_silu[:, k, b:b + 1], None,
                                            ALU.mult))
            dve.wait_ge(S["pe_setup"], 1)
            cols = R[0][:, 0:5 * 64].rearrange("p (w t) -> p w t", w=5)
            for i in range(2):
                setup(dve.tensor_copy(conv_par[:, :, i, :].rearrange("p k w -> p w k"), cols[:, :, i * KH:(i + 1) * KH]))
            for j in range(2):
                v = cols[:, :, 2 * KH:4 * KH].rearrange("p w (k j) -> p w k j", j=2)
                setup(dve.tensor_copy(conv_par[:, :, 2 + j, :].rearrange("p k w -> p w k"), v[:, :, :, j]))
            dve.wait_ge(S["pe_setup"], 2)
            setup(dve.tensor_copy(mod_t[:, :, :, :].rearrange("p v k b -> p (v k b)"), R[1][:, 0:4 * KD * BATCH]), True)
            for v in (1, 3):
                setup(dve.tensor_scalar(mod_t[:, v, :, :], mod_t[:, v, :, :], 1.0, None, ALU.add))
            for b, bank in enumerate((R[2], R[3], PB[0], PB[1])):
                row = bank[:, :].rearrange("p (g d) -> p g d", g=2)
                sign = vt[:, 0, :].rearrange("p (g d) -> p g d", g=2)
                setup(dve.tensor_scalar(sign, row, 0.0, 2.0, ALU.is_ge, ALU.mult), True)
                setup(dve.tensor_scalar(sign, sign, -1.0, None, ALU.add), True)
                setup(dve.tensor_tensor(gate_rows[:, b, :, :], row, sign, ALU.mult), True)
                setup(dve.scalar_tensor_tensor(out=gate_rows[:, b, :, :], in0=gate_rows[:, b, :, :], scalar=GATE_MIN,
                                               in1=sign, op0=ALU.max, op1=ALU.mult), True)
            setup(dve.tensor_reduce(out=ident_bl[:, :], in_=ident[:, :].rearrange("p (b c) -> p c b", c=BL), op=ALU.add,
                                    axis=mybir.AxisListType.X), True)
            setup(dve.tensor_copy(q0s[:, :, :], ident_bl[:, :].unsqueeze(1).to_broadcast([P, NU, BL])))
            setup(dve.tensor_reduce(out=second_half[:, :], in_=ident_bl[:, SB:BL], op=ALU.add, axis=mybir.AxisListType.X))
            for n in range(MLP_BATCHES):
                dve.wait_ge(S["pe_setup"], 3 + n)
                if n < 8:
                    k, o = n // 4, n % 4
                    dst = wgu_t[:, k, o * 512:(o + 1) * 512]
                else:
                    dst = wd_t[:, 2 * (n - 8):2 * (n - 8) + 2, :].rearrange("p i d -> p (i d)")
                setup(dve.tensor_copy(dst, R[n % 4][:, :]))
            assert step[0] == DVE_SETUP

            def taps(a, i):
                n = a.n
                dve.wait_ge(S["raw_in"], n * 4 + i + 1)
                dve.wait_ge(S["conv_in"], n * 4 + i + 1)
                for j in range(1, CONV_K):
                    dve.scalar_tensor_tensor(out=cv[:, i, :], in0=raw[:, i, TAIL - j:TAIL - j + TOK],
                                             scalar=cwp[:, i, j:j + 1], in1=cv[:, i, :], op0=ALU.mult, op1=ALU.add
                                             ).then_inc(S["conv_tap"], 1)
                    if j < CONV_K - 1:
                        dve.wait_ge(S["conv_tap"], n * 12 + 3 * i + j)

            def A(a):
                for i in range(3):
                    taps(a, i)

            def silu(s, i):
                n, p = s.n, s.p
                if i < 2:
                    dve.wait_ge(S["qs_done"], n * NC)
                else:
                    dve.wait_ge(S["v_tr"], n * 2)
                dst = (qt[p][:, :], kt[p][:, :], vt[:, 0, :], vt[:, 1, :])[i]
                dve.wait_ge(S["th_ready"], n * 4 + i + 1)
                dve.scalar_tensor_tensor(out=dst, in0=th[:, i, :], scalar=1.0, in1=cv[:, i, :],
                                         op0=ALU.add, op1=ALU.mult).then_inc(S["silu_done"], 1)

            def grams(s):
                n, p = s.n, s.p
                dve.wait_ge(S["kk_done"], n + 1)
                dve.tensor_tensor(kkm[:, :, :], PB[0][:, :].rearrange("p (c i) -> p c i", c=NC),
                                  mask_strict[:, :].unsqueeze(1).to_broadcast([P, NC, C]), ALU.mult).then_inc(S["kkm_ready"], 1)
                dve.wait_ge(S["kq_done"], n + 1)
                dve.tensor_tensor(kqm[:, :, :], PB[1][:, :].rearrange("p (c i) -> p c i", c=NC),
                                  mask_incl[:, :].unsqueeze(1).to_broadcast([P, NC, C]), ALU.mult).then_inc(S["kqm_ready"], 1)

            def norms(s):
                dve.wait_ge(S["norms_done"], s.n + 1)
                dve.tensor_scalar(ss[:, :], PB[0][:, 0:2 * NC], 4 * EPS_NORM, None, ALU.add).then_inc(S["ss_ready"], 1)

            def systems(s, h):
                n, p = s.n, s.p
                if h == 0:
                    dve.wait_ge(S["y_done"], n * NC)
                    dve.wait_ge(S["d_ready"], n * 2 + 2)
                    dve.wait_ge(S["sc_ready"], n * 4 + 4)
                    dve.wait_ge(S["kkm_ready"], n + 1)
                for c in range(NC):
                    u, e = unit(h, c), NAA + h * NC + c
                    dve.scalar_tensor_tensor(out=lt[p][:, u, :], in0=kkm[:, c, :], scalar=sca[p][:, e:e + 1],
                                             in1=dec[:, u, :], op0=ALU.mult, op1=ALU.mult).then_inc(S["lt_ready"], 1)

            def products(s):
                n, p = s.n, s.p
                dve.wait_ge(S["kqm_ready"], n + 1)
                for h in range(2):
                    us_ = slice(h * NC, (h + 1) * NC)
                    dve.tensor_tensor(pt[p][:, us_, :], kqm[:, :, :], dec[:, us_, :], ALU.mult).then_inc(S["pt_ready"], 1)

            def solve(s, j0, j1):
                base = s.n * SOLVE_OPS
                if j0 == 0:
                    dve.wait_ge(S["lb_in"], s.n * 32 + 32)
                    dve.wait_ge(S["tb_init"], s.n + 1)
                for j in range(j0, j1):
                    rows, cols = SB - 1 - j, j + 1
                    if j > 0:
                        dve.wait_ge(S["solve_step"], base + 2 * j)
                    coef = blocks[:, j * SB + j + 1:(j + 1) * SB].unsqueeze(2).to_broadcast([NU * NSB, rows, cols])
                    row = tinv[:, j * SB:j * SB + cols].unsqueeze(1).to_broadcast([NU * NSB, rows, cols])
                    prod = solve_tmp[:, 0:rows * cols].rearrange("p (i c) -> p i c", c=cols)
                    dve.tensor_tensor(prod, coef, row, ALU.mult).then_inc(S["solve_step"], 1)
                    dve.wait_ge(S["solve_step"], base + 2 * j + 1)
                    rest = tinv[:, (j + 1) * SB:].rearrange("p (i c) -> p i c", c=SB)[:, :, 0:cols]
                    dve.tensor_tensor(rest, rest, prod, ALU.add).then_inc(S["solve_step"], 1)

            def flush(c, j):
                n = c.n
                dve.wait_ge(S["rr_ready"], n * NC + j + 1)
                dve.wait_ge(S["sg_ready"], n * 2 + j // 2 + 1)
                dve.wait_ge(S["gtr_done"], n * NC + j)
                for h in range(2):
                    dve.scalar_tensor_tensor(out=gt[:, h, :], in0=ob[:, j % 2, h * P:(h + 1) * P], scalar=rr[:, j % 2, h:h + 1],
                                             in1=sg[:, j, h * P:(h + 1) * P], op0=ALU.mult, op1=ALU.mult
                                             ).then_inc(S["gt_ready"], 1)

            def slot(s, c, a):
                if s is not None:
                    silu(s, 0)
                    silu(s, 1)
                if c is not None:
                    n, p = c.n, c.p
                    dve.wait_ge(S["t16_in"], n * 16 + 16)
                    dve.wait_ge(S["mdiag_done"], n)
                    dve.transpose(t16_t[:, :, :].rearrange("p u i -> p (u i)"), t16[:, :, :].rearrange("p u i -> p (u i)")
                                  ).then_inc(S["t16t_ready"], 1)
                    dve.wait_ge(S["q0_done"], n + 1)
                    dve.scalar_tensor_tensor(out=q0s[:, :, 0:SB], in0=R[0][:, 0:NU * BL].rearrange(
                        "p (u i) -> p u i", u=NU)[:, :, 0:SB], scalar=second_half[:, 0:1],
                        in1=ident_bl[:, 0:SB].unsqueeze(1).to_broadcast([P, NU, SB]), op0=ALU.mult, op1=ALU.add
                        ).then_inc(S["q0_ready"], 1)
                if s is not None:
                    grams(s)
                if c is not None:
                    dve.wait_ge(S["mdiag_done"], n + 1)
                    dve.wait_ge(S["q1_done"], n)
                    dve.wait_ge(S["t64_diag"], n * 2)
                    dve.transpose(t32[:, :, :].rearrange("p u i -> p (u i)"), R[2][:, 0:NU * BL]).then_inc(S["t32_ready"], 1)
                    dve.wait_ge(S["w_done"], n * NC)
                    for b in range(NBL):
                        blk = slice(b * BL, (b + 1) * BL)
                        dve.tensor_copy(minv[blk, :, blk], R[2][blk, 0:NU * BL].rearrange("p (u i) -> p u i", u=NU)
                                        ).then_inc(S["mdiag"], 1)
                if s is not None:
                    norms(s)
                    silu(s, 2)
                    taps(s, 3)
                if c is not None:
                    dve.wait_ge(S["t21_done"], n + 1)
                    dve.tensor_copy(t64[BL:64, :, 0:BL], R[2][BL:64, 0:NU * BL].rearrange("p (u i) -> p u i", u=NU)
                                    ).then_inc(S["t21_ready"], 1)
                if s is not None:
                    silu(s, 3)
                    systems(s, 0)
                if c is not None:
                    dve.wait_ge(S["q2_done"], n + 1)
                    dve.tensor_copy(q2s[64:P, :, :], R[0][64:P, :].rearrange("p (u i) -> p u i", u=NU)
                                    ).then_inc(S["q2_ready"], 1)
                if s is not None:
                    systems(s, 1)
                    products(s)
                for j in range(NC):
                    if c is not None:
                        dve.wait_ge(S["ks_done"], n * NC + j + 1)
                        dve.wait_ge(S["vs_ready"], n * NU + NU)
                        dve.wait_ge(S["w_done"], n * NC + j)
                        for h in range(2):
                            dve.scalar_tensor_tensor(out=rn[:, h, :], in0=R[0][:, h * P:(h + 1) * P],
                                                     scalar=sc[p][:, EXP_G, j, h:h + 1], in1=vs[p][:, unit(h, j), :],
                                                     op0=ALU.mult, op1=ALU.subtract).then_inc(S["r_ready"], 1)
                    if s is not None and j > 0:
                        solve(s, *((0, 4), (4, 8), (12, SB - 1))[j - 1])
                    if c is not None:
                        dve.wait_ge(S["su_done"], n * NC + j + 1)
                        for h in range(2):
                            dve.scalar_tensor_tensor(out=sw[p][:, h * P:(h + 1) * P], in0=sw[p][:, h * P:(h + 1) * P],
                                                     scalar=sc[p][:, EXP_ALL, j, h:h + 1], in1=R[2][:, h * P:(h + 1) * P],
                                                     op0=ALU.mult, op1=ALU.add).then_inc(S["s_upd"], 1)
                        dve.wait_ge(S["pu_done"], n * NC + j + 1)
                        dve.wait_ge(S["tq_ready"], n * NU + 2 * j + 2)
                        dve.scalar_tensor_tensor(out=ob[:, j % 2, :], in0=R[1][:, 2 * P:4 * P],
                                                 scalar=sca[p][:, RQ + j:RQ + j + 1],
                                                 in1=tmpq[:, :, :].rearrange("p h i -> p (h i)"), op0=ALU.mult, op1=ALU.add
                                                 ).then_inc(S["o_ready"], 1)
                        if j > 0:
                            flush(c, j - 1)
                    if a is not None and j in (1, 3):
                        taps(a, j // 2)
                    if s is not None and j == 2:
                        solve(s, 8, 12)
                if c is not None:
                    flush(c, NC - 1)
                if a is not None:
                    taps(a, 2)

            def layernorm(src, t, second):
                base = t * 16 + 8 * second
                for c in range(NC):
                    dve.bn_stats(stats[:, c, :], src[:, c, :]).then_inc(S["ln_stats"], 1)
                wait_apart(dve, S["ln_stats"], base + 4)
                for c in range(NC):
                    dve.bn_aggr(mean_var[:, c, :], stats[:, c, :]).then_inc(S["ln_stats"], 1)
                dve.wait_ge(S["ln_stats"], base + 8)
                dve.wait_ge(S["ln_rstd"], t * 2 + second + 1)
                for c in range(NC):
                    dve.tensor_scalar(hn[:, c, :], src[:, c, :], mean_var[:, c, 0:1], rstd[:, c:c + 1], ALU.subtract, ALU.mult
                                      ).then_inc(S["hn_ready"], 1)

            def gated_add(dst, src, banks, gate, half_sem, done_sem, base):
                for i in range(2):
                    dve.tensor_tensor(y_tmp[:, 2 * i:2 * i + 2, :], banks[i][:, :].rearrange("p (c d) -> p c d", c=2),
                                      gate_b[:, gate, :].unsqueeze(1).to_broadcast([P, 2, D]), ALU.mult).then_inc(half_sem, 1)
                    dve.wait_ge(half_sem, base + i + 1)
                    dve.tensor_tensor(dst[:, 2 * i:2 * i + 2, :], y_tmp[:, 2 * i:2 * i + 2, :], src[:, 2 * i:2 * i + 2, :],
                                      ALU.add).then_inc(done_sem, 1)

            def tile(t, b, m0):
                n_end = (m0 + KH // 2) * 2
                dve.wait_ge(S["x_in"], t * 16 + 16)
                layernorm(xt, t, 0)
                dve.wait_ge(S["ba_done"], t + 1)
                dve.tensor_tensor(au[:, :, :], R[2][:, 0:NC * 2 * VH].rearrange("p (c h) -> p c h", c=NC)[:, :, VH:2 * VH],
                                  dt_b[:, :].unsqueeze(1).to_broadcast([P, NC, VH]), ALU.add).then_inc(S["au_ready"], 1)
                dve.wait_ge(S["aln_ready"], t + 1)
                dve.wait_ge(S["au_ready"], t + 1)
                dve.scalar_tensor_tensor(out=au[:, :, :], in0=au[:, :, :], scalar=0.0, in1=a_ln[:, :, :],
                                         op0=ALU.max, op1=ALU.add).then_inc(S["g_mul"], 1)
                dve.wait_ge(S["g_mul"], t + 1)
                dve.tensor_tensor(table[:, G_, :, :], au[:, :, :], neg_exp_a[:, :].unsqueeze(1).to_broadcast([P, NC, VH]),
                                  ALU.mult).then_inc(S["g_ready"], 1)
                slots(dve, m0, A, slot)
                dve.wait_ge(S["y_done"], n_end * NC + NC)
                dve.wait_ge(S["out_stored"], t * 16)
                dve.wait_ge(S["mod_copied"], t * 2 + 2)
                gated_add(x1, xt, Y, 0, S["x1_half"], S["x1_ready"], t * 2)
                dve.wait_ge(S["x1_ready"], t * 2 + 2)
                layernorm(x1, t, 1)
                for i in range(NI):
                    gate, up = (PB[0], PB[1]) if i % 2 == 0 else (R[2], R[3])
                    dve.wait_ge(S["th_ff"], t * NI + i + 1)
                    dve.wait_ge(S["ff_ready"], t * NI + max(i - 1, 0))
                    dve.scalar_tensor_tensor(out=ff_g[:, i % 2, :], in0=ff_th[:, i % 2, :], scalar=1.0, in1=gate[:, :],
                                             op0=ALU.add, op1=ALU.mult).then_inc(S["ff_half"], 1)
                    dve.wait_ge(S["ff_half"], t * NI + i + 1)
                    dve.wait_ge(S["up_done"], t * NI + i + 1)
                    dve.scalar_tensor_tensor(out=ff[:, i, :], in0=ff_g[:, i % 2, :], scalar=0.5, in1=up[:, :],
                                             op0=ALU.mult, op1=ALU.mult).then_inc(S["ff_ready"], 1)
                dve.wait_ge(S["down_done"], t * 2 + 2)
                gated_add(y_tmp, x1, R, 1, S["down_half"], S["out_ready"], t * 2)

            tile_loop(dve, tile)

        @block.tensor
        def _(pe):
            mm = pe.matmul

            pe.wait_ge(S["pool_setup"], POOL_SETUP)
            pe.wait_ge(S["in_conv"], 32)
            pe.wait_ge(S["dve_setup"], 4)
            taps_rows = x1[0:64, 0:2, :].rearrange("t a b -> t (a b)").rearrange("t (c w) -> t c w", w=CONV_K)
            for w in range(CONV_K):
                pe.transpose(R[0][:, w * 64:(w + 1) * 64], taps_rows[:, :, w], ident[0:64, 0:64])
            pe.transpose(R[0][:, 4 * 64:5 * 64], x1[0:64, 2, 0:P], ident[0:64, 0:64]).then_inc(S["pe_setup"], 1)
            pe.wait_ge(S["in_wmod"], 16)
            pe.wait_ge(S["dve_setup"], 4 + 3 + KD * BATCH)
            wm = ff[:, :, :].rearrange("p a b -> p (a b)")[:, 0:KD * 6 * D].rearrange("p (k n) -> p k n", k=KD)
            for i, v in enumerate(VEC):
                for hh in range(KD):
                    o = (i * KD + hh) * BATCH
                    for k in range(KD):
                        mm(R[1][:, o:o + BATCH], wm[:, k, v * D + hh * P:v * D + (hh + 1) * P], cond_silu[:, k, :],
                           start=(k == 0), stop=(k == KD - 1))
            cond_rows = hn[:, :, :].rearrange("p a (b i) -> p (a b) i", i=P)
            for b, bank in enumerate((R[2], R[3], PB[0], PB[1])):
                for i, v in enumerate((2, 5)):
                    for k in range(KD):
                        last = mm(bank[:, i * D:(i + 1) * D], cond_rows[:, k * BATCH + b, :], wm[:, k, v * D:(v + 1) * D],
                                  start=(k == 0), stop=(k == KD - 1))
            last.then_inc(S["pe_setup"], 1)
            pe.wait_ge(S["in_gu"], 16)
            pe.wait_ge(S["in_down"], 32)
            rows = ff[:, :, :].rearrange("p a (b n) -> p (a b) n", n=D)
            for n in range(MLP_BATCHES):
                pe.wait_ge(S["dve_setup"], DVE_SETUP - MLP_BATCHES + max(n - 3, 0))
                for i in range(4):
                    if n < 8:
                        k, o = n // 4, n % 4 * 4 + i
                        src = rows[:, o, k * P:(k + 1) * P]
                    else:
                        col = (2 * (n - 8) + i // 2) * P
                        src = raw[:, 2 * (i % 2) + col // TOK, col % TOK:col % TOK + P]
                    last = pe.transpose(R[n % 4][:, i * P:(i + 1) * P], src, ident[:, :])
                last.then_inc(S["pe_setup"], 1)

            def project(a, i, k):
                n = a.n
                if k == 0:
                    if i == 0:
                        pe.wait_ge(wa_in[a.p], a.m * 48 + 48)
                    if i < 2:
                        pe.wait_ge(S["vs_ready"], n * NU)
                    else:
                        pe.wait_ge(S["conv_in"], n * 4 + i - 1)
                last = mm(PB[i % 2][:, :], wa[a.p][:, k, i * P:(i + 1) * P], ht[:, k, :], start=(k == 0), stop=(k == KD - 1))
                if k == KD - 1:
                    last.then_inc(S["proj_done"], 1)

            def decay(a, h):
                n = a.n
                pe.wait_ge(S["gm_ready"], n * NU + NU)
                pe.wait_ge(S["conv_in"], n * 4 + 3 + h)
                mm(PB[h][:, :], mask_after[:, :], gm[:, h * NC:(h + 1) * NC, :].rearrange("p c i -> p (c i)"),
                   start=True, stop=True).then_inc(S["d_done"], 1)

            def A(a):
                for i in range(4):
                    for k in range(KD):
                        project(a, i, k)
                for h in range(2):
                    decay(a, h)

            def grams(s):
                n, p = s.n, s.p
                for i, (rhs, done) in enumerate(((kt[p], S["kk_done"]), (qt[p], S["kq_done"]))):
                    pe.wait_ge(S["d_ready"], n * 2 + i + 1)
                    pe.wait_ge(S["silu_done"], n * 4 + 2)
                    for c in range(NC):
                        cs = slice(c * C, (c + 1) * C)
                        last = mm(PB[i][:, cs], kt[p][:, cs], rhs[:, cs], start=True, stop=True)
                    last.then_inc(done, 1)

            def norms(s):
                n = s.n
                pe.wait_ge(S["kkm_ready"], n + 1)
                pe.wait_ge(S["sq_ready"], n * 2 + 2)
                for i in range(2):
                    for c in range(NC):
                        last = mm(PB[0][:, i * NC + c:i * NC + c + 1], sq[:, i, c * C:(c + 1) * C], ones[:, 0:1],
                                  start=True, stop=True)
                last.then_inc(S["norms_done"], 1)

            def k_rows(s):
                pe.wait_ge(S["kqm_ready"], s.n + 1)
                for c in range(NC):
                    last = pe.transpose(PB[1][:, c * P:(c + 1) * P], kt[s.p][:, c * C:(c + 1) * C], ident[:, :])
                last.then_inc(S["kt_done"], 1)

            def v_rows(s, h):
                n = s.n
                pe.wait_ge(S["ktok_ready"] if h else S["ss_ready"], n + 1)
                pe.wait_ge(S["silu_done"], n * 4 + 3 + h)
                for c in range(NC):
                    last = pe.transpose(PB[h][:, c * P:(c + 1) * P], vt[:, h, c * C:(c + 1) * C], ident[:, :])
                last.then_inc(S["v_tr"], 1)

            def to_value_channels(c, j):
                n = c.n
                pe.wait_ge(S["gt_ready"], n * NU + 2 * j + 2)
                pe.wait_ge(S["got_ready"], n * NC + j)
                if j == 0:
                    pe.wait_ge(S["z_ready"], n * 2 + 2)
                for h in range(2):
                    last = pe.transpose(R[3][:, h * P:(h + 1) * P], gt[:, h, :], ident[:, :])
                last.then_inc(S["gtr_done"], 1)

            def project_out(c, j):
                n, p = c.n, c.p
                pe.wait_ge(S["got_ready"], n * NC + j + 1)
                for h in range(2):
                    last = mm(Y[j // 2][:, j % 2 * D:(j % 2 + 1) * D], got[:, h, :], wo[p][:, h, :], start=False, stop=False,
                              skip_group_check=True)
                last.then_inc(S["y_done"], 1)

            def join16(c):
                n, p = c.n, c.p
                pe.wait_ge(S["lt_ready"], n * NU + NU)
                wait_apart(pe, S["t16_in"], n * 16 + 16)
                for u in range(NU):
                    for b in range(NBL):
                        blk = slice(b * BL, (b + 1) * BL)
                        last = mm(R[0][blk, u * BL:u * BL + SB], lt[p][blk, u, blk], t16[blk, u, 0:SB], start=True, stop=True)
                last.then_inc(S["q0_done"], 1)

            def make32(c):
                n = c.n
                pe.wait_ge(S["t16t_ready"], n + 1)
                pe.wait_ge(S["q0_ready"], n + 1)
                wait_apart(pe, S["z_ready"], n * 2 + 1)
                for u in range(NU):
                    for b in range(NBL):
                        blk = slice(b * BL, (b + 1) * BL)
                        last = mm(R[2][blk, u * BL:(u + 1) * BL], q0s[blk, u, :], t16_t[blk, u, :], start=True, stop=True)
                last.then_inc(S["mdiag_done"], 1)

            def join32(c):
                n, p = c.n, c.p
                wait_apart(pe, S["t32_ready"], n + 1)
                for u in range(NU):
                    for b in range(2):
                        lo, mid, hi = 64 * b, 64 * b + BL, 64 * b + 64
                        last = mm(R[0][mid:hi, u * BL:(u + 1) * BL], lt[p][lo:mid, u, mid:hi], t32[lo:mid, u, :],
                                  start=True, stop=True)
                last.then_inc(S["q1_done"], 1)

            def make64(c):
                n = c.n
                pe.wait_ge(S["q1_ready"], n + 1)
                pe.wait_ge(S["o_ready"], n * NC)
                wait_apart(pe, S["mdiag"], n * NBL + NBL)
                for u in range(NU):
                    for b in range(2):
                        lo, mid, hi = 64 * b, 64 * b + BL, 64 * b + 64
                        last = mm(R[1][lo:mid, u * BL:(u + 1) * BL], q1s[mid:hi, u, :], minv[mid:hi, u, mid:hi],
                                  start=True, stop=True)
                last.then_inc(S["m12_done"], 1)
                for u in range(NU):
                    last = mm(R[2][BL:64, u * BL:(u + 1) * BL], minv[BL:64, u, BL:64], q1s[BL:64, u, :], start=True, stop=True)
                last.then_inc(S["t21_done"], 1)

            def join64(c):
                n, p = c.n, c.p
                pe.wait_ge(S["t21_ready"], n + 1)
                wait_apart(pe, S["t64_diag"], n * 2 + 2)
                for u in range(NU):
                    last = mm(R[0][64:P, u * 64:(u + 1) * 64], lt[p][0:64, u, 64:P], t64[:, u, :], start=True, stop=True)
                last.then_inc(S["q2_done"], 1)

            def make128(c):
                n = c.n
                pe.wait_ge(S["q2_ready"], n + 1)
                wait_apart(pe, S["m12_ready"], n * 2 + 2)
                for u in range(NU):
                    last = mm(R[1][0:64, u * 64:(u + 1) * 64], q2s[64:P, u, :], minv[64:P, u, 64:P], start=True, stop=True)
                last.then_inc(S["m2_done"], 1)

            def states_in(c, j):
                n, p = c.n, c.p
                cs = slice(j * C, (j + 1) * C)
                if j == 0:
                    pe.wait_ge(S["s_load"], n + 1)
                    pe.wait_ge(S["minv_ready"], n + 1)
                else:
                    pe.wait_ge(S["s_upd"], n * NU + 2 * j)
                mm(R[0][:, 0:2 * P], kt[p][:, cs], sw[p][:, :], start=True, stop=True).then_inc(S["ks_done"], 1)
                if j > 0:
                    pe.wait_ge(S["o_ready"], n * NC + j)
                mm(R[1][:, 0:2 * P], qt[p][:, cs], sw[p][:, :], start=True, stop=True).then_inc(S["qs_done"], 1)

            def w_rows(c, j):
                n = c.n
                for h in range(2):
                    pe.wait_ge(S["r_ready"], n * NU + 2 * j + h + 1)
                    last = mm(R[2][:, (2 + h) * P:(3 + h) * P], minv[:, unit(h, j), :], rn[:, h, :], start=True, stop=True)
                last.then_inc(S["w_done"], 1)

            def chunk_out(c, j):
                n, p = c.n, c.p
                pe.wait_ge(S["k2_ready"], n * NU + NU)
                pe.wait_ge(S["u_ready"], n * NU + 2 * j + 2)
                for h in range(2):
                    last = mm(R[2][:, h * P:(h + 1) * P], k2[p][:, unit(h, j), :], us[:, h, :], start=True, stop=True)
                last.then_inc(S["su_done"], 1)
                pe.wait_ge(S["pt_ready"], n * 2 + 2)
                pe.wait_ge(S["tq_ready"], n * NU + 2 * j + 2)
                for h in range(2):
                    last = mm(R[1][:, (2 + h) * P:(3 + h) * P], pt[p][:, unit(h, j), :], us[:, h, :], start=True, stop=True)
                last.then_inc(S["pu_done"], 1)

            def z_rows(c, j):
                n, p = c.n, c.p
                if j == 0:
                    pe.wait_ge(wc_in[p], c.m * 32 + 32)
                    pe.wait_ge(S["s_upd"], n * NU)
                elif j == 2:
                    pe.wait_ge(S["got_ready"], n * NC)
                for k in range(KD):
                    last = mm(R[2 + j // 2][:, j % 2 * 2 * P:(j % 2 + 1) * 2 * P], ht[:, k, j * C:(j + 1) * C], wz[p][:, k, :],
                              start=(k == 0), stop=(k == KD - 1))
                if j % 2:
                    last.then_inc(S["z_done"], 1)

            def slot(s, c, a):
                if c is not None:
                    join16(c)
                if s is not None:
                    grams(s)
                if c is not None:
                    make32(c)
                if s is not None:
                    norms(s)
                if c is not None:
                    join32(c)
                if s is not None:
                    k_rows(s)
                if c is not None:
                    make64(c)
                if s is not None:
                    v_rows(s, 0)
                if c is not None:
                    z_rows(c, 2)
                    join64(c)
                    z_rows(c, 3)
                    make128(c)
                if s is not None:
                    v_rows(s, 1)
                for j in range(NC):
                    if c is not None:
                        states_in(c, j)
                        if j > 1:
                            to_value_channels(c, j - 2)
                        w_rows(c, j)
                    if a is not None:
                        project(a, j, 0)
                    if c is not None:
                        chunk_out(c, j)
                        if j > 1:
                            project_out(c, j - 2)
                    if a is not None:
                        project(a, j, 1)
                if c is not None:
                    to_value_channels(c, NC - 2)
                if a is not None:
                    for h in range(2):
                        decay(a, h)
                if c is not None:
                    project_out(c, NC - 2)
                    to_value_channels(c, NC - 1)
                if s is not None:
                    z_rows(s, 0)
                    z_rows(s, 1)
                if c is not None:
                    project_out(c, NC - 1)

            def to_channels(t, second):
                pe.wait_ge(S["hn_ready"], t * 8 + 4 * second + 4)
                for k in range(KD):
                    for c in range(NC):
                        last = pe.transpose(R[k][:, c * P:(c + 1) * P], hn[:, c, k * P:(k + 1) * P], ident[:, :])
                    last.then_inc(S["ht_psum"], 1)

            pe.sem_inc(S["y_done"], NC)
            pe.sem_inc(S["qs_done"], NC)

            def tile(t, b, m0):
                n_end = (m0 + KH // 2) * 2
                pe.wait_ge(S["dve_setup"], DVE_SETUP)
                pe.wait_ge(S["out_ready"], t * 2)
                pe.wait_ge(S["ff_ready"], t * NI)
                to_channels(t, 0)
                pe.wait_ge(S["x1_half"], t * 2)
                for y in Y:
                    last = mm(y[:, :], zero_b[:, 0:P], zero_b[:, :], start=True, stop=True)
                pe.wait_ge(S["ht_ready"], t * 4 + 2)
                for c in range(NC):
                    for k in range(KD):
                        last = mm(R[2][:, c * 2 * VH:(c + 1) * 2 * VH], ht[:, k, c * C:(c + 1) * C], w_ba[:, k, :],
                                  start=(k == 0), stop=(k == KD - 1))
                last.then_inc(S["ba_done"], 1)
                pe.wait_ge(S["g_ready"], t + 1)
                g_all = table[:, G_, :, :].rearrange("p c h -> p (c h)")
                for i, m in enumerate((mask_incl, mask_after, ones)):
                    last = mm(R[3][:, i * NC * VH:(i + 1) * NC * VH], m[:, :], g_all, start=True, stop=True)
                last.then_inc(S["cum_done"], 1)
                pe.wait_ge(S["thb_ready"], t + 1)
                pe.wait_ge(S["exp_ready"], t + 1)
                slots(pe, m0, A, slot)
                pe.wait_ge(S["o_ready"], n_end * NC)
                pe.wait_ge(S["tq_ready"], n_end * NU)
                to_channels(t, 1)
                pe.wait_ge(S["ht_ready"], t * 4 + 4)
                pe.wait_ge(S["vs_ready"], n_end * NU)
                pe.wait_ge(S["s_upd"], n_end * NU)
                pe.wait_ge(S["got_ready"], n_end * NC)
                for i in range(NI):
                    pair = (PB[0], PB[1]) if i % 2 == 0 else (R[2], R[3])
                    if i >= 2:
                        pe.wait_ge(S["ff_ready"], t * NI + i - 1)
                    for bank, o, done in ((pair[0], i, S["gate_done"]), (pair[1], NI + i, S["up_done"])):
                        for k in range(KD):
                            last = mm(bank[:, :], wgu_t[:, k, o * P:(o + 1) * P], ht[:, k, :], start=(k == 0), stop=(k == KD - 1))
                        last.then_inc(done, 1)
                pe.wait_ge(S["ff_ready"], t * NI + NI)
                for c in range(NC):
                    for i in range(NI):
                        last = mm(R[c // 2][:, c % 2 * D:(c % 2 + 1) * D], ff[:, i, c * C:(c + 1) * C], wd_t[:, i, :],
                                  start=(i == 0), stop=(i == NI - 1))
                    if c % 2:
                        last.then_inc(S["down_done"], 1)

            tile_loop(pe, tile)


_INS = ['L0_attn_hidden_states', 'L0_attn_W_qkv', 'L0_attn_W_z', 'L0_attn_W_b', 'L0_attn_W_a', 'L0_attn_conv_w',
        'L0_attn_conv_b', 'L0_attn_dt_bias', 'L0_attn_A_log', 'L0_attn_norm_gamma', 'L0_attn_W_out',
        'L0_ffn_w_gate_up', 'L0_ffn_w_down', 'L0_c', 'L0_wmod']
_OUTS = [((BATCH, SEQ, D), 'float32')]


def kernel(**inputs):
    import numpy as _np
    import concourse.bacc as _bacc
    from concourse import mybir as _mybir
    from concourse.bass_utils import run_bass_kernel_spmd as _run

    nc = _bacc.Bacc("TRN2", target_bir_lowering=False, num_devices=1)
    arrays, args = {}, []
    for name in _INS:
        a = _np.ascontiguousarray(inputs[name])
        arrays[f"in_{name}_dram"] = a
        args.append(nc.dram_tensor(f"in_{name}_dram", a.shape, _mybir.dt.from_np(a.dtype), kind="ExternalInput").ap())
    for i, (shape, dtype) in enumerate(_OUTS):
        dt = _mybir.dt.from_np(_np.dtype(dtype))
        args.append(nc.dram_tensor(f"out_{i}_dram", shape, dt, kind="ExternalOutput").ap())
    adaln_block(nc, *args)
    r = _run(nc, [arrays], core_ids=[0])
    return r.results[0]["out_0_dram"]
```

```python
from contextlib import ExitStack

import concourse.bass as bass
from concourse import mybir
from typing import Any, NamedTuple

F32 = mybir.dt.float32
BF16 = mybir.dt.bfloat16
ALU = mybir.AluOpType
ACT = mybir.ActivationFunctionType

P = 128
BATCH, SEQ, D = 4, 1024, 256
KH, VH = 16, 32
C = 128
NC = 4
TOK = C * NC
TILES_PER_BATCH = SEQ // TOK
KD = D // P
KEY_DIM = KH * P
CONV_K = 4
TAIL = CONV_K - 1
INTER = 1024
NI = INTER // P
NU = 2 * NC
START = 1
BL = 32
NBL = C // BL
SB = 16
NSB = C // SB
SOLVE_OPS = 2 * (SB - 1)
EPS_NORM = 1e-6
EPS_LN = 1e-5
GATE_MIN = 0.25
BETA, G_, EXP_G, EXP_REST, EXP_ALL = range(5)
RQ, NK, NAA, EGQ = 0, NC, 2 * NC, 4 * NC
VEC = (0, 1, 3, 4)
SCALAR_OPS = 8
MLP_BATCHES = 12
POOL_SETUP = 15
DVE_SETUP = 4 + 3 + KD * BATCH + 4 + 3 + 4 * BATCH + 3 + MLP_BATCHES


class Item(NamedTuple):

    m: Any
    p: int
    k: Any

    @property
    def n(self):
        return 2 * self.m + self.p


def adaln_block(nc, x, w_qkv, w_z, w_b, w_a, conv_w, conv_b, dt_bias, a_log, gamma, w_out,
                w_gate_up, w_down, cond, w_mod, out):
    ctx = ExitStack()

    def sb(name, shape, dt=F32):
        return ctx.enter_context(nc.sbuf_tensor(name, shape, dt))

    def sem(name):
        return ctx.enter_context(nc.semaphore(name))

    with ctx:
        mask_incl = sb("mask_incl", [P, P])
        mask_strict = sb("mask_strict", [P, P])
        mask_after = sb("mask_after", [P, P])
        ident = sb("ident", [P, P])
        ones = sb("ones", [P, P])
        eye_blocks = sb("eye_blocks", [NU * NSB, SB * SB])
        ident_bl = sb("ident_bl", [P, BL])
        second_half = sb("second_half", [P, 1])
        minus_half = sb("minus_half", [P, 8])
        zero_b = sb("zero_b", [P, 512], BF16)
        conv_par = sb("conv_par", [P, KH, 4, 5])
        w_ba = sb("w_ba", [P, KD, 2 * VH])
        dt_b = sb("dt_b", [P, VH])
        neg_exp_a = sb("neg_exp_a", [P, VH])
        gamma_c = sb("gamma_c", [P, 1])
        cond_t = sb("cond_t", [P, KD, BATCH])
        cond_th = sb("cond_th", [P, KD, BATCH])
        cond_silu = sb("cond_silu", [P, KD, BATCH])
        mod_t = sb("mod_t", [P, 4, KD, BATCH])
        gate_rows = sb("gate_rows", [P, BATCH, 2, D])
        wgu_t = sb("wgu_t", [P, KD, 2 * INTER])
        wd_t = sb("wd_t", [P, NI, D])
        xt = sb("xt", [P, NC, D])
        ht = sb("ht", [P, KD, TOK])
        stats = sb("stats", [P, NC, 6])
        mean_var = sb("mean_var", [P, NC, 2])
        rstd = sb("rstd", [P, NC])
        mod_b = sb("mod_b", [P, 4, KD])
        gate_b = sb("gate_b", [P, 2, D])
        au = sb("au", [P, NC, VH])
        th_b = sb("th_b", [P, NC, VH])
        table = sb("table", [P, 5, NC, VH])
        states = sb("states", [P, KH, 2 * P])
        tails = sb("tails", [P, KH, 4, TAIL])
        wa = [sb(f"wa{p}", [P, KD, 4 * P]) for p in range(2)]
        wz = [sb(f"wz{p}", [P, KD, 2 * P]) for p in range(2)]
        wo = [sb(f"wo{p}", [P, 2, D]) for p in range(2)]
        qt = [sb(f"qt{p}", [P, TOK]) for p in range(2)]
        kt = [sb(f"kt{p}", [P, TOK]) for p in range(2)]
        lt = [sb(f"lt{p}", [P, NU, C]) for p in range(2)]
        pt = [sb(f"pt{p}", [P, NU, C]) for p in range(2)]
        vs = [sb(f"vs{p}", [P, NU, P]) for p in range(2)]
        k2 = [sb(f"k2{p}", [P, NU, P]) for p in range(2)]
        sc = [sb(f"sc{p}", [P, 5, NC, 2]) for p in range(2)]
        sca = [sb(f"sca{p}", [P, 6 * NC]) for p in range(2)]
        sw = [sb(f"sw{p}", [P, 2 * P]) for p in range(2)]
        cwp = sb("cwp", [P, 4, 5])
        g_item = sb("g_item", [P, NC, 2])
        gm = sb("gm", [P, NU, C])
        raw = sb("raw", [P, 4, TAIL + TOK])
        cv_th = sb("cv_th", [P, 8, TOK])
        cv, th, ff = cv_th[:, 0:4, :], cv_th[:, 4:8, :], cv_th
        vt = sb("vt", [P, 2, TOK])
        sq = sb("sq", [P, 2, TOK])
        ff_th, ff_g = vt, sq
        dec = sb("dec", [P, NU, C])
        kkm = sb("kkm", [P, NC, C])
        kqm = sb("kqm", [P, NC, C])
        ss = sb("ss", [P, 2 * NC])
        ssk = sb("ssk", [P, NC])
        rs = sb("rs", [P, 2 * NC])
        rk2 = sb("rk2", [P, 3 * NC])
        ktok = sb("ktok", [P, NC, P])
        blocks = sb("blocks", [NU * NSB, SB * SB])
        tinv = sb("tinv", [NU * NSB, SB * SB])
        solve_tmp = sb("solve_tmp", [NU * NSB, SB * SB // 4 + SB])
        t16 = sb("t16", [P, NU, BL])
        t16_t = sb("t16_t", [P, NU, BL])
        q0s = sb("q0s", [P, NU, BL])
        t32 = sb("t32", [P, NU, BL])
        minv = sb("minv", [P, NU, C])
        t64 = sb("t64", [64, NU, 64])
        q1s = sb("q1s", [P, NU, BL])
        q2s = sb("q2s", [P, NU, 64])
        rn = sb("rn", [P, 2, P])
        tmpq = sb("tmpq", [P, 2, P])
        us = sb("us", [P, 2, P])
        thz = sb("thz", [P, 2, 2 * P])
        sg = sb("sg", [P, NC, 2 * P])
        ob = sb("ob", [P, 2, 2 * P])
        ssq = sb("ssq", [P, 2, 2])
        rr = sb("rr", [P, 2, 2])
        gt = sb("gt", [P, 2, P])
        got = sb("got", [P, 2, P])

        junk = q1s[:, 0:NC, :]
        hn = gm[:, :, :].rearrange("p (c a) i -> p c (a i)", c=NC)
        x1 = dec[:, :, :].rearrange("p (c a) i -> p c (a i)", c=NC)
        y_tmp = raw[:, :, 0:D]
        a_abs, a_exp, a_ln = (kqm[:, i, :].rearrange("p (c h) -> p c h", c=NC) for i in range(3))

        l_scr = nc.dram_tensor("l_scratch", [NU * NBL, BL * BL], F32, kind="Internal").ap()
        t_scr = nc.dram_tensor("t_scratch", [NU * NBL, BL * BL], F32, kind="Internal").ap()

        Y = [ctx.enter_context(nc.psum_tensor(f"y{i}", [P, 512], F32)) for i in range(2)]
        PB = [ctx.enter_context(nc.psum_tensor(f"pb{i}", [P, 512], F32)) for i in range(2)]
        R = [ctx.enter_context(nc.psum_tensor(f"r{i}", [P, 512], F32)) for i in range(4)]

        once = """pool_setup in_small in_cond in_wmod in_gu in_down in_conv act_setup pe_setup dve_setup scratch_zero"""
        counted = """x_in ln_stats ln_eps ln_rstd hn_ready ht_psum ht_ready ba_done au_ready thb_ready abs_ready aexp_ready
        aln_ready g_ready g_mul cum_done exp_ready beta_ready y_clear mod_copied
        x1_half x1_ready gate_done up_done th_ff ff_half ff_ready down_done down_half out_ready out_stored zeroed
        wa0 wa1 wc0 wc1
        a_in gm_ready proj_done raw_in conv_in conv_tap tail_saved d_done d_ready
        th_ready silu_done sq_ready kk_done kq_done kkm_ready kqm_ready norms_done ss_ready ssk_ready
        scal_step sc_ready kt_done ktok_ready k2_ready v_tr vs_ready lt_ready pt_ready
        lb_out lb_in tb_init solve_step tb_out t16_in
        t16t_ready q0_done q0_ready mdiag_done t32_ready
        mdiag t64_diag q1_done q1_ready m12_done t21_done m12_ready t21_ready q2_done q2_ready m2_done minv_ready
        s_load s_store ks_done qs_done r_ready tq_ready w_done u_ready su_done pu_done s_upd o_ready
        z_done z_ready sg_ready og_ready sq_acc rr_eps rr_ready gt_ready gtr_done got_ready y_done"""
        S = {n: sem(n) for n in once.split() + counted.split()}
        passed = {eng: sem(f"passed_{name}") for name, eng in
                  (("sp", nc.sync), ("pool", nc.gpsimd), ("dve", nc.vector), ("pe", nc.tensor))}
        wa_in, wc_in = [S["wa0"], S["wa1"]], [S["wc0"], S["wc1"]]

        def wait_apart(eng, sem, value):
            eng.wait_ge(sem, value)
            eng.sem_inc(passed[eng], 1)

        def tile_loop(eng, body, batch_start=None):
            with eng.Fori(0, BATCH) as b:
                if batch_start:
                    batch_start(b)
                with eng.Fori(0, TILES_PER_BATCH) as half:
                    t = b * TILES_PER_BATCH + half
                    body(t, b, b * (TILES_PER_BATCH * KH // 2) + half * (KH // 2))

        def slots(eng, m0, A, slot):
            last = m0 + (KH // 2 - 1)
            A(Item(m0, 0, 0))
            slot(Item(m0, 0, 0), None, Item(m0, 1, 1))
            with eng.Fori(0, KH // 2 - 1) as i:
                slot(Item(m0 + i, 1, 2 * i + 1), Item(m0 + i, 0, 2 * i), Item(m0 + i + 1, 0, 2 * i + 2))
                slot(Item(m0 + i + 1, 0, 2 * i + 2), Item(m0 + i, 1, 2 * i + 1), Item(m0 + i + 1, 1, 2 * i + 3))
            slot(Item(last, 1, KH - 1), Item(last, 0, KH - 2), None)
            slot(None, Item(last, 1, KH - 1), None)

        def unit(h, c):
            return h * NC + c

        block = ctx.enter_context(nc.Block())

        @block.sync
        def _(sp):
            with nc.allow_non_contiguous_dma(reason="small vectors, once"):
                sp.dma_start(cond_t[:, 0, :], cond[:, 0:P].rearrange("b p -> p b")).then_inc(S["in_cond"], 16)
                sp.dma_start(cond_t[:, 1, :], cond[:, P:2 * P].rearrange("b p -> p b")).then_inc(S["in_cond"], 16)
                sp.dma_start(gamma_c[:, :], gamma.rearrange("(p a) -> p a", a=1)).then_inc(S["in_small"], 16)
            sp.dma_start(dt_b[:, :], dt_bias.rearrange("(a h) -> a h", a=1).to_broadcast([P, VH])).then_inc(S["in_small"], 16)
            sp.dma_start(neg_exp_a[:, :], a_log.rearrange("(a h) -> a h", a=1).to_broadcast([P, VH])).then_inc(S["in_small"], 16)
            sp.dma_start(w_ba[:, :, 0:VH], w_b.rearrange("(k p) h -> p k h", p=P)).then_inc(S["in_small"], 16)
            sp.dma_start(w_ba[:, :, VH:2 * VH], w_a.rearrange("(k p) h -> p k h", p=P)).then_inc(S["in_small"], 16)
            sp.dma_start(x1[0:64, 0:2, :].rearrange("t a b -> t (a b)"),
                         conv_w.rearrange("(t c) k -> t (c k)", c=P)).then_inc(S["in_conv"], 16)
            sp.dma_start(x1[0:64, 2, 0:P], conv_b.rearrange("(t c) -> t c", c=P)).then_inc(S["in_conv"], 16)
            sp.dma_start(ff[:, :, :].rearrange("p a b -> p (a b)")[:, 0:KD * 6 * D].rearrange("p (k n) -> p k n", k=KD),
                         w_mod.rearrange("(k p) n -> p k n", p=P)).then_inc(S["in_wmod"], 16)
            for k in range(KD):
                sp.dma_start(raw[:, 2 * k:2 * k + 2, 0:TOK],
                             w_down[k * P:(k + 1) * P, :].rearrange("p (a b) -> p a b", b=TOK)).then_inc(S["in_down"], 16)
            sp.wait_ge(S["pe_setup"], 2)
            sp.dma_start(ff[:, :, :].rearrange("p a (b n) -> p (a b) n", n=D),
                         w_gate_up.rearrange("(o p) n -> p o n", p=P)).then_inc(S["in_gu"], 16)

            sp.wait_ge(S["pool_setup"], POOL_SETUP)
            sp.dma_start(t_scr, minv[0:NU * NBL, :, :].rearrange("p u i -> p (u i)")).then_inc(S["scratch_zero"], 16)
            sp.wait_ge(S["scratch_zero"], 16)

            for name in counted.split():
                sp.sem_inc(S[name], START)

            def load_wa(p, k):
                w = w_qkv.rearrange("(k p) n -> p k n", p=P)
                sp.dma_start(wa[p][:, :, 0:P], w[:, :, bass.ds(k * P, P)]).then_inc(wa_in[p], 16)
                sp.dma_start(wa[p][:, :, P:2 * P], w[:, :, bass.ds(k * P + KEY_DIM, P)]).then_inc(wa_in[p], 16)
                sp.dma_start(wa[p][:, :, 2 * P:4 * P], w[:, :, bass.ds(k * (2 * P) + 2 * KEY_DIM, 2 * P)]).then_inc(wa_in[p], 16)

            def A(a):
                wait_apart(sp, S["proj_done"], START + a.n * 4)
                load_wa(0, 0)
                load_wa(1, 1)

            def slot(s, c, a):
                if s is None:
                    return
                n = s.n
                if not (isinstance(s.k, int)):
                    wait_apart(sp, S["proj_done"], START + n * 4)
                    load_wa(1 - s.p, s.k + 1)
                wait_apart(sp, S["y_done"], START + n * NC)
                sp.dma_start(wz[s.p][:, :, :], w_z.rearrange("(k p) n -> p k n", p=P)[:, :, bass.ds(s.k * (2 * P), 2 * P)]
                             ).then_inc(wc_in[s.p], 16)
                sp.dma_start(wo[s.p][:, :, :], w_out.rearrange("(h p) n -> p h n", p=P)[:, bass.ds(s.k * 2, 2), :]
                             ).then_inc(wc_in[s.p], 16)
                wait_apart(sp, S["lt_ready"], START + n * NU + NU)
                wait_apart(sp, S["lb_in"], START + n * 32)
                for b in range(NBL):
                    sp.dma_start(l_scr.rearrange("(u b) (j i) -> b j u i", b=NBL, i=BL)[b],
                                 lt[s.p][b * BL:(b + 1) * BL, :, b * BL:(b + 1) * BL]).then_inc(S["lb_out"], 16)
                wait_apart(sp, S["lb_out"], START + n * (16 * NBL) + 16 * NBL)
                wait_apart(sp, S["solve_step"], START + n * SOLVE_OPS)
                for half in range(2):
                    ps, hs = slice(half * NU * NBL, (half + 1) * NU * NBL), slice(half * SB, (half + 1) * SB)
                    sp.dma_start(blocks[ps, :].rearrange("u (j i) -> u j i", i=SB),
                                 l_scr.rearrange("u (j i) -> u j i", i=BL)[:, hs, hs]).then_inc(S["lb_in"], 16)
                wait_apart(sp, S["solve_step"], START + n * SOLVE_OPS + SOLVE_OPS)
                wait_apart(sp, S["t16_in"], START + n * 16)
                for half in range(2):
                    ps, hs = slice(half * NU * NBL, (half + 1) * NU * NBL), slice(half * SB, (half + 1) * SB)
                    sp.dma_start(t_scr.rearrange("u (i c) -> u i c", c=BL)[:, hs, hs],
                                 tinv[ps, :].rearrange("u (i c) -> u i c", c=SB)).then_inc(S["tb_out"], 16)
                wait_apart(sp, S["tb_out"], START + n * 32 + 32)
                wait_apart(sp, S["t16t_ready"], START + n)
                wait_apart(sp, S["q0_done"], START + n)
                sp.dma_start(t16[:, :, :], t_scr.rearrange("(u b) (i c) -> (b i) u c", b=NBL, c=BL)).then_inc(S["t16_in"], 16)

            def tile(t, b, m0):
                wait_apart(sp, S["x1_ready"], START + t * 2)
                by_tile = x.rearrange("b (t c p) d -> (b t) p c d", c=NC, p=P)
                sp.dma_start(xt[:, :, :], by_tile[bass.ds(t, 1), :, :, :].rearrange("a p c d -> p (a c) d")
                             ).then_inc(S["x_in"], 16)
                slots(sp, m0, A, slot)

            tile_loop(sp, tile)
            sp.wait_ge(S["out_stored"], START + 16 * BATCH * TILES_PER_BATCH)

        @block.gpsimd
        def _(pool):
            step = [0]

            def setup(ins, wait=True):
                step[0] += 1
                ins.then_inc(S["pool_setup"], 1)
                if wait:
                    pool.wait_ge(S["pool_setup"], step[0])

            setup(pool.memset(ones[:, :], 1.0), False)
            setup(pool.memset(minus_half[:, :], -0.5), False)
            setup(pool.memset(zero_b[:, :], 0.0), False)
            setup(pool.memset(minv[:, :, :], 0.0), False)
            setup(pool.memset(t64[:, :, :], 0.0), False)
            for m, value in ((mask_incl, 1.0), (mask_strict, 1.0), (mask_after, 1.0), (ident, 0.0)):
                setup(pool.memset(m[:, :], value), False)
            setup(pool.memset(eye_blocks[:, :], 0.0))
            setup(pool.affine_select(out=mask_incl[:, :], in_=mask_incl[:, :], compare_op=ALU.is_ge, fill=0.0,
                                     base=0, pattern=[[1, P]], channel_multiplier=-1), False)
            setup(pool.affine_select(out=mask_strict[:, :], in_=mask_strict[:, :], compare_op=ALU.is_gt, fill=0.0,
                                     base=0, pattern=[[1, P]], channel_multiplier=-1), False)
            setup(pool.affine_select(out=mask_after[:, :], in_=mask_after[:, :], compare_op=ALU.is_gt, fill=0.0,
                                     base=0, pattern=[[-1, P]], channel_multiplier=1), False)
            setup(pool.affine_select(out=ident[:, :], in_=ident[:, :], compare_op=ALU.not_equal, fill=1.0,
                                     base=0, pattern=[[-1, P]], channel_multiplier=1), False)
            setup(pool.affine_select(out=eye_blocks[:, :], in_=eye_blocks[:, :], compare_op=ALU.not_equal, fill=1.0,
                                     base=0, pattern=[[1, SB], [-1, SB]], channel_multiplier=0))

            def deviations(count):
                pool.tensor_scalar(rstd[:, :], mean_var[:, :, 1], 1.0, EPS_LN, ALU.mult, ALU.add).then_inc(S["ln_eps"], 1)
                pool.wait_ge(S["ln_eps"], START + count)
                pool.tensor_tensor(rstd[:, :], rstd[:, :], minus_half[:, 0:NC], ALU.pow).then_inc(S["ln_rstd"], 1)

            def head(a):
                n = a.n
                wait_apart(pool, S["conv_tap"], START + n * 12)
                pool.tensor_copy(cwp[:, :, :], conv_par[:, bass.ds(a.k, 1), :, :].rearrange("p a t w -> p (a t) w")
                                 ).then_inc(S["a_in"], 1)
                wait_apart(pool, S["gm_ready"], START + n * NU)
                pool.tensor_copy(g_item[:, :, :], table[:, G_, :, bass.ds(2 * a.k, 2)]).then_inc(S["a_in"], 1)
                pool.tensor_copy(raw[:, :, 0:TAIL], tails[:, bass.ds(a.k, 1), :, :].rearrange("p a t w -> p (a t) w")
                                 ).then_inc(S["a_in"], 1)

            def masked_g(a):
                n = a.n
                wait_apart(pool, S["a_in"], START + n * 3 + 3)
                wait_apart(pool, S["d_done"], START + n * 2)
                for h in range(2):
                    for c in range(NC):
                        pool.tensor_scalar(gm[:, unit(h, c), :], mask_incl[:, :], g_item[:, c, h:h + 1], 1.0,
                                           ALU.mult, ALU.mult).then_inc(S["gm_ready"], 1)

            def save_tail(a):
                wait_apart(pool, S["raw_in"], START + a.n * 4 + 4)
                pool.tensor_copy(tails[:, bass.ds(a.k, 1), :, :].rearrange("p a t w -> p (a t) w"),
                                 raw[:, :, TOK:TOK + TAIL]).then_inc(S["tail_saved"], 1)

            def A(a):
                head(a)
                masked_g(a)
                save_tail(a)

            def B(s):
                n, p = s.n, s.p
                wait_apart(pool, S["y_done"], START + n * NC)
                base = n * SCALAR_OPS
                pool.tensor_copy(sc[p][:, :, :, :], table[:, :, :, bass.ds(2 * s.k, 2)]).then_inc(S["scal_step"], 1)
                wait_apart(pool, S["ssk_ready"], START + n * NC + NC)
                pool.tensor_scalar(ss[:, NC:2 * NC], ssk[:, :], 1.0, 4 * EPS_NORM, ALU.mult, ALU.add).then_inc(S["scal_step"], 1)
                pool.wait_ge(S["scal_step"], START + base + 2)
                pool.wait_ge(S["ss_ready"], START + n + 1)
                rk = rs[:, NC:2 * NC]
                pool.tensor_tensor(rs[:, :], ss[:, :], minus_half[:, :], ALU.pow).then_inc(S["scal_step"], 1)
                wait_apart(pool, S["scal_step"], START + base + 3)
                pool.tensor_scalar(sca[p][:, RQ:RQ + NC], rs[:, 0:NC], float(P) ** -0.5, 1.0, ALU.mult, ALU.mult
                                   ).then_inc(S["scal_step"], 1)
                pool.tensor_tensor(rk2[:, 0:NC], ss[:, NC:2 * NC], rk, ALU.mult).then_inc(S["scal_step"], 1)
                pool.tensor_scalar(rk2[:, NC:2 * NC], rk, -1.0, 1.0, ALU.mult, ALU.mult).then_inc(S["scal_step"], 1)
                wait_apart(pool, S["scal_step"], START + base + 6)
                pool.tensor_scalar(sca[p][:, NK:NK + NC], rk2[:, 0:NC], 0.5, 1.0, ALU.mult, ALU.mult
                                   ).then_inc(S["scal_step"], 1)
                pool.tensor_tensor(rk2[:, 2 * NC:3 * NC], rk2[:, NC:2 * NC], rk, ALU.mult).then_inc(S["scal_step"], 1)
                wait_apart(pool, S["scal_step"], START + base + 8)
                for h in range(2):
                    pool.tensor_tensor(sca[p][:, NAA + h * NC:NAA + (h + 1) * NC], rk2[:, 2 * NC:3 * NC],
                                       sc[p][:, BETA, :, h], ALU.mult).then_inc(S["sc_ready"], 1)
                    pool.tensor_tensor(sca[p][:, EGQ + h * NC:EGQ + (h + 1) * NC], sca[p][:, RQ:RQ + NC],
                                       sc[p][:, EXP_G, :, h], ALU.mult).then_inc(S["sc_ready"], 1)
                wait_apart(pool, S["ktok_ready"], START + n + 1)
                for h in range(2):
                    for c in range(NC):
                        pool.tensor_scalar(k2[p][:, unit(h, c), :], ktok[:, c, :], sc[p][:, EXP_REST, c, h:h + 1], 1.0,
                                           ALU.mult, ALU.mult).then_inc(S["k2_ready"], 1)

            def load_state(c):
                wait_apart(pool, S["s_store"], START + c.n)
                pool.tensor_copy(sw[c.p][:, :], states[:, bass.ds(c.k, 1), :].rearrange("p a n -> p (a n)")
                                 ).then_inc(S["s_load"], 1)

            def store_state(c):
                wait_apart(pool, S["s_upd"], START + c.n * NU + NU)
                pool.tensor_copy(states[:, bass.ds(c.k, 1), :].rearrange("p a n -> p (a n)"), sw[c.p][:, :]
                                 ).then_inc(S["s_store"], 1)

            def gates(c, i):
                n = c.n
                wait_apart(pool, S["z_ready"], START + n * 2 + i + 1)
                wait_apart(pool, S["gt_ready"], START + n * NU)
                pool.tensor_scalar(sg[:, 2 * i:2 * i + 2, :], thz[:, :, :], 0.5, 0.5, ALU.mult, ALU.add
                                   ).then_inc(S["sg_ready"], 1)

            def step(c, j):
                n = c.n
                wait_apart(pool, S["sg_ready"], START + n * 2 + j // 2 + 1)
                wait_apart(pool, S["gtr_done"], START + n * NC + j)
                pool.wait_ge(S["o_ready"], START + n * NC + j + 1)
                pool.tensor_tensor(gt[:, :, :].rearrange("p h i -> p (h i)"), ob[:, j % 2, :], sg[:, j, :], ALU.mult
                                   ).then_inc(S["og_ready"], 1)
                wait_apart(pool, S["sq_acc"], START + n * NU + 2 * j + 2)
                pool.tensor_scalar(ssq[:, j % 2, :], ssq[:, j % 2, :], 1.0 / P, EPS_NORM, ALU.mult, ALU.add
                                   ).then_inc(S["rr_eps"], 1)
                pool.wait_ge(S["rr_eps"], START + n * NC + j + 1)
                pool.tensor_tensor(rr[:, j % 2, :], ssq[:, j % 2, :], minus_half[:, 0:2], ALU.pow
                                   ).then_inc(S["rr_ready"], 1)
                wait_apart(pool, S["og_ready"], START + n * NC + j + 1)
                wait_apart(pool, S["rr_ready"], START + n * NC + j + 1)
                for h in range(2):
                    pool.tensor_scalar(gt[:, h, :], gt[:, h, :], rr[:, j % 2, h:h + 1], 1.0, ALU.mult, ALU.mult
                                       ).then_inc(S["gt_ready"], 1)

            def slot(s, c, a):
                if c is not None:
                    load_state(c)
                if s is not None:
                    B(s)
                if a is not None:
                    head(a)
                if s is not None:
                    wait_apart(pool, S["tb_out"], START + s.n * 32)
                    pool.tensor_copy(tinv[:, :], eye_blocks[:, :]).then_inc(S["tb_init"], 1)
                if a is not None:
                    masked_g(a)
                if c is not None:
                    gates(c, 1)
                    for j in range(NC):
                        step(c, j)
                if a is not None:
                    save_tail(a)
                if c is not None:
                    store_state(c)
                if s is not None:
                    gates(s, 0)

            def batch_start(b):
                wait_apart(pool, S["s_store"], START + b * (TILES_PER_BATCH * KH))
                pool.memset(states[:, :, :], 0.0).then_inc(S["zeroed"], 1)
                pool.memset(tails[:, :, :, :], 0.0).then_inc(S["zeroed"], 1)
                wait_apart(pool, S["zeroed"], START + b * 2 + 2)

            def tile(t, b, m0):
                pool.wait_ge(S["dve_setup"], DVE_SETUP)
                pool.wait_ge(S["ht_ready"], START + t * 4)
                wait_apart(pool, S["out_ready"], START + t * 2)
                pool.tensor_copy(mod_b[:, :, :], mod_t[:, :, :, bass.ds(b, 1)].rearrange("p v k a -> p v (k a)")
                                 ).then_inc(S["mod_copied"], 1)
                pool.tensor_copy(gate_b[:, :, :], gate_rows[:, bass.ds(b, 1), :, :].rearrange("p a g d -> p (a g) d")
                                 ).then_inc(S["mod_copied"], 1)
                wait_apart(pool, S["ln_stats"], START + t * 16 + 8)
                deviations(t * 2 + 1)
                wait_apart(pool, S["thb_ready"], START + t + 1)
                pool.tensor_scalar(table[:, BETA, :, :], th_b[:, :, :], 0.5, 0.5, ALU.mult, ALU.add).then_inc(S["beta_ready"], 1)
                pool.wait_ge(S["beta_ready"], START + t + 1)
                pool.wait_ge(S["g_ready"], START + t + 1)
                pool.wait_ge(S["exp_ready"], START + t + 1)
                wait_apart(pool, S["out_stored"], START + t * 16)
                slots(pool, m0, A, slot)
                wait_apart(pool, S["ln_stats"], START + t * 16 + 16)
                deviations(t * 2 + 2)

            tile_loop(pool, tile, batch_start)

        @block.scalar
        def _(act):
            act.wait_ge(S["in_cond"], 32)
            act.activation(cond_th[:, :, :], cond_t[:, :, :], ACT.Tanh, scale=0.5).then_inc(S["act_setup"], 1)
            act.wait_ge(S["in_small"], 16 * 5)
            act.activation(neg_exp_a[:, :], neg_exp_a[:, :], ACT.Exp).then_inc(S["act_setup"], 1)

            def evacuate(a, i):
                n = a.n
                act.wait_ge(S["proj_done"], START + n * 4 + i + 1)
                if i == 0:
                    act.wait_ge(S["a_in"], START + n * 3 + 3)
                    act.wait_ge(S["silu_done"], START + n * 4)
                    act.wait_ge(S["tail_saved"], START + n)
                act.activation(raw[:, i, TAIL:TAIL + TOK], PB[i % 2][:, :], ACT.Copy).then_inc(S["raw_in"], 1)
                act.activation(cv[:, i, :], PB[i % 2][:, :], ACT.Identity, bias=cwp[:, i, 4:5], scale=cwp[:, i, 0:1]
                               ).then_inc(S["conv_in"], 1)

            def decay(a, h):
                act.wait_ge(S["d_done"], START + a.n * 2 + h + 1)
                act.wait_ge(S["pt_ready"], START + a.n * 2)
                act.activation(dec[:, h * NC:(h + 1) * NC, :], PB[h][:, :].rearrange("p (c i) -> p c i", c=NC), ACT.Exp
                               ).then_inc(S["d_ready"], 1)

            def tanh(a, i):
                act.wait_ge(S["conv_tap"], START + a.n * 12 + 3 * i + 3)
                act.wait_ge(S["silu_done"], START + a.n * 4)
                act.activation(th[:, i, :], cv[:, i, :], ACT.Tanh, scale=0.5).then_inc(S["th_ready"], 1)

            def A(a):
                for i in range(4):
                    evacuate(a, i)
                for h in range(2):
                    decay(a, h)
                for i in range(3):
                    tanh(a, i)

            def k_rows(s):
                n, p = s.n, s.p
                act.wait_ge(S["norms_done"], START + n)
                act.wait_ge(S["silu_done"], START + n * 4 + 1)
                act.activation(sq[:, 0, :], qt[p][:, :], ACT.Square).then_inc(S["sq_ready"], 1)
                act.wait_ge(S["kt_done"], START + n + 1)
                act.wait_ge(S["k2_ready"], START + n * NU)
                act.activation(ktok[:, :, :], PB[1][:, :].rearrange("p (c i) -> p c i", c=NC), ACT.Copy
                               ).then_inc(S["ktok_ready"], 1)
                act.wait_ge(S["ktok_ready"], START + n + 1)
                act.wait_ge(S["scal_step"], START + n * SCALAR_OPS)
                for c in range(NC):
                    act.activation(junk, ktok[:, c, :].rearrange("p (a b) -> p a b", a=NC), ACT.Square,
                                   accum_out=ssk[:, c:c + 1]).then_inc(S["ssk_ready"], 1)
                    act.wait_ge(S["ssk_ready"], START + n * NC + c + 1)

            def v_rows(s, h):
                n, p = s.n, s.p
                act.wait_ge(S["y_done"], START + n * NC)
                act.wait_ge(S["sc_ready"], START + n * 4 + 4)
                act.wait_ge(S["v_tr"], START + n * 2 + h + 1)
                for c in range(NC):
                    act.activation(vs[p][:, unit(h, c), :], PB[h][:, c * P:(c + 1) * P], ACT.Copy,
                                   scale=sca[p][:, NK + c:NK + c + 1]).then_inc(S["vs_ready"], 1)

            def flush(c, j):
                n = c.n
                act.wait_ge(S["gtr_done"], START + n * NC + j + 1)
                act.wait_ge(S["y_done"], START + n * NC + j + NC)
                act.activation(got[:, :, :], R[3][:, 0:2 * P].rearrange("p (h i) -> p h i", h=2), ACT.Copy,
                               scale=gamma_c[:, 0:1]).then_inc(S["got_ready"], 1)

            def gates(c, i):
                n = c.n
                act.wait_ge(S["z_done"], START + n * 2 + i + 1)
                act.wait_ge(S["sg_ready"], START + n * 2 + i)
                act.activation(thz[:, :, :], R[2 + i][:, :].rearrange("p (j i) -> p j i", j=2), ACT.Tanh, scale=0.5
                               ).then_inc(S["z_ready"], 1)

            def slot(s, c, a):
                if s is not None:
                    k_rows(s)
                if c is not None:
                    n, p = c.n, c.p
                    act.wait_ge(S["t32_ready"], START + n + 1)
                    act.wait_ge(S["q2_done"], START + n)
                    for b in range(2):
                        act.activation(t64[b * BL:(b + 1) * BL, :, b * BL:(b + 1) * BL], t32[b * BL:(b + 1) * BL, :, :],
                                       ACT.Copy).then_inc(S["t64_diag"], 1)
                    act.wait_ge(S["w_done"], START + n * NC)
                    for b in range(NBL):
                        blk = slice(b * BL, (b + 1) * BL)
                        act.activation(minv[blk, :, blk], R[2][blk, 0:NU * BL].rearrange("p (u i) -> p u i", u=NU), ACT.Copy
                                       ).then_inc(S["mdiag"], 1)
                    act.wait_ge(S["q1_done"], START + n + 1)
                    act.activation(q1s[:, :, :], R[0][:, 0:NU * BL].rearrange("p (u i) -> p u i", u=NU), ACT.Copy
                                   ).then_inc(S["q1_ready"], 1)
                if s is not None:
                    tanh(s, 3)
                if c is not None:
                    act.wait_ge(S["m12_done"], START + n + 1)
                    act.wait_ge(S["mdiag"], START + n * NBL + NBL)
                    for b in range(2):
                        lo, mid = 64 * b, 64 * b + BL
                        act.activation(minv[lo:mid, :, mid:mid + BL],
                                       R[1][lo:mid, 0:NU * BL].rearrange("p (u i) -> p u i", u=NU), ACT.Copy
                                       ).then_inc(S["m12_ready"], 1)
                if s is not None:
                    v_rows(s, 0)
                if c is not None:
                    gates(c, 1)
                    act.wait_ge(S["m2_done"], START + n + 1)
                    act.activation(minv[0:64, :, 64:P], R[1][0:64, :].rearrange("p (u i) -> p u i", u=NU), ACT.Copy
                                   ).then_inc(S["minv_ready"], 1)
                if s is not None:
                    v_rows(s, 1)
                for j in range(NC):
                    if c is not None:
                        act.wait_ge(S["qs_done"], START + n * NC + j + 1 + NC)
                        act.wait_ge(S["o_ready"], START + n * NC + j)
                        for h in range(2):
                            e = EGQ + h * NC + j
                            act.activation(tmpq[:, h, :], R[1][:, h * P:(h + 1) * P], ACT.Copy, scale=sca[p][:, e:e + 1]
                                           ).then_inc(S["tq_ready"], 1)
                    if a is not None and j == 3:
                        tanh(a, 0)
                    if c is not None:
                        act.wait_ge(S["w_done"], START + n * NC + j + 1)
                        act.wait_ge(S["pu_done"], START + n * NC + j)
                        for h in range(2):
                            e = NAA + h * NC + j
                            act.activation(us[:, h, :], R[2][:, (2 + h) * P:(3 + h) * P], ACT.Copy, scale=sca[p][:, e:e + 1]
                                           ).then_inc(S["u_ready"], 1)
                        if j > 1:
                            flush(c, j - 2)
                        if a is not None and j > 0:
                            evacuate(a, j - 1)
                        act.wait_ge(S["o_ready"], START + n * NC + j + 1)
                        for h in range(2):
                            act.activation(junk, ob[:, j % 2, h * P:(h + 1) * P].rearrange("p (a b) -> p a b", a=NC),
                                           ACT.Square, accum_out=ssq[:, j % 2, h:h + 1]).then_inc(S["sq_acc"], 1)
                            act.wait_ge(S["sq_acc"], START + n * NU + 2 * j + h + 1)
                    elif a is not None and j > 0:
                        evacuate(a, j - 1)
                if c is not None:
                    flush(c, NC - 2)
                if a is not None:
                    evacuate(a, NC - 1)
                    for h in range(2):
                        decay(a, h)
                    tanh(a, 1)
                if c is not None:
                    flush(c, NC - 1)
                if s is not None:
                    gates(s, 0)
                if a is not None:
                    tanh(a, 2)

            def modulate(count, mods, v):
                act.wait_ge(S["mod_copied"], START + mods)
                for k in range(KD):
                    act.wait_ge(S["ht_psum"], START + count + k + 1)
                    act.activation(ht[:, k, :], R[k][:, :], ACT.Identity, bias=mod_b[:, v, k:k + 1],
                                   scale=mod_b[:, v + 1, k:k + 1]).then_inc(S["ht_ready"], 1)

            def tile(t, b, m0):
                modulate(t * 4, t * 2 + 2, 0)
                act.wait_ge(S["au_ready"], START + t + 1)
                act.activation(th_b[:, :, :], R[2][:, 0:NC * 2 * VH].rearrange("p (c h) -> p c h", c=NC)[:, :, 0:VH], ACT.Tanh,
                               scale=0.5).then_inc(S["thb_ready"], 1)
                act.activation(a_abs[:, :, :], au[:, :, :], ACT.Abs).then_inc(S["abs_ready"], 1)
                act.wait_ge(S["abs_ready"], START + t + 1)
                act.activation(a_exp[:, :, :], a_abs[:, :, :], ACT.Exp, scale=-1.0).then_inc(S["aexp_ready"], 1)
                act.wait_ge(S["aexp_ready"], START + t + 1)
                act.activation(a_ln[:, :, :], a_exp[:, :, :], ACT.Ln, bias=ones[:, 0:1]).then_inc(S["aln_ready"], 1)
                act.wait_ge(S["cum_done"], START + t + 1)
                act.activation(table[:, EXP_G:EXP_ALL + 1, :, :].rearrange("p e c h -> p (e c h)"), R[3][:, 0:3 * NC * VH],
                               ACT.Exp).then_inc(S["exp_ready"], 1)
                act.wait_ge(S["out_stored"], START + t * 16)
                slots(act, m0, A, slot)
                modulate(t * 4 + 2, t * 2 + 2, 2)
                for i in range(NI):
                    bank = PB[0] if i % 2 == 0 else R[2]
                    act.wait_ge(S["gate_done"], START + t * NI + i + 1)
                    if i >= 2:
                        act.wait_ge(S["ff_half"], START + t * NI + i - 1)
                    else:
                        act.wait_ge(S["ff_half"], START + t * NI)
                    act.activation(ff_th[:, i % 2, :], bank[:, :], ACT.Tanh, scale=0.5).then_inc(S["th_ff"], 1)
                act.wait_ge(S["out_ready"], START + t * 2 + 2)
                by_tile = out.rearrange("b (t c p) d -> (b t) p c d", c=NC, p=P)
                act.dma_start(by_tile[bass.ds(t, 1), :, :, :].rearrange("a p c d -> p (a c) d"), y_tmp[:, :, :]
                              ).then_inc(S["out_stored"], 16)

            tile_loop(act, tile)

        @block.vector
        def _(dve):
            step = [0]

            def setup(ins, wait=False):
                step[0] += 1
                ins.then_inc(S["dve_setup"], 1)
                if wait:
                    dve.wait_ge(S["dve_setup"], step[0])

            for r in R:
                setup(dve.memset(r[:, :], 0.0))
            dve.wait_ge(S["act_setup"], 2)
            setup(dve.tensor_scalar(neg_exp_a[:, :], neg_exp_a[:, :], -1.0, None, ALU.mult))
            setup(dve.scalar_tensor_tensor(out=cond_silu[:, :, :], in0=cond_th[:, :, :], scalar=1.0, in1=cond_t[:, :, :],
                                           op0=ALU.add, op1=ALU.mult), True)
            setup(dve.tensor_scalar(cond_silu[:, :, :], cond_silu[:, :, :], 0.5, None, ALU.mult), True)
            dve.wait_ge(S["pool_setup"], POOL_SETUP)
            cond_rows = hn[:, :, :].rearrange("p a (b i) -> p (a b) i", i=P)
            for k in range(KD):
                for b in range(BATCH):
                    setup(dve.tensor_scalar(cond_rows[:, k * BATCH + b, :], ones[:, :], cond_silu[:, k, b:b + 1], None,
                                            ALU.mult))
            dve.wait_ge(S["pe_setup"], 1)
            cols = R[0][:, 0:5 * 64].rearrange("p (w t) -> p w t", w=5)
            for i in range(2):
                setup(dve.tensor_copy(conv_par[:, :, i, :].rearrange("p k w -> p w k"), cols[:, :, i * KH:(i + 1) * KH]))
            for j in range(2):
                v = cols[:, :, 2 * KH:4 * KH].rearrange("p w (k j) -> p w k j", j=2)
                setup(dve.tensor_copy(conv_par[:, :, 2 + j, :].rearrange("p k w -> p w k"), v[:, :, :, j]))
            dve.wait_ge(S["pe_setup"], 2)
            setup(dve.tensor_copy(mod_t[:, :, :, :].rearrange("p v k b -> p (v k b)"), R[1][:, 0:4 * KD * BATCH]), True)
            for v in (1, 3):
                setup(dve.tensor_scalar(mod_t[:, v, :, :], mod_t[:, v, :, :], 1.0, None, ALU.add))
            for b, bank in enumerate((R[2], R[3], PB[0], PB[1])):
                row = bank[:, :].rearrange("p (g d) -> p g d", g=2)
                sign = vt[:, 0, :].rearrange("p (g d) -> p g d", g=2)
                setup(dve.tensor_scalar(sign, row, 0.0, 2.0, ALU.is_ge, ALU.mult), True)
                setup(dve.tensor_scalar(sign, sign, -1.0, None, ALU.add), True)
                setup(dve.tensor_tensor(gate_rows[:, b, :, :], row, sign, ALU.mult), True)
                setup(dve.scalar_tensor_tensor(out=gate_rows[:, b, :, :], in0=gate_rows[:, b, :, :], scalar=GATE_MIN,
                                               in1=sign, op0=ALU.max, op1=ALU.mult), True)
            setup(dve.tensor_reduce(out=ident_bl[:, :], in_=ident[:, :].rearrange("p (b c) -> p c b", c=BL), op=ALU.add,
                                    axis=mybir.AxisListType.X), True)
            setup(dve.tensor_copy(q0s[:, :, :], ident_bl[:, :].unsqueeze(1).to_broadcast([P, NU, BL])))
            setup(dve.tensor_reduce(out=second_half[:, :], in_=ident_bl[:, SB:BL], op=ALU.add, axis=mybir.AxisListType.X))
            for n in range(MLP_BATCHES):
                dve.wait_ge(S["pe_setup"], 3 + n)
                if n < 8:
                    k, o = n // 4, n % 4
                    dst = wgu_t[:, k, o * 512:(o + 1) * 512]
                else:
                    dst = wd_t[:, 2 * (n - 8):2 * (n - 8) + 2, :].rearrange("p i d -> p (i d)")
                setup(dve.tensor_copy(dst, R[n % 4][:, :]))
            assert step[0] == DVE_SETUP

            def taps(a, lo, hi):
                n = a.n
                for step in range(lo, hi):
                    i, j = step // TAIL, step % TAIL + 1
                    if j == 1:
                        dve.wait_ge(S["raw_in"], START + n * 4 + i + 1)
                        dve.wait_ge(S["conv_in"], START + n * 4 + i + 1)
                    else:
                        dve.wait_ge(S["conv_tap"], START + n * 12 + step)
                    dve.scalar_tensor_tensor(out=cv[:, i, :], in0=raw[:, i, TAIL - j:TAIL - j + TOK],
                                             scalar=cwp[:, i, j:j + 1], in1=cv[:, i, :], op0=ALU.mult, op1=ALU.add
                                             ).then_inc(S["conv_tap"], 1)

            def A(a):
                taps(a, 0, 9)

            def silu(s, i):
                n, p = s.n, s.p
                if i < 2:
                    dve.wait_ge(S["qs_done"], START + n * NC)
                else:
                    dve.wait_ge(S["v_tr"], START + n * 2)
                dst = (qt[p][:, :], kt[p][:, :], vt[:, 0, :], vt[:, 1, :])[i]
                dve.wait_ge(S["th_ready"], START + n * 4 + i + 1)
                dve.scalar_tensor_tensor(out=dst, in0=th[:, i, :], scalar=1.0, in1=cv[:, i, :],
                                         op0=ALU.add, op1=ALU.mult).then_inc(S["silu_done"], 1)

            def mask_kk(s):
                n = s.n
                dve.wait_ge(S["kk_done"], START + n + 1)
                dve.tensor_tensor(kkm[:, :, :], PB[0][:, :].rearrange("p (c i) -> p c i", c=NC),
                                  mask_strict[:, :].unsqueeze(1).to_broadcast([P, NC, C]), ALU.mult).then_inc(S["kkm_ready"], 1)

            def mask_kq(s):
                n = s.n
                dve.wait_ge(S["kq_done"], START + n + 1)
                dve.tensor_tensor(kqm[:, :, :], PB[1][:, :].rearrange("p (c i) -> p c i", c=NC),
                                  mask_incl[:, :].unsqueeze(1).to_broadcast([P, NC, C]), ALU.mult).then_inc(S["kqm_ready"], 1)

            def norms(s):
                dve.wait_ge(S["norms_done"], START + s.n + 1)
                dve.tensor_scalar(ss[:, 0:NC], PB[0][:, 0:NC], 4 * EPS_NORM, None, ALU.add).then_inc(S["ss_ready"], 1)

            def systems(s, h):
                n, p = s.n, s.p
                if h == 0:
                    dve.wait_ge(S["y_done"], START + n * NC)
                    dve.wait_ge(S["d_ready"], START + n * 2 + 2)
                    dve.wait_ge(S["sc_ready"], START + n * 4 + 4)
                    dve.wait_ge(S["kkm_ready"], START + n + 1)
                for c in range(NC):
                    u, e = unit(h, c), NAA + h * NC + c
                    dve.scalar_tensor_tensor(out=lt[p][:, u, :], in0=kkm[:, c, :], scalar=sca[p][:, e:e + 1],
                                             in1=dec[:, u, :], op0=ALU.mult, op1=ALU.mult).then_inc(S["lt_ready"], 1)

            def products(s):
                n, p = s.n, s.p
                dve.wait_ge(S["kqm_ready"], START + n + 1)
                for h in range(2):
                    us_ = slice(h * NC, (h + 1) * NC)
                    dve.tensor_tensor(pt[p][:, us_, :], kqm[:, :, :], dec[:, us_, :], ALU.mult).then_inc(S["pt_ready"], 1)

            def solve(s, j0, j1):
                base = s.n * SOLVE_OPS
                if j0 == 0:
                    dve.wait_ge(S["lb_in"], START + s.n * 32 + 32)
                    dve.wait_ge(S["tb_init"], START + s.n + 1)
                for j in range(j0, j1):
                    rows, cols = SB - 1 - j, j + 1
                    if j > 0:
                        dve.wait_ge(S["solve_step"], START + base + 2 * j)
                    coef = blocks[:, j * SB + j + 1:(j + 1) * SB].unsqueeze(2).to_broadcast([NU * NSB, rows, cols])
                    row = tinv[:, j * SB:j * SB + cols].unsqueeze(1).to_broadcast([NU * NSB, rows, cols])
                    prod = solve_tmp[:, 0:rows * cols].rearrange("p (i c) -> p i c", c=cols)
                    dve.tensor_tensor(prod, coef, row, ALU.mult).then_inc(S["solve_step"], 1)
                    dve.wait_ge(S["solve_step"], START + base + 2 * j + 1)
                    rest = tinv[:, (j + 1) * SB:].rearrange("p (i c) -> p i c", c=SB)[:, :, 0:cols]
                    dve.tensor_tensor(rest, rest, prod, ALU.add).then_inc(S["solve_step"], 1)

            def slot(s, c, a):
                if s is not None:
                    silu(s, 0)
                    silu(s, 1)
                if c is not None:
                    n, p = c.n, c.p
                    dve.wait_ge(S["t16_in"], START + n * 16 + 16)
                    dve.wait_ge(S["mdiag_done"], START + n)
                    dve.transpose(t16_t[:, :, :].rearrange("p u i -> p (u i)"), t16[:, :, :].rearrange("p u i -> p (u i)")
                                  ).then_inc(S["t16t_ready"], 1)
                    dve.wait_ge(S["q0_done"], START + n + 1)
                    dve.scalar_tensor_tensor(out=q0s[:, :, 0:SB], in0=R[0][:, 0:NU * BL].rearrange(
                        "p (u i) -> p u i", u=NU)[:, :, 0:SB], scalar=second_half[:, 0:1],
                        in1=ident_bl[:, 0:SB].unsqueeze(1).to_broadcast([P, NU, SB]), op0=ALU.mult, op1=ALU.add
                        ).then_inc(S["q0_ready"], 1)
                if s is not None:
                    mask_kk(s)
                if c is not None:
                    dve.wait_ge(S["mdiag_done"], START + n + 1)
                    dve.wait_ge(S["q1_done"], START + n)
                    dve.wait_ge(S["t64_diag"], START + n * 2)
                    dve.transpose(t32[:, :, :].rearrange("p u i -> p (u i)"), R[2][:, 0:NU * BL]).then_inc(S["t32_ready"], 1)
                if s is not None:
                    mask_kq(s)
                    norms(s)
                    silu(s, 2)
                    taps(s, 9, 11)
                if c is not None:
                    dve.wait_ge(S["t21_done"], START + n + 1)
                    dve.tensor_copy(t64[BL:64, :, 0:BL], R[2][BL:64, 0:NU * BL].rearrange("p (u i) -> p u i", u=NU)
                                    ).then_inc(S["t21_ready"], 1)
                if s is not None:
                    taps(s, 11, 12)
                if c is not None:
                    dve.wait_ge(S["q2_done"], START + n + 1)
                    dve.tensor_copy(q2s[64:P, :, :], R[0][64:P, :].rearrange("p (u i) -> p u i", u=NU)
                                    ).then_inc(S["q2_ready"], 1)
                if s is not None:
                    silu(s, 3)
                    systems(s, 0)
                    systems(s, 1)
                for j in range(NC):
                    if c is not None:
                        dve.wait_ge(S["ks_done"], START + n * NC + j + 1)
                        dve.wait_ge(S["vs_ready"], START + n * NU + NU)
                        dve.wait_ge(S["w_done"], START + n * NC + j)
                        for h in range(2):
                            dve.scalar_tensor_tensor(out=rn[:, h, :], in0=R[0][:, h * P:(h + 1) * P],
                                                     scalar=sc[p][:, EXP_G, j, h:h + 1], in1=vs[p][:, unit(h, j), :],
                                                     op0=ALU.mult, op1=ALU.subtract).then_inc(S["r_ready"], 1)
                    if s is not None and j == 0:
                        products(s)
                    if s is not None and j > 0:
                        solve(s, *((0, 4), (4, 8), (8, SB - 1))[j - 1])
                    if a is not None and j == 2:
                        taps(a, 1, 2)
                    if c is not None:
                        dve.wait_ge(S["su_done"], START + n * NC + j + 1)
                        for h in range(2):
                            dve.scalar_tensor_tensor(out=sw[p][:, h * P:(h + 1) * P], in0=sw[p][:, h * P:(h + 1) * P],
                                                     scalar=sc[p][:, EXP_ALL, j, h:h + 1], in1=R[2][:, h * P:(h + 1) * P],
                                                     op0=ALU.mult, op1=ALU.add).then_inc(S["s_upd"], 1)
                        dve.wait_ge(S["pu_done"], START + n * NC + j + 1)
                        dve.wait_ge(S["tq_ready"], START + n * NU + 2 * j + 2)
                        dve.wait_ge(S["gt_ready"], START + n * NU + 2 * max(j - 1, 0))
                        dve.scalar_tensor_tensor(out=ob[:, j % 2, :], in0=R[1][:, 2 * P:4 * P],
                                                 scalar=sca[p][:, RQ + j:RQ + j + 1],
                                                 in1=tmpq[:, :, :].rearrange("p h i -> p (h i)"), op0=ALU.mult, op1=ALU.add
                                                 ).then_inc(S["o_ready"], 1)
                    if a is not None and j in (1, 2):
                        taps(a, *((0, 1), (2, 3))[j - 1])
                if a is not None:
                    taps(a, 3, 9)

            def layernorm(src, t, second):
                base = t * 16 + 8 * second
                for c in range(NC):
                    dve.bn_stats(stats[:, c, :], src[:, c, :]).then_inc(S["ln_stats"], 1)
                wait_apart(dve, S["ln_stats"], START + base + 4)
                for c in range(NC):
                    dve.bn_aggr(mean_var[:, c, :], stats[:, c, :]).then_inc(S["ln_stats"], 1)
                dve.wait_ge(S["ln_stats"], START + base + 8)
                dve.wait_ge(S["ln_rstd"], START + t * 2 + second + 1)
                for c in range(NC):
                    dve.tensor_scalar(hn[:, c, :], src[:, c, :], mean_var[:, c, 0:1], rstd[:, c:c + 1], ALU.subtract, ALU.mult
                                      ).then_inc(S["hn_ready"], 1)

            def gated_add(dst, src, banks, gate, half_sem, done_sem, base):
                for i in range(2):
                    dve.tensor_tensor(y_tmp[:, 2 * i:2 * i + 2, :], banks[i][:, :].rearrange("p (c d) -> p c d", c=2),
                                      gate_b[:, gate, :].unsqueeze(1).to_broadcast([P, 2, D]), ALU.mult).then_inc(half_sem, 1)
                    dve.wait_ge(half_sem, START + base + i + 1)
                    dve.tensor_tensor(dst[:, 2 * i:2 * i + 2, :], y_tmp[:, 2 * i:2 * i + 2, :], src[:, 2 * i:2 * i + 2, :],
                                      ALU.add).then_inc(done_sem, 1)

            def tile(t, b, m0):
                n_end = (m0 + KH // 2) * 2
                dve.wait_ge(S["x_in"], START + t * 16 + 16)
                layernorm(xt, t, 0)
                dve.wait_ge(S["ba_done"], START + t + 1)
                dve.tensor_tensor(au[:, :, :], R[2][:, 0:NC * 2 * VH].rearrange("p (c h) -> p c h", c=NC)[:, :, VH:2 * VH],
                                  dt_b[:, :].unsqueeze(1).to_broadcast([P, NC, VH]), ALU.add).then_inc(S["au_ready"], 1)
                dve.wait_ge(S["aln_ready"], START + t + 1)
                dve.wait_ge(S["au_ready"], START + t + 1)
                dve.scalar_tensor_tensor(out=au[:, :, :], in0=au[:, :, :], scalar=0.0, in1=a_ln[:, :, :],
                                         op0=ALU.max, op1=ALU.add).then_inc(S["g_mul"], 1)
                dve.wait_ge(S["g_mul"], START + t + 1)
                dve.tensor_tensor(table[:, G_, :, :], au[:, :, :], neg_exp_a[:, :].unsqueeze(1).to_broadcast([P, NC, VH]),
                                  ALU.mult).then_inc(S["g_ready"], 1)
                slots(dve, m0, A, slot)
                dve.wait_ge(S["y_done"], START + n_end * NC + NC)
                dve.wait_ge(S["out_stored"], START + t * 16)
                dve.wait_ge(S["mod_copied"], START + t * 2 + 2)
                gated_add(x1, xt, Y, 0, S["x1_half"], S["x1_ready"], t * 2)
                dve.wait_ge(S["x1_ready"], START + t * 2 + 2)
                layernorm(x1, t, 1)
                for i in range(NI):
                    gate, up = (PB[0], PB[1]) if i % 2 == 0 else (R[2], R[3])
                    dve.wait_ge(S["th_ff"], START + t * NI + i + 1)
                    dve.wait_ge(S["ff_ready"], START + t * NI + max(i - 1, 0))
                    dve.scalar_tensor_tensor(out=ff_g[:, i % 2, :], in0=ff_th[:, i % 2, :], scalar=1.0, in1=gate[:, :],
                                             op0=ALU.add, op1=ALU.mult).then_inc(S["ff_half"], 1)
                    dve.wait_ge(S["ff_half"], START + t * NI + i + 1)
                    dve.wait_ge(S["up_done"], START + t * NI + i + 1)
                    dve.scalar_tensor_tensor(out=ff[:, i, :], in0=ff_g[:, i % 2, :], scalar=0.5, in1=up[:, :],
                                             op0=ALU.mult, op1=ALU.mult).then_inc(S["ff_ready"], 1)
                dve.wait_ge(S["down_done"], START + t * 2 + 2)
                gated_add(y_tmp, x1, R, 1, S["down_half"], S["out_ready"], t * 2)

            tile_loop(dve, tile)

        @block.tensor
        def _(pe):
            mm = pe.matmul

            pe.wait_ge(S["pool_setup"], POOL_SETUP)
            pe.wait_ge(S["in_conv"], 32)
            pe.wait_ge(S["dve_setup"], 4)
            taps_rows = x1[0:64, 0:2, :].rearrange("t a b -> t (a b)").rearrange("t (c w) -> t c w", w=CONV_K)
            for w in range(CONV_K):
                pe.transpose(R[0][:, w * 64:(w + 1) * 64], taps_rows[:, :, w], ident[0:64, 0:64])
            pe.transpose(R[0][:, 4 * 64:5 * 64], x1[0:64, 2, 0:P], ident[0:64, 0:64]).then_inc(S["pe_setup"], 1)
            pe.wait_ge(S["in_wmod"], 16)
            pe.wait_ge(S["dve_setup"], 4 + 3 + KD * BATCH)
            wm = ff[:, :, :].rearrange("p a b -> p (a b)")[:, 0:KD * 6 * D].rearrange("p (k n) -> p k n", k=KD)
            for i, v in enumerate(VEC):
                for hh in range(KD):
                    o = (i * KD + hh) * BATCH
                    for k in range(KD):
                        mm(R[1][:, o:o + BATCH], wm[:, k, v * D + hh * P:v * D + (hh + 1) * P], cond_silu[:, k, :],
                           start=(k == 0), stop=(k == KD - 1))
            cond_rows = hn[:, :, :].rearrange("p a (b i) -> p (a b) i", i=P)
            for b, bank in enumerate((R[2], R[3], PB[0], PB[1])):
                for i, v in enumerate((2, 5)):
                    for k in range(KD):
                        last = mm(bank[:, i * D:(i + 1) * D], cond_rows[:, k * BATCH + b, :], wm[:, k, v * D:(v + 1) * D],
                                  start=(k == 0), stop=(k == KD - 1))
            last.then_inc(S["pe_setup"], 1)
            pe.wait_ge(S["in_gu"], 16)
            pe.wait_ge(S["in_down"], 32)
            rows = ff[:, :, :].rearrange("p a (b n) -> p (a b) n", n=D)
            for n in range(MLP_BATCHES):
                pe.wait_ge(S["dve_setup"], DVE_SETUP - MLP_BATCHES + max(n - 3, 0))
                for i in range(4):
                    if n < 8:
                        k, o = n // 4, n % 4 * 4 + i
                        src = rows[:, o, k * P:(k + 1) * P]
                    else:
                        col = (2 * (n - 8) + i // 2) * P
                        src = raw[:, 2 * (i % 2) + col // TOK, col % TOK:col % TOK + P]
                    last = pe.transpose(R[n % 4][:, i * P:(i + 1) * P], src, ident[:, :])
                last.then_inc(S["pe_setup"], 1)

            def project(a, i, k):
                n = a.n
                if k == 0:
                    if i == 0:
                        pe.wait_ge(wa_in[a.p], START + a.m * 48 + 48)
                    if i < 2:
                        pe.wait_ge(S["vs_ready"], START + n * NU)
                    else:
                        pe.wait_ge(S["conv_in"], START + n * 4 + i - 1)
                last = mm(PB[i % 2][:, :], wa[a.p][:, k, i * P:(i + 1) * P], ht[:, k, :], start=(k == 0), stop=(k == KD - 1))
                if k == KD - 1:
                    last.then_inc(S["proj_done"], 1)

            def decay(a, h):
                n = a.n
                pe.wait_ge(S["gm_ready"], START + n * NU + NU)
                pe.wait_ge(S["conv_in"], START + n * 4 + 3 + h)
                mm(PB[h][:, :], mask_after[:, :], gm[:, h * NC:(h + 1) * NC, :].rearrange("p c i -> p (c i)"),
                   start=True, stop=True).then_inc(S["d_done"], 1)

            def A(a):
                for i in range(4):
                    for k in range(KD):
                        project(a, i, k)
                for h in range(2):
                    decay(a, h)

            def k_rows(s):
                n, p = s.n, s.p
                pe.wait_ge(S["d_ready"], START + n * 2 + 2)
                pe.wait_ge(S["silu_done"], START + n * 4 + 2)
                for c in range(NC):
                    last = pe.transpose(PB[1][:, c * P:(c + 1) * P], kt[p][:, c * C:(c + 1) * C], ident[:, :])
                last.then_inc(S["kt_done"], 1)

            def gram(s, i):
                n, p = s.n, s.p
                rhs, done = ((kt[p], S["kk_done"]), (qt[p], S["kq_done"]))[i]
                if i == 1:
                    pe.wait_ge(S["ktok_ready"], START + n + 1)
                for c in range(NC):
                    cs = slice(c * C, (c + 1) * C)
                    last = mm(PB[i][:, cs], kt[p][:, cs], rhs[:, cs], start=True, stop=True)
                last.then_inc(done, 1)

            def z_rows(c, j):
                n, p = c.n, c.p
                if j == 0:
                    pe.wait_ge(wc_in[p], START + c.m * 32 + 32)
                    pe.wait_ge(S["s_upd"], START + n * NU)
                elif j == 2:
                    pe.wait_ge(S["got_ready"], START + n * NC)
                for k in range(KD):
                    last = mm(R[2 + j // 2][:, j % 2 * 2 * P:(j % 2 + 1) * 2 * P], ht[:, k, j * C:(j + 1) * C], wz[p][:, k, :],
                              start=(k == 0), stop=(k == KD - 1))
                if j % 2:
                    last.then_inc(S["z_done"], 1)

            def norms(s):
                n = s.n
                pe.wait_ge(S["kkm_ready"], START + n + 1)
                pe.wait_ge(S["sq_ready"], START + n + 1)
                for c in range(NC):
                    last = mm(PB[0][:, c:c + 1], sq[:, 0, c * C:(c + 1) * C], ones[:, 0:1], start=True, stop=True)
                last.then_inc(S["norms_done"], 1)

            def v_rows(s, h):
                n = s.n
                pe.wait_ge(S["kqm_ready"] if h else S["ss_ready"], START + n + 1)
                pe.wait_ge(S["silu_done"], START + n * 4 + 3 + h)
                for c in range(NC):
                    last = pe.transpose(PB[h][:, c * P:(c + 1) * P], vt[:, h, c * C:(c + 1) * C], ident[:, :])
                last.then_inc(S["v_tr"], 1)

            def to_value_channels(c, j):
                n = c.n
                pe.wait_ge(S["gt_ready"], START + n * NU + 2 * j + 2)
                pe.wait_ge(S["got_ready"], START + n * NC + j)
                if j == 0:
                    pe.wait_ge(S["z_ready"], START + n * 2 + 2)
                for h in range(2):
                    last = pe.transpose(R[3][:, h * P:(h + 1) * P], gt[:, h, :], ident[:, :])
                last.then_inc(S["gtr_done"], 1)

            def project_out(c, j):
                n, p = c.n, c.p
                pe.wait_ge(S["got_ready"], START + n * NC + j + 1)
                for h in range(2):
                    last = mm(Y[j // 2][:, j % 2 * D:(j % 2 + 1) * D], got[:, h, :], wo[p][:, h, :], start=False, stop=False,
                              skip_group_check=True)
                last.then_inc(S["y_done"], 1)

            def join16(c):
                n, p = c.n, c.p
                pe.wait_ge(S["lt_ready"], START + n * NU + NU)
                wait_apart(pe, S["t16_in"], START + n * 16 + 16)
                for u in range(NU):
                    for b in range(NBL):
                        blk = slice(b * BL, (b + 1) * BL)
                        last = mm(R[0][blk, u * BL:u * BL + SB], lt[p][blk, u, blk], t16[blk, u, 0:SB], start=True, stop=True)
                last.then_inc(S["q0_done"], 1)

            def make32(c):
                n = c.n
                pe.wait_ge(S["t16t_ready"], START + n + 1)
                pe.wait_ge(S["q0_ready"], START + n + 1)
                wait_apart(pe, S["z_ready"], START + n * 2 + 1)
                for u in range(NU):
                    for b in range(NBL):
                        blk = slice(b * BL, (b + 1) * BL)
                        last = mm(R[2][blk, u * BL:(u + 1) * BL], q0s[blk, u, :], t16_t[blk, u, :], start=True, stop=True)
                last.then_inc(S["mdiag_done"], 1)

            def join32(c):
                n, p = c.n, c.p
                wait_apart(pe, S["t32_ready"], START + n + 1)
                for u in range(NU):
                    for b in range(2):
                        lo, mid, hi = 64 * b, 64 * b + BL, 64 * b + 64
                        last = mm(R[0][mid:hi, u * BL:(u + 1) * BL], lt[p][lo:mid, u, mid:hi], t32[lo:mid, u, :],
                                  start=True, stop=True)
                last.then_inc(S["q1_done"], 1)

            def make64(c):
                n = c.n
                pe.wait_ge(S["q1_ready"], START + n + 1)
                pe.wait_ge(S["o_ready"], START + n * NC)
                wait_apart(pe, S["mdiag"], START + n * NBL + NBL)
                for u in range(NU):
                    for b in range(2):
                        lo, mid, hi = 64 * b, 64 * b + BL, 64 * b + 64
                        last = mm(R[1][lo:mid, u * BL:(u + 1) * BL], q1s[mid:hi, u, :], minv[mid:hi, u, mid:hi],
                                  start=True, stop=True)
                last.then_inc(S["m12_done"], 1)
                for u in range(NU):
                    last = mm(R[2][BL:64, u * BL:(u + 1) * BL], minv[BL:64, u, BL:64], q1s[BL:64, u, :], start=True, stop=True)
                last.then_inc(S["t21_done"], 1)

            def join64(c):
                n, p = c.n, c.p
                pe.wait_ge(S["t21_ready"], START + n + 1)
                wait_apart(pe, S["t64_diag"], START + n * 2 + 2)
                for u in range(NU):
                    last = mm(R[0][64:P, u * 64:(u + 1) * 64], lt[p][0:64, u, 64:P], t64[:, u, :], start=True, stop=True)
                last.then_inc(S["q2_done"], 1)

            def make128(c):
                n = c.n
                pe.wait_ge(S["q2_ready"], START + n + 1)
                wait_apart(pe, S["m12_ready"], START + n * 2 + 2)
                for u in range(NU):
                    last = mm(R[1][0:64, u * 64:(u + 1) * 64], q2s[64:P, u, :], minv[64:P, u, 64:P], start=True, stop=True)
                last.then_inc(S["m2_done"], 1)

            def states_in(c, j):
                n, p = c.n, c.p
                cs = slice(j * C, (j + 1) * C)
                if j == 0:
                    pe.wait_ge(S["s_load"], START + n + 1)
                    pe.wait_ge(S["minv_ready"], START + n + 1)
                else:
                    pe.wait_ge(S["s_upd"], START + n * NU + 2 * j)
                mm(R[0][:, 0:2 * P], kt[p][:, cs], sw[p][:, :], start=True, stop=True).then_inc(S["ks_done"], 1)
                if j > 0:
                    pe.wait_ge(S["o_ready"], START + n * NC + j)
                mm(R[1][:, 0:2 * P], qt[p][:, cs], sw[p][:, :], start=True, stop=True).then_inc(S["qs_done"], 1)

            def w_rows(c, j):
                n = c.n
                for h in range(2):
                    pe.wait_ge(S["r_ready"], START + n * NU + 2 * j + h + 1)
                    last = mm(R[2][:, (2 + h) * P:(3 + h) * P], minv[:, unit(h, j), :], rn[:, h, :], start=True, stop=True)
                last.then_inc(S["w_done"], 1)

            def chunk_out(c, j):
                n, p = c.n, c.p
                pe.wait_ge(S["k2_ready"], START + n * NU + NU)
                pe.wait_ge(S["u_ready"], START + n * NU + 2 * j + 2)
                for h in range(2):
                    last = mm(R[2][:, h * P:(h + 1) * P], k2[p][:, unit(h, j), :], us[:, h, :], start=True, stop=True)
                last.then_inc(S["su_done"], 1)
                pe.wait_ge(S["pt_ready"], START + n * 2 + 2)
                pe.wait_ge(S["tq_ready"], START + n * NU + 2 * j + 2)
                for h in range(2):
                    last = mm(R[1][:, (2 + h) * P:(3 + h) * P], pt[p][:, unit(h, j), :], us[:, h, :], start=True, stop=True)
                last.then_inc(S["pu_done"], 1)

            def slot(s, c, a):
                if c is not None:
                    join16(c)
                if s is not None:
                    k_rows(s)
                    gram(s, 0)
                if c is not None:
                    make32(c)
                if s is not None:
                    gram(s, 1)
                    norms(s)
                if c is not None:
                    join32(c)
                    z_rows(c, 2)
                    make64(c)
                if s is not None:
                    v_rows(s, 0)
                if c is not None:
                    join64(c)
                    z_rows(c, 3)
                    make128(c)
                if s is not None:
                    v_rows(s, 1)
                for j in range(NC):
                    if c is not None:
                        states_in(c, j)
                        if j > 1:
                            to_value_channels(c, j - 2)
                        w_rows(c, j)
                    if a is not None:
                        project(a, j, 0)
                    if c is not None:
                        chunk_out(c, j)
                        if j > 1:
                            project_out(c, j - 2)
                    if a is not None:
                        project(a, j, 1)
                if c is not None:
                    to_value_channels(c, NC - 2)
                if a is not None:
                    decay(a, 0)
                if c is not None:
                    project_out(c, NC - 2)
                if s is not None:
                    z_rows(s, 0)
                if a is not None:
                    decay(a, 1)
                if c is not None:
                    to_value_channels(c, NC - 1)
                if s is not None:
                    z_rows(s, 1)
                if c is not None:
                    project_out(c, NC - 1)

            def to_channels(t, second):
                pe.wait_ge(S["hn_ready"], START + t * 8 + 4 * second + 4)
                for k in range(KD):
                    for c in range(NC):
                        last = pe.transpose(R[k][:, c * P:(c + 1) * P], hn[:, c, k * P:(k + 1) * P], ident[:, :])
                    last.then_inc(S["ht_psum"], 1)

            pe.sem_inc(S["y_done"], NC)
            pe.sem_inc(S["qs_done"], NC)

            def tile(t, b, m0):
                n_end = (m0 + KH // 2) * 2
                pe.wait_ge(S["dve_setup"], DVE_SETUP)
                pe.wait_ge(S["out_ready"], START + t * 2)
                pe.wait_ge(S["ff_ready"], START + t * NI)
                to_channels(t, 0)
                pe.wait_ge(S["x1_half"], START + t * 2)
                for y in Y:
                    last = mm(y[:, :], zero_b[:, 0:P], zero_b[:, :], start=True, stop=True)
                pe.wait_ge(S["ht_ready"], START + t * 4 + 2)
                for c in range(NC):
                    for k in range(KD):
                        last = mm(R[2][:, c * 2 * VH:(c + 1) * 2 * VH], ht[:, k, c * C:(c + 1) * C], w_ba[:, k, :],
                                  start=(k == 0), stop=(k == KD - 1))
                last.then_inc(S["ba_done"], 1)
                pe.wait_ge(S["g_ready"], START + t + 1)
                g_all = table[:, G_, :, :].rearrange("p c h -> p (c h)")
                for i, m in enumerate((mask_incl, mask_after, ones)):
                    last = mm(R[3][:, i * NC * VH:(i + 1) * NC * VH], m[:, :], g_all, start=True, stop=True)
                last.then_inc(S["cum_done"], 1)
                pe.wait_ge(S["thb_ready"], START + t + 1)
                pe.wait_ge(S["exp_ready"], START + t + 1)
                slots(pe, m0, A, slot)
                pe.wait_ge(S["o_ready"], START + n_end * NC)
                pe.wait_ge(S["tq_ready"], START + n_end * NU)
                to_channels(t, 1)
                pe.wait_ge(S["ht_ready"], START + t * 4 + 4)
                pe.wait_ge(S["vs_ready"], START + n_end * NU)
                pe.wait_ge(S["s_upd"], START + n_end * NU)
                pe.wait_ge(S["got_ready"], START + n_end * NC)
                for i in range(NI):
                    pair = (PB[0], PB[1]) if i % 2 == 0 else (R[2], R[3])
                    if i >= 2:
                        pe.wait_ge(S["ff_ready"], START + t * NI + i - 1)
                    for bank, o, done in ((pair[0], i, S["gate_done"]), (pair[1], NI + i, S["up_done"])):
                        for k in range(KD):
                            last = mm(bank[:, :], wgu_t[:, k, o * P:(o + 1) * P], ht[:, k, :], start=(k == 0), stop=(k == KD - 1))
                        last.then_inc(done, 1)
                pe.wait_ge(S["ff_ready"], START + t * NI + NI)
                for c in range(NC):
                    for i in range(NI):
                        last = mm(R[c // 2][:, c % 2 * D:(c % 2 + 1) * D], ff[:, i, c * C:(c + 1) * C], wd_t[:, i, :],
                                  start=(i == 0), stop=(i == NI - 1))
                    if c % 2:
                        last.then_inc(S["down_done"], 1)

            tile_loop(pe, tile)


_INS = ['L0_attn_hidden_states', 'L0_attn_W_qkv', 'L0_attn_W_z', 'L0_attn_W_b', 'L0_attn_W_a', 'L0_attn_conv_w',
        'L0_attn_conv_b', 'L0_attn_dt_bias', 'L0_attn_A_log', 'L0_attn_norm_gamma', 'L0_attn_W_out',
        'L0_ffn_w_gate_up', 'L0_ffn_w_down', 'L0_c', 'L0_wmod']
_OUTS = [((BATCH, SEQ, D), 'float32')]


def kernel(**inputs):
    import numpy as _np
    import concourse.bacc as _bacc
    from concourse import mybir as _mybir
    from concourse.bass_utils import run_bass_kernel_spmd as _run

    nc = _bacc.Bacc("TRN2", target_bir_lowering=False, num_devices=1)
    arrays, args = {}, []
    for name in _INS:
        a = _np.ascontiguousarray(inputs[name])
        arrays[f"in_{name}_dram"] = a
        args.append(nc.dram_tensor(f"in_{name}_dram", a.shape, _mybir.dt.from_np(a.dtype), kind="ExternalInput").ap())
    for i, (shape, dtype) in enumerate(_OUTS):
        dt = _mybir.dt.from_np(_np.dtype(dtype))
        args.append(nc.dram_tensor(f"out_{i}_dram", shape, dt, kind="ExternalOutput").ap())
    adaln_block(nc, *args)
    r = _run(nc, [arrays], core_ids=[0])
    return r.results[0]["out_0_dram"]
```
